# Optimizing a Trainium2 kernel written in Bass

```python
import numpy as np
import jax
import jax.numpy as jnp

def _softmax(x, axis=-1):
    return jax.nn.softmax(x, axis=axis)

def _gelu(x):
    return jax.nn.gelu(x, approximate=True)

def _silu(x):
    return jax.nn.silu(x)

def _sigmoid(x):
    return jax.nn.sigmoid(x)

def _layernorm(x, axis=-1, eps=1e-05):
    m = jnp.mean(x, axis=axis, keepdims=True)
    v = jnp.var(x, axis=axis, keepdims=True)
    return (x - m) / jnp.sqrt(v + eps)

def _scatter_add(tgt, idx, src, axis=0):
    return tgt.at[idx].add(src)

def _segment_sum(src, seg, n):
    return jax.ops.segment_sum(src, seg, n)
kernel_name = 'mk_lm_tower_d2_tok_ids768_r4_9ce8ab'

def setup_inputs(seed: int=0):
    np.random.seed(seed)
    _w = jnp.asarray

    def _rec_inputs():
        import jax
        import jax.numpy as jnp
        _rk = jax.random.key(seed)
        x = jax.random.randint(jax.random.fold_in(_rk, 1), (128, 128), 0, 128, jnp.int32)
        mask_BS_i1_0 = jnp.where(jnp.ones((128, 128), dtype=bool), 1, 0).astype(jnp.int32)
        return (x, mask_BS_i1_0)
    x, mask_BS_i1_0 = _rec_inputs()

    def _L0_tok_setup():
        import jax, jax.numpy as jnp
        import numpy as np
        VOCAB = 8000
        D_MODEL = 192
        MAX_LEN = 128
        TYPE_VOCAB = 2
        PADDING_IDX = 1
        LN_EPS = 1e-12
        key = jax.random.key(seed)
        k1, k2, k3, k4, k5, k6 = jax.random.split(key, 6)
        B, S = (8, 1024)
        x = jax.random.randint(k1, (B, S), 0, MAX_LEN, dtype=jnp.int64)
        token_type_ids = jax.random.randint(k2, (B, S), 0, TYPE_VOCAB, dtype=jnp.int64)
        tok_table = jax.random.normal(k3, (VOCAB, D_MODEL), dtype=jnp.float32) * 0.02
        tok_table = tok_table.at[PADDING_IDX].set(0.0)
        pos_table = jax.random.normal(k4, (MAX_LEN, D_MODEL), dtype=jnp.float32) * 0.02
        type_table = jax.random.normal(k5, (TYPE_VOCAB, D_MODEL), dtype=jnp.float32) * 0.02
        gamma = jnp.ones((D_MODEL,), dtype=jnp.float32)
        beta = jnp.zeros((D_MODEL,), dtype=jnp.float32)
        return {'x': x, 'token_type_ids': token_type_ids, 'tok_table': tok_table, 'pos_table': pos_table, 'type_table': type_table, 'gamma': gamma, 'beta': beta}
    _L0_tok_all = _L0_tok_setup()
    _L0_tok_in = {k: v for k, v in _L0_tok_all.items() if k in ('tok_table', 'pos_table', 'type_table', 'gamma', 'beta')}
    del _L0_tok_all

    def _L0_attn_setup():
        import jax, jax.numpy as jnp
        import numpy as np
        EPS = 1e-06

        def _ln(x, g, b):
            mu = x.mean(-1, keepdims=True)
            var = ((x - mu) ** 2).mean(-1, keepdims=True)
            return (x - mu) * jax.lax.rsqrt(var + EPS) * g + b

        def _ln_l2_grad(z, target, g, b):
            d = z.shape[-1]
            mu = z.mean(-1, keepdims=True)
            var = ((z - mu) ** 2).mean(-1, keepdims=True)
            std = jnp.sqrt(var + EPS)
            zh = (z - mu) / std
            go = zh * g + b - target
            gxh = go * g
            return (d * gxh - gxh.sum(-1, keepdims=True) - zh * (gxh * zh).sum(-1, keepdims=True)) / (d * std)

        def _forward(x, W_down, b_down, Wq, Wk, Wv, Wo, W1, b1, ttt_g, ttt_b, lr_w, lr_b, post_g, post_b, norm_g, norm_b, W_up, b_up):
            B, S, D = x.shape
            A = W_down.shape[1]
            H, hd, _ = W1.shape
            h = jax.nn.silu(x @ W_down + b_down)
            xq = (h @ Wq).reshape(B, S, H, hd)
            xk = (h @ Wk).reshape(B, S, H, hd)
            xv = (h @ Wv).reshape(B, S, H, hd)
            eta = jax.nn.sigmoid(h @ lr_w + lr_b) / hd
            W1_0 = jnp.broadcast_to(W1, (B, H, hd, hd))
            b1_0 = jnp.broadcast_to(b1, (B, H, 1, hd))
            xs = (xq.transpose(1, 0, 2, 3), xk.transpose(1, 0, 2, 3), xv.transpose(1, 0, 2, 3), eta.transpose(1, 0, 2))

            def step(carry, ins):
                W, bb = carry
                q, k, v, e = ins
                Z = jnp.einsum('bhd,bhde->bhe', k, W) + bb[:, :, 0, :]
                g = _ln_l2_grad(Z, v - k, ttt_g, ttt_b)
                e4 = e[:, :, None, None]
                Wn = W - e4 * (k[..., :, None] * g[..., None, :])
                bn = bb - e4 * g[:, :, None, :]
                Zq = jnp.einsum('bhd,bhde->bhe', q, Wn) + bn[:, :, 0, :]
                out = q + _ln(Zq, ttt_g, ttt_b)
                return ((Wn, bn), out)
            _, ys = jax.lax.scan(step, (W1_0, b1_0), xs)
            t = ys.transpose(1, 0, 2, 3).reshape(B, S, A)
            t = _ln(t, post_g, post_b) @ Wo
            out = _ln(t, norm_g, norm_b)
            return out @ W_up + b_up
        key = jax.random.key(seed)
        ks = jax.random.split(key, 12)
        B, S, D, A, H = (4, 256, 192, 192, 3)
        hd = A // H
        s = 0.02
        return {'x': jax.random.normal(ks[0], (B, S, D), jnp.float32), 'W_down': jax.random.normal(ks[1], (D, A), jnp.float32) * s, 'b_down': jnp.zeros((A,), jnp.float32), 'Wq': jax.random.normal(ks[2], (A, A), jnp.float32) * s, 'Wk': jax.random.normal(ks[3], (A, A), jnp.float32) * s, 'Wv': jax.random.normal(ks[4], (A, A), jnp.float32) * s, 'Wo': jax.random.normal(ks[5], (A, A), jnp.float32) * s, 'W1': jax.random.normal(ks[6], (H, hd, hd), jnp.float32) * s, 'b1': jnp.zeros((H, 1, hd), jnp.float32), 'ttt_g': jnp.ones((H, hd), jnp.float32), 'ttt_b': jnp.zeros((H, hd), jnp.float32), 'lr_w': jax.random.normal(ks[7], (A, H), jnp.float32) * s, 'lr_b': jnp.zeros((H,), jnp.float32), 'post_g': jnp.ones((A,), jnp.float32), 'post_b': jnp.zeros((A,), jnp.float32), 'norm_g': jnp.ones((A,), jnp.float32), 'norm_b': jnp.zeros((A,), jnp.float32), 'W_up': jax.random.normal(ks[8], (A, D), jnp.float32) * s, 'b_up': jnp.zeros((D,), jnp.float32)}
    _L0_attn_all = _L0_attn_setup()
    _L0_attn_in = {k: v for k, v in _L0_attn_all.items() if k in ('W_down', 'b_down', 'Wq', 'Wk', 'Wv', 'Wo', 'W1', 'b1', 'ttt_g', 'ttt_b', 'lr_w', 'lr_b', 'post_g', 'post_b', 'norm_g', 'norm_b', 'W_up', 'b_up')}
    del _L0_attn_all

    def _L0_ffn_setup():
        import jax, jax.numpy as jnp
        import numpy as np
        B, S, D = (4, 256, 192)
        E = 8
        H = 192
        HS = 768
        TOPK_ROUTED = 2
        key = jax.random.key(seed)
        ks = jax.random.split(key, 10)
        w = lambda k, shape: jax.random.normal(k, shape, dtype=jnp.float32) * 0.02
        return {'x': jax.random.normal(ks[0], (B, S, D), dtype=jnp.float32), 'router_w': w(ks[1], (D, E)), 'w_gate': w(ks[2], (E, D, H)), 'w_up': w(ks[3], (E, D, H)), 'w_down': w(ks[4], (E, H, D)), 'ws_gate': w(ks[5], (D, HS)), 'ws_up': w(ks[6], (D, HS)), 'ws_down': w(ks[7], (HS, D)), 'sg_w': w(ks[8], (D, 1)), 'sg_b': jnp.zeros((1,), jnp.float32)}
    _L0_ffn_all = _L0_ffn_setup()
    _L0_ffn_in = {k: v for k, v in _L0_ffn_all.items() if k in ('router_w', 'w_gate', 'w_up', 'w_down', 'ws_gate', 'ws_up', 'ws_down', 'sg_w', 'sg_b')}
    del _L0_ffn_all

    def _L1_attn_setup():
        import jax, jax.numpy as jnp
        import numpy as np
        D_MODEL = 192
        D_STATE = 128
        D_CONV = 4
        EXPAND = 2
        HEADDIM = 64
        NGROUPS = 1
        D_INNER = EXPAND * D_MODEL
        NHEADS = D_INNER // HEADDIM
        CONV_DIM = D_INNER + 2 * NGROUPS * D_STATE
        D_IN_PROJ = 2 * D_INNER + 2 * NGROUPS * D_STATE + NHEADS
        EPS = 1e-05

        def _mamba2(u, in_proj_w, conv_w, conv_b, dt_bias, A_log, D, norm_w, out_proj_w):
            b, l, _ = u.shape
            zxbcdt = jnp.einsum('bld,ed->ble', u, in_proj_w)
            z, xBC, dt = jnp.split(zxbcdt, [D_INNER, D_INNER + CONV_DIM], axis=-1)
            dt = jax.nn.softplus(dt + dt_bias)
            xc = jnp.transpose(xBC, (0, 2, 1))
            xc = jax.lax.conv_general_dilated(xc, conv_w[:, None, :], (1,), [(D_CONV - 1, 0)], dimension_numbers=('NCH', 'OIH', 'NCH'), feature_group_count=CONV_DIM)
            xBC = jax.nn.silu(jnp.transpose(xc, (0, 2, 1)) + conv_b)
            x, B, C = jnp.split(xBC, [D_INNER, D_INNER + NGROUPS * D_STATE], axis=-1)
            x = x.reshape(b, l, NHEADS, HEADDIM)
            A = -jnp.exp(A_log)
            dA = jnp.exp(dt * A)

            def step(h, inp):
                dA_t, dt_t, x_t, B_t, C_t = inp
                h = h * dA_t[..., None, None] + (dt_t[..., None] * x_t)[..., None] * B_t[:, None, None, :]
                y = jnp.einsum('bhpn,bn->bhp', h, C_t)
                return (h, y)
            h0 = jnp.zeros((b, NHEADS, HEADDIM, D_STATE), u.dtype)
            xs = (jnp.moveaxis(dA, 1, 0), jnp.moveaxis(dt, 1, 0), jnp.moveaxis(x, 1, 0), jnp.moveaxis(B, 1, 0), jnp.moveaxis(C, 1, 0))
            _, ys = jax.lax.scan(step, h0, xs)
            y = jnp.moveaxis(ys, 0, 1) + x * D[None, None, :, None]
            y = y.reshape(b, l, D_INNER)
            y = y * jax.nn.silu(z)
            y = y * jax.lax.rsqrt(jnp.mean(y * y, axis=-1, keepdims=True) + EPS) * norm_w
            return jnp.einsum('bld,ed->ble', y, out_proj_w)
        key = jax.random.key(seed)
        ks = jax.random.split(key, 8)
        b, l = (4, 512)
        return {'feature': jax.random.normal(ks[0], (b, l, D_MODEL), jnp.float32), 'in_proj_w': jax.random.normal(ks[1], (D_IN_PROJ, D_MODEL), jnp.float32) * 0.02, 'conv_w': jax.random.normal(ks[2], (CONV_DIM, D_CONV), jnp.float32) * 0.2, 'conv_b': jnp.zeros((CONV_DIM,), jnp.float32), 'dt_bias': jax.random.normal(ks[3], (NHEADS,), jnp.float32) * 0.1, 'A_log': jnp.log(1.0 + 15.0 * jax.random.uniform(ks[4], (NHEADS,), jnp.float32)), 'D': jnp.ones((NHEADS,), jnp.float32), 'norm_w': jnp.ones((D_INNER,), jnp.float32), 'out_proj_w': jax.random.normal(ks[5], (D_MODEL, D_INNER), jnp.float32) * 0.02, 'gate1': jnp.float32(0.6)}
    _L1_attn_all = _L1_attn_setup()
    _L1_attn_in = {k: v for k, v in _L1_attn_all.items() if k in ('in_proj_w', 'conv_w', 'conv_b', 'dt_bias', 'A_log', 'D', 'norm_w', 'out_proj_w', 'gate1')}
    del _L1_attn_all

    def _L1_ffn_setup():
        import jax, jax.numpy as jnp
        import numpy as np
        DEPTH = 11

        def _fff_forward(inputs, weights_in, weights_out, depth=DEPTH):
            B, S, _ = inputs.shape
            n_nodes = weights_in.shape[0]
            max_index = n_nodes - 1
            all_logits = jnp.einsum('bsd,nd->bsn', inputs, weights_in)

            def step(prev_idx, _):
                sel = jnp.clip(prev_idx, 0, max_index)
                logits = jnp.take_along_axis(all_logits, sel[..., None], axis=-1)[..., 0]
                new_idx = jnp.clip(2 * sel + 1 + (logits > 0).astype(sel.dtype), 0, max_index)
                return (new_idx, (logits, new_idx))
            idx0 = jnp.zeros((B, S), dtype=jnp.int32)
            _, (logits_seq, idx_seq) = jax.lax.scan(step, idx0, None, length=depth - 1)
            logits = jnp.concatenate([jnp.zeros((1, B, S), all_logits.dtype), logits_seq], axis=0)
            node_idx = jnp.concatenate([idx0[None], idx_seq], axis=0)
            act = jax.nn.gelu(logits, approximate=False)
            onehot = jax.nn.one_hot(node_idx, n_nodes, dtype=act.dtype)
            coeff = jnp.einsum('dbs,dbsn->bsn', act, onehot)
            return jnp.einsum('bsn,nd->bsd', coeff, weights_out)
        key = jax.random.key(seed)
        k1, k2, k3 = jax.random.split(key, 3)
        B, S, D = (4, 1024, 192)
        n_nodes = 2 * DEPTH - 1
        return {'inputs': jax.random.normal(k1, (B, S, D), dtype=jnp.float32), 'weights_in': jax.random.normal(k2, (n_nodes, D), dtype=jnp.float32), 'weights_out': jax.random.normal(k3, (n_nodes, D), dtype=jnp.float32)}
    _L1_ffn_all = _L1_ffn_setup()
    _L1_ffn_in = {k: v for k, v in _L1_ffn_all.items() if k in ('weights_in', 'weights_out')}
    del _L1_ffn_all
    return {'x': x, 'mask_BS_i1_0': mask_BS_i1_0, 'L0_tok_tok_table': _L0_tok_in['tok_table'], 'L0_tok_pos_table': _L0_tok_in['pos_table'], 'L0_tok_type_table': _L0_tok_in['type_table'], 'L0_tok_gamma': _L0_tok_in['gamma'], 'L0_tok_beta': _L0_tok_in['beta'], 'L0_attn_W_down': _L0_attn_in['W_down'], 'L0_attn_b_down': _L0_attn_in['b_down'], 'L0_attn_Wq': _L0_attn_in['Wq'], 'L0_attn_Wk': _L0_attn_in['Wk'], 'L0_attn_Wv': _L0_attn_in['Wv'], 'L0_attn_Wo': _L0_attn_in['Wo'], 'L0_attn_W1': _L0_attn_in['W1'], 'L0_attn_b1': _L0_attn_in['b1'], 'L0_attn_ttt_g': _L0_attn_in['ttt_g'], 'L0_attn_ttt_b': _L0_attn_in['ttt_b'], 'L0_attn_lr_w': _L0_attn_in['lr_w'], 'L0_attn_lr_b': _L0_attn_in['lr_b'], 'L0_attn_post_g': _L0_attn_in['post_g'], 'L0_attn_post_b': _L0_attn_in['post_b'], 'L0_attn_norm_g': _L0_attn_in['norm_g'], 'L0_attn_norm_b': _L0_attn_in['norm_b'], 'L0_attn_W_up': _L0_attn_in['W_up'], 'L0_attn_b_up': _L0_attn_in['b_up'], 'L0_ffn_router_w': _L0_ffn_in['router_w'], 'L0_ffn_w_gate': _L0_ffn_in['w_gate'], 'L0_ffn_w_up': _L0_ffn_in['w_up'], 'L0_ffn_w_down': _L0_ffn_in['w_down'], 'L0_ffn_ws_gate': _L0_ffn_in['ws_gate'], 'L0_ffn_ws_up': _L0_ffn_in['ws_up'], 'L0_ffn_ws_down': _L0_ffn_in['ws_down'], 'L0_ffn_sg_w': _L0_ffn_in['sg_w'], 'L0_ffn_sg_b': _L0_ffn_in['sg_b'], 'L1_attn_in_proj_w': _L1_attn_in['in_proj_w'], 'L1_attn_conv_w': _L1_attn_in['conv_w'], 'L1_attn_conv_b': _L1_attn_in['conv_b'], 'L1_attn_dt_bias': _L1_attn_in['dt_bias'], 'L1_attn_A_log': _L1_attn_in['A_log'], 'L1_attn_D': _L1_attn_in['D'], 'L1_attn_norm_w': _L1_attn_in['norm_w'], 'L1_attn_out_proj_w': _L1_attn_in['out_proj_w'], 'L1_attn_gate1': _L1_attn_in['gate1'], 'L1_ffn_weights_in': _L1_ffn_in['weights_in'], 'L1_ffn_weights_out': _L1_ffn_in['weights_out']}

def reference(x, mask_BS_i1_0, L0_tok_tok_table, L0_tok_pos_table, L0_tok_type_table, L0_tok_gamma, L0_tok_beta, L0_attn_W_down, L0_attn_b_down, L0_attn_Wq, L0_attn_Wk, L0_attn_Wv, L0_attn_Wo, L0_attn_W1, L0_attn_b1, L0_attn_ttt_g, L0_attn_ttt_b, L0_attn_lr_w, L0_attn_lr_b, L0_attn_post_g, L0_attn_post_b, L0_attn_norm_g, L0_attn_norm_b, L0_attn_W_up, L0_attn_b_up, L0_ffn_router_w, L0_ffn_w_gate, L0_ffn_w_up, L0_ffn_w_down, L0_ffn_ws_gate, L0_ffn_ws_up, L0_ffn_ws_down, L0_ffn_sg_w, L0_ffn_sg_b, L1_attn_in_proj_w, L1_attn_conv_w, L1_attn_conv_b, L1_attn_dt_bias, L1_attn_A_log, L1_attn_D, L1_attn_norm_w, L1_attn_out_proj_w, L1_attn_gate1, L1_ffn_weights_in, L1_ffn_weights_out):
    import jax
    import jax.numpy as jnp

    def _L0_tok_ref(x, token_type_ids, tok_table, pos_table, type_table, gamma, beta):
        import jax, jax.numpy as jnp
        import numpy as np
        VOCAB = 8000
        D_MODEL = 192
        MAX_LEN = 128
        TYPE_VOCAB = 2
        PADDING_IDX = 1
        LN_EPS = 1e-12
        emb = tok_table[x] + pos_table[x] + type_table[token_type_ids]
        mean = jnp.mean(emb, axis=-1, keepdims=True)
        var = jnp.mean(jnp.square(emb - mean), axis=-1, keepdims=True)
        out = (emb - mean) * jax.lax.rsqrt(var + LN_EPS) * gamma + beta
        return out

    def _L0_attn_ref(x, W_down, b_down, Wq, Wk, Wv, Wo, W1, b1, ttt_g, ttt_b, lr_w, lr_b, post_g, post_b, norm_g, norm_b, W_up, b_up):
        import jax, jax.numpy as jnp
        import numpy as np
        EPS = 1e-06

        def _ln(x, g, b):
            mu = x.mean(-1, keepdims=True)
            var = ((x - mu) ** 2).mean(-1, keepdims=True)
            return (x - mu) * jax.lax.rsqrt(var + EPS) * g + b

        def _ln_l2_grad(z, target, g, b):
            d = z.shape[-1]
            mu = z.mean(-1, keepdims=True)
            var = ((z - mu) ** 2).mean(-1, keepdims=True)
            std = jnp.sqrt(var + EPS)
            zh = (z - mu) / std
            go = zh * g + b - target
            gxh = go * g
            return (d * gxh - gxh.sum(-1, keepdims=True) - zh * (gxh * zh).sum(-1, keepdims=True)) / (d * std)

        def _forward(x, W_down, b_down, Wq, Wk, Wv, Wo, W1, b1, ttt_g, ttt_b, lr_w, lr_b, post_g, post_b, norm_g, norm_b, W_up, b_up):
            B, S, D = x.shape
            A = W_down.shape[1]
            H, hd, _ = W1.shape
            h = jax.nn.silu(x @ W_down + b_down)
            xq = (h @ Wq).reshape(B, S, H, hd)
            xk = (h @ Wk).reshape(B, S, H, hd)
            xv = (h @ Wv).reshape(B, S, H, hd)
            eta = jax.nn.sigmoid(h @ lr_w + lr_b) / hd
            W1_0 = jnp.broadcast_to(W1, (B, H, hd, hd))
            b1_0 = jnp.broadcast_to(b1, (B, H, 1, hd))
            xs = (xq.transpose(1, 0, 2, 3), xk.transpose(1, 0, 2, 3), xv.transpose(1, 0, 2, 3), eta.transpose(1, 0, 2))

            def step(carry, ins):
                W, bb = carry
                q, k, v, e = ins
                Z = jnp.einsum('bhd,bhde->bhe', k, W) + bb[:, :, 0, :]
                g = _ln_l2_grad(Z, v - k, ttt_g, ttt_b)
                e4 = e[:, :, None, None]
                Wn = W - e4 * (k[..., :, None] * g[..., None, :])
                bn = bb - e4 * g[:, :, None, :]
                Zq = jnp.einsum('bhd,bhde->bhe', q, Wn) + bn[:, :, 0, :]
                out = q + _ln(Zq, ttt_g, ttt_b)
                return ((Wn, bn), out)
            _, ys = jax.lax.scan(step, (W1_0, b1_0), xs)
            t = ys.transpose(1, 0, 2, 3).reshape(B, S, A)
            t = _ln(t, post_g, post_b) @ Wo
            out = _ln(t, norm_g, norm_b)
            return out @ W_up + b_up
        return _forward(x, W_down, b_down, Wq, Wk, Wv, Wo, W1, b1, ttt_g, ttt_b, lr_w, lr_b, post_g, post_b, norm_g, norm_b, W_up, b_up)

    def _L0_ffn_ref(x, router_w, w_gate, w_up, w_down, ws_gate, ws_up, ws_down, sg_w, sg_b):
        import jax, jax.numpy as jnp
        import numpy as np
        B, S, D = (4, 256, 192)
        E = 8
        H = 192
        HS = 768
        TOPK_ROUTED = 2
        probs = jax.nn.softmax(x @ router_w, axis=-1)
        gates, idx = jax.lax.top_k(probs, TOPK_ROUTED)
        gates = gates / jnp.sum(gates, axis=-1, keepdims=True)
        n_exp = router_w.shape[1]
        dense_g = jnp.sum(jax.nn.one_hot(idx, n_exp, dtype=x.dtype) * gates[..., None], axis=-2)
        g = jax.nn.silu(jnp.einsum('bsd,edh->bseh', x, w_gate))
        u = jnp.einsum('bsd,edh->bseh', x, w_up)
        expert_out = jnp.einsum('bseh,ehd->bsed', g * u, w_down)
        routed = jnp.einsum('bse,bsed->bsd', dense_g, expert_out)
        shared = jax.nn.silu(x @ ws_gate) * (x @ ws_up) @ ws_down
        alpha = jax.nn.sigmoid(x @ sg_w + sg_b)
        return alpha * shared + (1.0 - alpha) * routed

    def _L1_attn_ref(feature, in_proj_w, conv_w, conv_b, dt_bias, A_log, D, norm_w, out_proj_w, gate1):
        import jax, jax.numpy as jnp
        import numpy as np
        D_MODEL = 192
        D_STATE = 128
        D_CONV = 4
        EXPAND = 2
        HEADDIM = 64
        NGROUPS = 1
        D_INNER = EXPAND * D_MODEL
        NHEADS = D_INNER // HEADDIM
        CONV_DIM = D_INNER + 2 * NGROUPS * D_STATE
        D_IN_PROJ = 2 * D_INNER + 2 * NGROUPS * D_STATE + NHEADS
        EPS = 1e-05

        def _mamba2(u, in_proj_w, conv_w, conv_b, dt_bias, A_log, D, norm_w, out_proj_w):
            b, l, _ = u.shape
            zxbcdt = jnp.einsum('bld,ed->ble', u, in_proj_w)
            z, xBC, dt = jnp.split(zxbcdt, [D_INNER, D_INNER + CONV_DIM], axis=-1)
            dt = jax.nn.softplus(dt + dt_bias)
            xc = jnp.transpose(xBC, (0, 2, 1))
            xc = jax.lax.conv_general_dilated(xc, conv_w[:, None, :], (1,), [(D_CONV - 1, 0)], dimension_numbers=('NCH', 'OIH', 'NCH'), feature_group_count=CONV_DIM)
            xBC = jax.nn.silu(jnp.transpose(xc, (0, 2, 1)) + conv_b)
            x, B, C = jnp.split(xBC, [D_INNER, D_INNER + NGROUPS * D_STATE], axis=-1)
            x = x.reshape(b, l, NHEADS, HEADDIM)
            A = -jnp.exp(A_log)
            dA = jnp.exp(dt * A)

            def step(h, inp):
                dA_t, dt_t, x_t, B_t, C_t = inp
                h = h * dA_t[..., None, None] + (dt_t[..., None] * x_t)[..., None] * B_t[:, None, None, :]
                y = jnp.einsum('bhpn,bn->bhp', h, C_t)
                return (h, y)
            h0 = jnp.zeros((b, NHEADS, HEADDIM, D_STATE), u.dtype)
            xs = (jnp.moveaxis(dA, 1, 0), jnp.moveaxis(dt, 1, 0), jnp.moveaxis(x, 1, 0), jnp.moveaxis(B, 1, 0), jnp.moveaxis(C, 1, 0))
            _, ys = jax.lax.scan(step, h0, xs)
            y = jnp.moveaxis(ys, 0, 1) + x * D[None, None, :, None]
            y = y.reshape(b, l, D_INNER)
            y = y * jax.nn.silu(z)
            y = y * jax.lax.rsqrt(jnp.mean(y * y, axis=-1, keepdims=True) + EPS) * norm_w
            return jnp.einsum('bld,ed->ble', y, out_proj_w)
        out = _mamba2(feature, in_proj_w, conv_w, conv_b, dt_bias, A_log, D, norm_w, out_proj_w)
        return jax.nn.sigmoid(gate1) * out

    def _L1_ffn_ref(inputs, weights_in, weights_out):
        import jax, jax.numpy as jnp
        import numpy as np
        DEPTH = 11

        def _fff_forward(inputs, weights_in, weights_out, depth=DEPTH):
            B, S, _ = inputs.shape
            n_nodes = weights_in.shape[0]
            max_index = n_nodes - 1
            all_logits = jnp.einsum('bsd,nd->bsn', inputs, weights_in)

            def step(prev_idx, _):
                sel = jnp.clip(prev_idx, 0, max_index)
                logits = jnp.take_along_axis(all_logits, sel[..., None], axis=-1)[..., 0]
                new_idx = jnp.clip(2 * sel + 1 + (logits > 0).astype(sel.dtype), 0, max_index)
                return (new_idx, (logits, new_idx))
            idx0 = jnp.zeros((B, S), dtype=jnp.int32)
            _, (logits_seq, idx_seq) = jax.lax.scan(step, idx0, None, length=depth - 1)
            logits = jnp.concatenate([jnp.zeros((1, B, S), all_logits.dtype), logits_seq], axis=0)
            node_idx = jnp.concatenate([idx0[None], idx_seq], axis=0)
            act = jax.nn.gelu(logits, approximate=False)
            onehot = jax.nn.one_hot(node_idx, n_nodes, dtype=act.dtype)
            coeff = jnp.einsum('dbs,dbsn->bsn', act, onehot)
            return jnp.einsum('bsn,nd->bsd', coeff, weights_out)
        return _fff_forward(inputs, weights_in, weights_out)
    h = _L0_tok_ref(x, mask_BS_i1_0, L0_tok_tok_table, L0_tok_pos_table, L0_tok_type_table, L0_tok_gamma, L0_tok_beta)
    h = h + _L0_attn_ref(_layernorm(h, axis=-1), L0_attn_W_down, L0_attn_b_down, L0_attn_Wq, L0_attn_Wk, L0_attn_Wv, L0_attn_Wo, L0_attn_W1, L0_attn_b1, L0_attn_ttt_g, L0_attn_ttt_b, L0_attn_lr_w, L0_attn_lr_b, L0_attn_post_g, L0_attn_post_b, L0_attn_norm_g, L0_attn_norm_b, L0_attn_W_up, L0_attn_b_up)
    h = h + _L0_ffn_ref(_layernorm(h, axis=-1), L0_ffn_router_w, L0_ffn_w_gate, L0_ffn_w_up, L0_ffn_w_down, L0_ffn_ws_gate, L0_ffn_ws_up, L0_ffn_ws_down, L0_ffn_sg_w, L0_ffn_sg_b)
    h = h + _L1_attn_ref(_layernorm(h, axis=-1), L1_attn_in_proj_w, L1_attn_conv_w, L1_attn_conv_b, L1_attn_dt_bias, L1_attn_A_log, L1_attn_D, L1_attn_norm_w, L1_attn_out_proj_w, L1_attn_gate1)
    h = h + _L1_ffn_ref(_layernorm(h, axis=-1), L1_ffn_weights_in, L1_ffn_weights_out)
    return h

_drawn_inputs = setup_inputs


def setup_inputs(seed=0):
    import zlib

    import numpy as np

    out = dict(_drawn_inputs(seed))
    spreads = {'L0_tok_gamma': (1.0, 0.2),
     'L0_tok_beta': (0.0, 0.1),
     'L0_attn_b_down': (0.0, 0.1),
     'L0_attn_b1': (0.0, 0.1),
     'L0_attn_ttt_g': (1.0, 0.2),
     'L0_attn_ttt_b': (0.0, 0.1),
     'L0_attn_lr_b': (0.0, 0.1),
     'L0_attn_post_g': (1.0, 0.2),
     'L0_attn_post_b': (0.0, 0.1),
     'L0_attn_norm_g': (1.0, 0.2),
     'L0_attn_norm_b': (0.0, 0.1),
     'L0_attn_b_up': (0.0, 0.1),
     'L1_attn_conv_b': (0.0, 0.1),
     'L1_attn_D': (1.0, 0.2),
     'L1_attn_norm_w': (1.0, 0.2)}
    factors = {'L0_attn_lr_w': 4.277,
     'L0_ffn_sg_w': 3.519,
     'L1_attn_dt_bias': 17.436,
     'L1_attn_A_log': 30.208}
    for name, (base, spread) in spreads.items():
        noise = np.random.default_rng([zlib.crc32(name.encode()), seed]).standard_normal(out[name].shape)
        drawn = base * np.exp(spread * noise) if base else spread * noise
        out[name] = jnp.asarray(drawn.astype(out[name].dtype))
    for name, factor in factors.items():
        out[name] = (out[name] * factor).astype(out[name].dtype)
    return out
```

```python
import concourse.bass as bass
from concourse import mybir
from contextlib import ExitStack

F32 = mybir.dt.float32
BF16 = mybir.dt.bfloat16
I32 = mybir.dt.int32
U32 = mybir.dt.uint32
ACT = mybir.ActivationFunctionType
ALU = mybir.AluOpType
AX = mybir.AxisListType

B, T, D = 128, 128, 192
GB = 4
NG = B // GB
DL, DH = 128, D - 128
H, HD = 3, 64
C = 16
NC = T // C
CREDIT = 1
LOG_POS = 128
P1_DVE = 9


class Chain:

    def __init__(self, eng, sem, turn=0, per=0):
        self.eng, self.sem, self.base, self.per, self.n = eng, sem, turn * per, per, 0

    def __call__(self, ins):
        ins.then_inc(self.sem, 1)
        self.n += 1
        self.eng.wait_ge(self.sem, self.base + self.n + CREDIT)

    def close(self):
        assert self.n == self.per, f"chain has {self.n} links, not {self.per}"


class Mem:

    def __init__(self, nc, ctx, tag):
        self.nc, self.ctx, self.tag, self.sems = nc, ctx, tag, []

    def sb(self, name, shape, dt=F32):
        return self.ctx.enter_context(self.nc.sbuf_tensor(f"{self.tag}_{name}", shape, dt))

    def banks(self, n=8):
        return [self.ctx.enter_context(self.nc.psum_tensor(f"{self.tag}_bank{i}", [128, 512], F32)) for i in range(n)]

    def sem(self, name):
        self.sems.append(self.sem_of_pool_dma(name))
        return self.sems[-1]

    def sem_of_pool_dma(self, name):
        return self.ctx.enter_context(self.nc.semaphore(f"{self.tag}_{name}"))

    def block(self):
        with self.nc.Block() as credits:
            @credits.sync
            def _(sp):
                for sem in self.sems:
                    sp.sem_clear(sem)
                    sp.sem_inc(sem, CREDIT)
        return self.ctx.enter_context(self.nc.Block())


def rows(ap, n):
    return ap[None, :].to_broadcast([n, ap.shape[0]])


def ttt_prepare(nc, a, s, keep):
    with ExitStack() as ctx:
        m = Mem(nc, ctx, "p1")
        sb, sem = m.sb, m.sem
        ident, mask2 = keep.ident, keep.mask2
        xi, ti = sb("xi", [B, T], I32), sb("ti", [B, T], I32)
        xf, tf, pf, junk, junk_pool = sb("xf", [B, T]), sb("tf", [B, T]), sb("pf", [B, T]), sb("junk", [128, 1]), sb("junk_pool", [128, 1])
        idx, idx_now = sb("idx", [T, 2, B], I32), sb("idx_now", [T, 2, GB], I32)
        pt = sb("pt", [LOG_POS, 2, D])
        typ = sb("typ", [128, 2, D])
        gam_tok, bet_tok = sb("gam_tok", [128, D]), sb("bet_tok", [128, D])
        wd0, wd1 = sb("wd0", [DL, D]), sb("wd1", [DH, D])
        bd0, bd1 = sb("bd0", [DL, 1]), sb("bd1", [DH, 1])
        NW = 3 * D + H
        wc0, wc1 = sb("wc0", [DL, NW]), sb("wc1", [DH + 1, NW])
        wk0, wk1 = sb("wk0", [DL, D]), sb("wk1", [DH, D])
        gam = sb("gam", [128, D])
        w1 = sb("w1", [HD + 1, H, HD])
        w1m = sb("w1m", [HD + 1, H])
        half = sb("half", [128, GB])
        te, pe_ = sb("te", [128, GB, D]), sb("pe", [128, GB, D])
        st, mv, rs = sb("st", [128, GB, 6]), sb("mv", [128, GB, 2]), sb("rs", [128, 2, GB])
        h0 = sb("h0", [128, GB, D])
        xn = sb("xn", [128, GB, D])
        xt0, xt1 = sb("xt0", [DL, GB, T]), sb("xt1", [DH, GB, T])
        ht0, ht1 = sb("ht0", [DL, GB, T]), sb("ht1", [DH + 1, GB, T])
        ksb = sb("ksb", [128, 2, D])
        eta = sb("eta", [128, 2, H])
        qz, zc = sb("qz", [128, GB, 2 * D]), sb("zc", [128, GB, 2 * D])
        kqt = sb("kqt", [HD + 1, 2, H, 2, T])
        mk, mq = sb("mk", [128, 2, NC, H, C]), sb("mq", [128, 2, H, T])
        bk = m.banks()

        ids_in, setup_done, idx_t, idx_out = sem("ids_in"), sem("setup_done"), sem("idx_t"), sem("idx_out")
        weights_in, pt_ready, pt_stored, act_chain, dve_chain, pool_chain = (
            sem("weights_in"), sem("pt_ready"), sem("pt_stored"), sem("act_chain"), sem("dve_chain"), sem("pool_chain"))
        setup_chain, half_set = sem("setup_chain"), sem("half_set")
        emb_sum, base_half = sem("emb_sum"), sem("base_half")
        gathered, emb_read, var_ready, rstd_ready = m.sem_of_pool_dma("gathered"), sem("emb_read"), sem("var_ready"), sem("rstd_ready")
        h0_ready, h0_stored, xn_ready = sem("h0_ready"), sem("h0_stored"), sem("xn_ready")
        xt_done, xt_copied_a, xt_copied_v, ht_done, ht_ready = (
            sem("xt_done"), sem("xt_copied_a"), sem("xt_copied_v"), sem("ht_done"), sem("ht_ready"))
        qkv_done, qk_copied, c_copied, eta_tanh, eta_copied = sem("qkv_done"), sem("qk_copied"), sem("c_copied"), sem("eta_tanh"), sem("eta_copied")
        kqt_done, kqt_copied_a, kqt_copied_v = sem("kqt_done"), sem("kqt_copied_a"), sem("kqt_copied_v")
        gram_done, m_ready, base_copied, zq_stored = (
            sem("gram_done"), sem("m_ready"), sem("base_copied"), sem("zq_stored"))
        m_stored = [sem(f"m_stored_{p}") for p in range(2)]

        block = m.block()

        @block.sync
        def _(sp):
            sp.dma_start(ident[:, :], a.c_ident).then_inc(ids_in, 16)
            sp.dma_start(mask2[:, :, :], a.c_mask2).then_inc(ids_in, 16)
            sp.dma_start(xi[:, :], a.x).then_inc(ids_in, 16)
            sp.dma_start(ti[:, :], a.mask_BS_i1_0).then_inc(ids_in, 16)
            sp.dma_start(pt[:, 0, :], a.L0_tok_pos_table).then_inc(ids_in, 16)
            sp.dma_start(pt[:, 1, :], a.L0_tok_pos_table).then_inc(ids_in, 16)
            for k in range(2):
                sp.dma_start(typ[:, k, :], rows(a.L0_tok_type_table[k, :], 128)).then_inc(ids_in, 16)
            loads = [
                (gam_tok[:, :], rows(a.L0_tok_gamma, 128)), (bet_tok[:, :], rows(a.L0_tok_beta, 128)),
                (wd0[:, :], a.L0_attn_W_down[0:DL, :]), (wd1[:, :], a.L0_attn_W_down[DL:D, :]),
                (bd0[:, :], a.L0_attn_b_down[0:DL, None]), (bd1[:, :], a.L0_attn_b_down[DL:D, None]),
                (wk0[:, :], a.L0_attn_Wk[0:DL, :]), (wk1[:, :], a.L0_attn_Wk[DL:D, :]),
                (gam[:, :], rows(a.L0_attn_ttt_g.rearrange("h e -> (h e)"), 128)),
                (w1[0:HD, :, :], a.L0_attn_W1.rearrange("h d e -> d h e")),
                (w1[HD:HD + 1, :, :], a.L0_attn_b1.rearrange("h o e -> o h e")),
                (wc1[DH:DH + 1, 2 * D:3 * D], a.L0_attn_ttt_b.rearrange("h e -> (h e)")[None, :]),
                (wc1[DH:DH + 1, 3 * D:NW], a.L0_attn_lr_b[None, :]),
            ]
            for dst, lo, hi in ((wc0, 0, DL), (wc1, DL, D)):
                n = hi - lo
                loads += [(dst[0:n, 0:D], a.L0_attn_Wq[lo:hi, :]), (dst[0:n, D:2 * D], a.L0_attn_Wk[lo:hi, :]),
                          (dst[0:n, 2 * D:3 * D], a.L0_attn_Wv[lo:hi, :]), (dst[0:n, 3 * D:NW], a.L0_attn_lr_w[lo:hi, :])]
            assert len(loads) == 21
            for dst, src in loads:
                sp.dma_start(dst, src).then_inc(weights_in, 16)
            sp.wait_ge(pt_ready, 1 + CREDIT)
            sp.dma_start(s.pt.rearrange("(k p) d -> p k d", p=LOG_POS), pt[:, :, :]).then_inc(pt_stored, 16)
            with sp.Fori(0, NG) as g:
                sp.wait_ge(h0_ready, g + 1 + CREDIT)
                sp.dma_start(s.h[bass.ts(g, GB), :, :].rearrange("b t d -> t b d"), h0[:, :, :]).then_inc(h0_stored, 16)
                for j in range(GB):
                    b = g * GB + j
                    sp.wait_ge(m_ready, g * GB + j + 1 + CREDIT)
                    sp.dma_start(s.mk[bass.ds(b, 1), :, :, :, :].rearrange("o s c h t -> (o s) (c h t)"),
                                 mk[:, j % 2, :, :, :].rearrange("s c h t -> s (c h t)")).then_inc(m_stored[j % 2], 16)
                    sp.dma_start(s.mq[bass.ds(b, 1), :, :, :].rearrange("o s h t -> (o s) (h t)"),
                                 mq[:, j % 2, :, :].rearrange("s h t -> s (h t)")).then_inc(m_stored[j % 2], 16)
                sp.wait_ge(base_copied, (g + 1) * GB + CREDIT)
                sp.wait_ge(c_copied, (g + 1) * GB + CREDIT)
                sp.dma_start(s.zc[bass.ts(g, GB), :, :].rearrange("b t d -> t b d"), zc[:, :, :]).then_inc(zq_stored, 16)
                sp.dma_start(s.qz[bass.ts(g, GB), :, :].rearrange("b t d -> t b d"), qz[:, :, :]).then_inc(zq_stored, 16)
            sp.wait_ge(h0_stored, 16 * NG + CREDIT)
            for p in range(2):
                sp.wait_ge(m_stored[p], 32 * B // 2 + CREDIT)
            sp.wait_ge(zq_stored, 32 * NG + CREDIT)

        @block.gpsimd
        def _(pool):
            nc.gpsimd.memset(half[:, :], -0.5).then_inc(half_set, 1)
            pool.wait_ge(half_set, 1 + CREDIT)
            pool.wait_ge(idx_out, 2 + CREDIT)
            pool.wait_ge(pt_stored, 16 + CREDIT)
            with pool.Fori(0, NG) as g:
                pool.wait_ge(emb_read, g + CREDIT)
                nc.gpsimd.tensor_tensor(junk_pool[:, :], half[:, 0:1], half[:, 0:1], ALU.mult)
                nc.gpsimd.tensor_copy(idx_now[:, :, :], idx[:, :, bass.ts(g, GB)]).then_inc(pool_chain, 1)
                pool.wait_ge(pool_chain, g + 1 + CREDIT)
                nc.gpsimd.tensor_tensor(junk_pool[:, :], half[:, 0:1], half[:, 0:1], ALU.mult)
                for j in range(GB):
                    nc.gpsimd.indirect_dma_start(
                        out=te[:, j, :], out_offset=None, in_=a.L0_tok_tok_table,
                        in_offset=bass.IndirectOffsetOnAxis(ap=idx_now[:, 0, j:j + 1].bitcast(U32), axis=0),
                    ).then_inc(gathered, 16)
                    nc.gpsimd.indirect_dma_start(
                        out=pe_[:, j, :], out_offset=None, in_=s.pt,
                        in_offset=bass.IndirectOffsetOnAxis(ap=idx_now[:, 1, j:j + 1].bitcast(U32), axis=0),
                    ).then_inc(gathered, 16)
                for k in range(2):
                    pool.wait_ge(var_ready, 2 * g + k + 1 + CREDIT)
                    nc.gpsimd.tensor_tensor(rs[:, k, :], mv[:, :, 1], half[:, :], ALU.pow).then_inc(rstd_ready, 1)

        @block.scalar
        def _(act):
            with act.Fori(0, NG) as g:
                act.wait_ge(xt_done, g + 1 + CREDIT)
                act.wait_ge(ht_done, g + CREDIT)
                nc.scalar.activation(xt1[:, :, :], bk[1][0:DH, :].rearrange("p (j t) -> p j t", j=GB), ACT.Copy).then_inc(xt_copied_a, 1)
                act.wait_ge(ht_done, g + 1 + CREDIT)
                act.wait_ge(qkv_done, g * GB + CREDIT)
                nc.scalar.activation(ht0[:, :, :], bk[2][:, :].rearrange("p (j t) -> p j t", j=GB), ACT.Silu, bias=bd0[:, :]).then_inc(ht_ready, 1)
                nc.scalar.activation(ht1[0:DH, :, :], bk[3][0:DH, :].rearrange("p (j t) -> p j t", j=GB), ACT.Silu, bias=bd1[:, :]).then_inc(ht_ready, 1)
                act.wait_ge(zq_stored, 32 * g + CREDIT)

                def copy_qk(j):
                    p = j % 2
                    act.wait_ge(qkv_done, g * GB + j + 1 + CREDIT)
                    nc.scalar.activation(qz[:, j, 0:D], bk[4 + p][:, 0:D], ACT.Copy).then_inc(qk_copied, 1)
                    nc.scalar.activation(ksb[:, p, :], bk[4 + p][:, D:2 * D], ACT.Copy).then_inc(qk_copied, 1)
                    act.wait_ge(eta_copied, g * GB + j + 1 + CREDIT)
                    nc.scalar.activation(eta[:, p, :], eta[:, p, :], ACT.Tanh, scale=0.5).then_inc(eta_tanh, 1)

                def copy_kqt(j):
                    p = j % 2
                    act.wait_ge(kqt_done, g * GB + j + 1 + CREDIT)
                    if j >= 2:
                        act.wait_ge(gram_done, g * GB + j - 1 + CREDIT)
                    else:
                        act.wait_ge(gram_done, g * GB + CREDIT)
                    nc.scalar.activation(kqt[0:HD, p, 2, :, :], bk[1][0:HD, 0:2 * T].rearrange("p (q t) -> p q t", q=2), ACT.Copy).then_inc(kqt_copied_a, 1)

                def copy_base(j):
                    p = j % 2
                    act.wait_ge(gram_done, g * GB + j + 1 + CREDIT)
                    nc.scalar.activation(zc[:, j, 0:D], bk[4 + p][:, 0:D], ACT.Copy).then_inc(base_half, 1)
                    act.wait_ge(base_half, g * GB + j + 1 + CREDIT)
                    nc.scalar.activation(qz[:, j, D:2 * D], bk[4 + p][:, D:2 * D], ACT.Copy).then_inc(base_copied, 1)

                for step in range(GB + 2):
                    if step >= 2:
                        copy_base(step - 2)
                    if 1 <= step < GB + 1:
                        copy_kqt(step - 1)
                    if step < GB:
                        copy_qk(step)

        @block.vector
        def _(dve):
            setup = Chain(dve, setup_chain)
            dve.wait_ge(ids_in, 8 * 16 + CREDIT)
            setup(nc.vector.tensor_copy(xf[:, :], xi[:, :]))
            setup(nc.vector.tensor_copy(tf[:, :], ti[:, :]))
            setup(nc.vector.tensor_scalar(pf[:, :], xf[:, :], float(LOG_POS - 1), None, ALU.min))
            setup(nc.vector.scalar_tensor_tensor(out=tf[:, :], in0=tf[:, :], scalar=float(LOG_POS), in1=pf[:, :],
                                                 op0=ALU.mult, op1=ALU.add))
            nc.vector.tensor_tensor(pt[:, :, :], pt[:, :, :], typ[:, :, :], ALU.add).then_inc(pt_ready, 1)
            setup(nc.vector.memset(ht1[DH:DH + 1, :, :], 1.0))
            setup(nc.vector.memset(kqt[HD:HD + 1, :, :, :, :], 1.0))
            dve.wait_ge(weights_in, 21 * 16 + CREDIT)
            for w, k, n in ((wc0, wk0, DL), (wc1, wk1, DH)):
                wv = w[0:n, 2 * D:3 * D]
                setup(nc.vector.tensor_tensor(wv, wv, k[:, :], ALU.subtract))
                setup(nc.vector.tensor_tensor(wv, wv, gam[0:n, :], ALU.mult))
            bias = wc1[DH:DH + 1, 2 * D:3 * D]
            setup(nc.vector.scalar_tensor_tensor(out=bias, in0=bias, scalar=-1.0, in1=gam[DH:DH + 1, :], op0=ALU.mult, op1=ALU.mult))
            setup(nc.vector.memset(wc1[DH:DH + 1, 0:2 * D], 0.0))
            setup(nc.vector.tensor_reduce(w1m[:, :], w1[:, :, :], AX.X, ALU.add))
            setup(nc.vector.tensor_scalar(w1m[:, :], w1m[:, :], 1.0 / HD, None, ALU.mult))
            setup(nc.vector.tensor_tensor(w1[:, :, :], w1[:, :, :], w1m[:, :].unsqueeze(2).to_broadcast([HD + 1, H, HD]), ALU.subtract))
            dve.wait_ge(idx_t, 2 + CREDIT)
            nc.vector.tensor_copy(idx[:, 0, :], bk[0][:, 0:B]).then_inc(idx_out, 1)
            nc.vector.tensor_copy(idx[:, 1, :], bk[1][:, 0:B]).then_inc(idx_out, 1)
            nc.vector.memset(junk[:, :], 0.0).then_inc(setup_done, 1)
            with dve.Fori(0, NG) as g:
                c = Chain(dve, dve_chain, g, P1_DVE)

                def norm(src, k, eps, dst):
                    for j in range(GB):
                        last = nc.vector.bn_stats(st[:, j, :], src[:, j, :])
                    c(last)
                    nc.vector.memset(junk[:, :], 0.0)
                    for j in range(GB):
                        last = nc.vector.bn_aggr(mv[:, j, :], st[:, j, :])
                    c(last)
                    nc.vector.tensor_scalar(mv[:, :, 1], mv[:, :, 1], eps, None, ALU.add).then_inc(var_ready, 1)
                    dve.wait_ge(rstd_ready, 2 * g + k + 1 + CREDIT)
                    for j in range(GB):
                        last = nc.vector.tensor_scalar(dst[:, j, :], src[:, j, :], mv[:, j, 0:1], rs[:, k, j:j + 1], ALU.subtract, ALU.mult)
                    if k == 1:
                        last.then_inc(xn_ready, 1)
                    else:
                        c(last)

                dve.wait_ge(gathered, (g + 1) * (2 * GB * 16))
                nc.vector.tensor_tensor(te[:, :, :], te[:, :, :], pe_[:, :, :], ALU.add).then_inc(emb_sum, 1)
                dve.wait_ge(emb_sum, g + 1 + CREDIT)
                dve.wait_ge(h0_stored, 16 * g + CREDIT)
                norm(te, 0, 1e-12, h0)
                bc = lambda v: v[:, :].unsqueeze(1).to_broadcast([128, GB, D])
                nc.vector.tensor_tensor(h0[:, :, :], h0[:, :, :], bc(gam_tok), ALU.mult).then_inc(emb_read, 1)
                dve.wait_ge(emb_read, g + 1 + CREDIT)
                nc.vector.tensor_tensor(h0[:, :, :], h0[:, :, :], bc(bet_tok), ALU.add).then_inc(h0_ready, 1)
                dve.wait_ge(h0_ready, g + 1 + CREDIT)
                dve.wait_ge(xt_done, g + CREDIT)
                norm(h0, 1, 1e-5, xn)
                dve.wait_ge(xt_done, g + 1 + CREDIT)
                nc.vector.tensor_copy(xt0[:, :, :], bk[0][:, :].rearrange("p (j t) -> p j t", j=GB)).then_inc(xt_copied_v, 1)
                dve.wait_ge(zq_stored, 32 * g + CREDIT)

                def copy_c(j):
                    p = j % 2
                    dve.wait_ge(qkv_done, g * GB + j + 1 + CREDIT)
                    nc.vector.tensor_copy(eta[:, p, :], bk[6 + p][:, D:D + H]).then_inc(eta_copied, 1)
                    nc.vector.tensor_copy(zc[:, j, D:2 * D], bk[6 + p][:, 0:D]).then_inc(c_copied, 1)
                    dve.wait_ge(eta_tanh, g * GB + j + 1 + CREDIT)
                    c(nc.vector.tensor_scalar(eta[:, p, :], eta[:, p, :], 0.5 / HD, 0.5 / HD, ALU.mult, ALU.add))

                def copy_kqt(j):
                    p = j % 2
                    dve.wait_ge(kqt_done, g * GB + j + 1 + CREDIT)
                    if j >= 2:
                        dve.wait_ge(gram_done, g * GB + j - 1 + CREDIT)
                    else:
                        dve.wait_ge(gram_done, g * GB + CREDIT)
                    nc.vector.tensor_copy(kqt[0:HD, p, 0:2, :, :], bk[0][0:HD, :].rearrange("p (h q t) -> p h q t", h=2, q=2)).then_inc(kqt_copied_v, 1)

                def gram_scale(j):
                    p = j % 2
                    dve.wait_ge(gram_done, g * GB + j + 1 + CREDIT)
                    dve.wait_ge(m_stored[p], 32 * (g * (GB // 2) + j // 2) + CREDIT)
                    for h in range(H):
                        gr = bk[2][:, h * 2 * T:(h + 1) * 2 * T] if h < 2 else bk[6 + p][:, 2 * T:4 * T]
                        nc.vector.scalar_tensor_tensor(
                            out=mk[:, p, :, h, :], in0=gr[:, 0:T].rearrange("p (c t) -> p c t", c=NC), scalar=eta[:, p, h:h + 1],
                            in1=mask2[:, 0, :].rearrange("p (c t) -> p c t", c=NC), op0=ALU.mult, op1=ALU.mult)
                        last = nc.vector.scalar_tensor_tensor(
                            out=mq[:, p, h, :], in0=gr[:, T:2 * T], scalar=eta[:, p, h:h + 1],
                            in1=mask2[:, 1, :], op0=ALU.mult, op1=ALU.mult)
                    last.then_inc(m_ready, 1)

                for step in range(GB + 2):
                    if step >= 2:
                        gram_scale(step - 2)
                    if 1 <= step < GB + 1:
                        copy_kqt(step - 1)
                    if step < GB:
                        copy_c(step)
                c.close()

        @block.tensor
        def _(pe):
            pe.wait_ge(ids_in, 8 * 16 + CREDIT)
            pe.wait_ge(setup_chain, 4 + CREDIT)
            nc.tensor.transpose(bk[0][:, 0:B], xf[:, :], ident[:, :]).then_inc(idx_t, 1)
            nc.tensor.transpose(bk[1][:, 0:B], tf[:, :], ident[:, :]).then_inc(idx_t, 1)
            pe.wait_ge(setup_done, 1 + CREDIT)
            with pe.Fori(0, NG) as g:
                pe.wait_ge(xn_ready, g + 1 + CREDIT)
                pe.wait_ge(kqt_copied_v, g * GB + CREDIT)
                pe.wait_ge(kqt_copied_a, g * GB + CREDIT)
                for j in range(GB):
                    nc.tensor.transpose(bk[0][:, j * T:(j + 1) * T], xn[:, j, 0:DL], ident[:, :])
                for j in range(GB):
                    last = nc.tensor.transpose(bk[1][0:DH, j * T:(j + 1) * T], xn[:, j, DL:D], ident[:, :])
                last.then_inc(xt_done, 1)
                pe.wait_ge(xt_copied_v, g + 1 + CREDIT)
                pe.wait_ge(xt_copied_a, g + 1 + CREDIT)
                pe.wait_ge(m_ready, g * GB + CREDIT)
                for bank, lo, n in ((bk[2], 0, DL), (bk[3], DL, DH)):
                    nc.tensor.matmul(bank[0:n, :], wd0[:, lo:lo + n], xt0[:, :, :].rearrange("p j t -> p (j t)"), start=True, stop=False)
                    last = nc.tensor.matmul(bank[0:n, :], wd1[:, lo:lo + n], xt1[:, :, :].rearrange("p j t -> p (j t)"), start=False, stop=True)
                last.then_inc(ht_done, 1)
                pe.wait_ge(ht_ready, 2 * (g + 1) + CREDIT)

                def qkv(j):
                    p = j % 2
                    n = g * GB + max(j - 1, 0)
                    pe.wait_ge(base_copied, n + CREDIT)
                    pe.wait_ge(m_ready, n + CREDIT)
                    for bank, lo, w in ((bk[4 + p], 0, 2 * D), (bk[6 + p], 2 * D, D + H)):
                        nc.tensor.matmul(bank[:, 0:w], ht0[:, j, :], wc0[:, lo:lo + w], start=True, stop=False)
                        last = nc.tensor.matmul(bank[:, 0:w], ht1[:, j, :], wc1[:, lo:lo + w], start=False, stop=True)
                    last.then_inc(qkv_done, 1)

                def flip(j):
                    p = j % 2
                    pe.wait_ge(qk_copied, 2 * (g * GB + j + 1) + CREDIT)
                    pe.wait_ge(kqt_copied_v, g * GB + j + CREDIT)
                    pe.wait_ge(kqt_copied_a, g * GB + j + CREDIT)
                    nc.tensor.transpose(bk[0][:, 0:T], ident[:, :], ident[:, :])
                    for h in range(H):
                        for q in range(2):
                            src = qz[:, j, h * HD:(h + 1) * HD] if q else ksb[:, p, h * HD:(h + 1) * HD]
                            col = (2 * h + q) % 4 * T
                            last = nc.tensor.transpose(bk[h // 2][0:HD, col:col + T], src, ident[:, :])
                    last.then_inc(kqt_done, 1)

                def gram(j):
                    p = j % 2
                    pe.wait_ge(kqt_copied_v, g * GB + j + 1 + CREDIT)
                    pe.wait_ge(kqt_copied_a, g * GB + j + 1 + CREDIT)
                    pe.wait_ge(m_ready, g * GB + j + CREDIT)
                    pe.wait_ge(c_copied, g * GB + j + 1 + CREDIT)
                    for h in range(H):
                        out = bk[2][:, h * 2 * T:(h + 1) * 2 * T] if h < 2 else bk[6 + p][:, 2 * T:4 * T]
                        nc.tensor.matmul(out, kqt[:, p, h, 0, :], kqt[:, p, h, :, :].rearrange("p q t -> p (q t)"), start=True, stop=True)
                    for q in range(2):
                        for h in range(H):
                            col = q * D + h * HD
                            last = nc.tensor.matmul(bk[4 + p][:, col:col + HD], kqt[:, p, h, q, :], w1[:, h, :], start=True, stop=True)
                    last.then_inc(gram_done, 1)

                for step in range(GB + 2):
                    if step >= 2:
                        gram(step - 2)
                    if 1 <= step < GB + 1:
                        flip(step - 1)
                    if step < GB:
                        qkv(step)


EPS_TTT = 1e-6
CB = 32
P2_DVE = 1 + 12 * C + 3 * (C - 1)


def ttt_scan(nc, a, s, keep):
    with ExitStack() as ctx:
        m = Mem(nc, ctx, "p2")
        sb, sem = m.sb, m.sem
        hist = keep.hist
        zc = sb("zc", [B, 2, C, 2, D])
        mkb = sb("mkb", [B, 2, C, H, C])
        mkc = sb("mkc", [T, 2, CB, H * C])
        corr = sb("corr", [B, C, D])
        cev = sb("cev", [128, 1, CB // 4, D])
        gout = sb("gout", [B, C, D])
        tmp = corr
        gam = sb("gam", [B, D])
        prod = sb("prod", [B, 4, D])
        sums = sb("sums", [B, 4, H])
        mean = sb("mean", [B, H])
        varb = sb("varb", [B, H])
        coef = sb("coef", [B, 4, H])
        scs = sb("scs", [B, C, 2, H])
        xx = sb("xx", [B, 2, D])
        half = sb("half", [B, H])
        bk = m.banks()

        const_in, half_set, hist_zero, bank_zero = sem("const_in"), sem("half_set"), sem("hist_zero"), sem("bank_zero")
        zc_in = [sem(f"zc_in_{p}") for p in range(2)]
        mkc_in = [sem(f"mkc_in_{p}") for p in range(2)]
        caught, evac_a, evac_v = sem("caught"), sem("evac_a"), sem("evac_v")
        corr_in, corr_used = sem("corr_in"), sem("corr_used")
        sq_ready, rstd_ready, chunk_done, hist_in, chain = (
            sem("sq_ready"), sem("rstd_ready"), sem("chunk_done"), sem("hist_in"), sem("chain"))
        var_set, corr_out, g_out = sem("var_set"), sem("corr_out"), sem("g_out")
        setup_chain = sem("setup_chain")
        block = m.block()
        NQ = B // CB

        @block.sync
        def _(sp):
            sp.dma_start(gam[:, :], rows(a.L0_attn_ttt_g.rearrange("h e -> (h e)"), B)).then_inc(const_in, 16)

            def load_chunk(c, p, first):
                sp.dma_start(zc[:, p, :, :, :], s.zc[:, bass.ts(c, C), :].rearrange("b t (k d) -> b t k d", k=2)).then_inc(zc_in[p], 16)
                sp.dma_start(mkb[:, p, :, :, :].rearrange("b s h t -> b s (h t)"),
                             s.mk[:, bass.ts(c, C), bass.ds(c, 1), :, :].rearrange("b s o h t -> b s (o h t)")).then_inc(zc_in[p], 16)

            def load_grams(c, q, n):
                if q >= 2 or n is not None:
                    sp.wait_ge(caught, (q - 1) + (0 if n is None else n) + CREDIT)
                sp.dma_start(mkc[:, q % 2, :, :], s.mk[q * CB:(q + 1) * CB, :, bass.ds(c, 1), :, :].rearrange("b s o h t -> s b (o h t)")).then_inc(mkc_in[q % 2], 16)

            def spread(c, q, n):
                sp.wait_ge(evac_a, n + q + 1 + CREDIT)
                sp.wait_ge(evac_v, n + q + 1 + CREDIT)
                for r in range(4):
                    sp.dma_start(s.corr[q * CB + r:(q + 1) * CB:4, :, :].rearrange("b t d -> t b d"),
                                 cev[32 * r:32 * r + C, 0, :, :]).then_inc(corr_out, 16)
                if q == NQ - 1:
                    sp.wait_ge(corr_out, 64 * (n + q + 1) + CREDIT)
                    sp.dma_start(corr[:, :, :], s.corr).then_inc(corr_in, 16)

            def keep_gradients(c, n):
                sp.wait_ge(chunk_done, n + CREDIT)
                sp.dma_start(s.g[:, bass.ts(c, C), :], gout[:, :, :]).then_inc(g_out, 16)
                sp.wait_ge(g_out, 16 * n + CREDIT)
                sp.dma_start(hist[bass.ts(c, C), :, :], s.g[:, bass.ts(c, C), :].rearrange("b t d -> t b d")).then_inc(hist_in, 16)

            load_chunk(0, 0, True)
            load_chunk(1, 1, True)
            sp.wait_ge(hist_zero, 1 + CREDIT)
            keep_gradients(0, 1)
            for q in range(2):
                load_grams(1, q, None)
            def chunk(c, p, n, last):
                for q in range(NQ):
                    spread(c, q, n)
                    if q + 2 < NQ:
                        load_grams(c, q + 2, n)
                if not last:
                    load_chunk(c + 1, 1 - p, False)
                keep_gradients(c, c + 1)
                if not last:
                    for q in range(2):
                        load_grams(c + 1, q, n + NQ)

            for c in range(1, NC):
                chunk(c, c % 2, (c - 1) * NQ, c == NC - 1)
            sp.wait_ge(hist_in, 16 * NC + CREDIT)

        @block.gpsimd
        def _(pool):
            nc.gpsimd.memset(half[:, :], -0.5).then_inc(half_set, 1)
            pool.wait_ge(half_set, 1 + CREDIT)
            with pool.Fori(0, T) as t:
                pool.wait_ge(sq_ready, t + 1 + CREDIT)
                nc.gpsimd.tensor_tensor(coef[:, 2, :], varb[:, :], half[:, :], ALU.pow).then_inc(var_set, 1)
                pool.wait_ge(var_set, t + 1 + CREDIT)
                nc.gpsimd.tensor_tensor(coef[:, 3, :], coef[:, 2, :], coef[:, 2, :], ALU.mult).then_inc(rstd_ready, 1)

        def chunks(eng, body, first):
            first()
            with eng.Fori(0, (NC - 2) // 2) as i:
                body(2 * i + 1, 1, (2 * i) * NQ, i, 0)
                body(2 * i + 2, 0, (2 * i + 1) * NQ, i, 1)
            body(NC - 1, 1, (NC - 2) * NQ, (NC - 2) // 2, 0)

        @block.scalar
        def _(act):
            def body(c, p, n, i, k):
                for q in range(NQ):
                    act.wait_ge(caught, n + q + 1 + CREDIT)
                    if q == 0:
                        act.wait_ge(corr_out, 64 * n + CREDIT)
                    else:
                        act.wait_ge(corr_out, 64 * (n + q) + CREDIT)
                    o = q % 2 * 4
                    for x in range(2):
                        last = nc.scalar.activation(cev[:, 0, 2 * x:2 * x + 2, :], bk[o + x][:, 0:2 * D].rearrange("p (k d) -> p k d", k=2), ACT.Copy)
                    last.then_inc(evac_a, 1)
            chunks(act, body, lambda: None)

        @block.tensor
        def _(pe):
            pe.wait_ge(bank_zero, 1 + CREDIT)

            def body(c, p, n, i, k):
                pe.wait_ge(hist_in, 16 * c + CREDIT)
                for q in range(NQ):
                    pe.wait_ge(mkc_in[q % 2], 16 * (n // 2 + q // 2 + 1) + CREDIT if isinstance(n, int) else 16 * ((2 * i + k) * (NQ // 2) + q // 2 + 1) + CREDIT)
                    pe.wait_ge(evac_a, n + q - 1 + CREDIT if q >= 2 else n + CREDIT)
                    pe.wait_ge(evac_v, n + q - 1 + CREDIT if q >= 2 else n + CREDIT)
                    o = q % 2 * 4
                    for b in range(CB):
                        r, kk = b % 4, b // 4
                        for h in range(H):
                            col = kk % 2 * D + h * HD
                            last = nc.tensor.matmul(bk[o + kk // 2][32 * r:32 * r + C, col:col + HD],
                                                    mkc[:, q % 2, b, h * C:(h + 1) * C], hist[:, q * CB + b, h * HD:(h + 1) * HD],
                                                    start=True, stop=True)
                    last.then_inc(caught, 1)
            chunks(pe, body, lambda: None)

        @block.vector
        def _(dve):
            for b in range(8):
                last = nc.vector.memset(bk[b][:, :], 0.0)
            last.then_inc(bank_zero, 1)
            nc.vector.memset(hist[:, :, :], 0.0).then_inc(hist_zero, 1)
            dve.wait_ge(const_in, 16 + CREDIT)
            su = Chain(dve, setup_chain, 0, 1)
            su(nc.vector.tensor_tensor(gam[:, :], gam[:, :], gam[:, :], ALU.mult))

            def scan(c, p):
                ch = Chain(dve, chain, c, P2_DVE)
                ch(nc.vector.tensor_reduce(scs[:, :, 0, :], zc[:, p, :, 1, :].rearrange("b t (h e) -> b t h e", h=H), AX.X, ALU.add))
                for j in range(C):
                    z, cz = zc[:, p, j, 0, :], zc[:, p, j, :, :]
                    zh = z.rearrange("b (h e) -> b h e", h=H)
                    ch(nc.vector.tensor_reduce(mean[:, :], zh, AX.X, ALU.add))
                    ch(nc.vector.scalar_tensor_tensor(out=zh, in0=mean[:, :].unsqueeze(2).to_broadcast([B, H, HD]), scalar=-1.0 / HD, in1=zh,
                                                      op0=ALU.mult, op1=ALU.add))
                    ch(nc.vector.tensor_tensor(prod[:, 0:2, :], cz, z.unsqueeze(1).to_broadcast([B, 2, D]), ALU.mult))
                    ch(nc.vector.tensor_reduce(sums[:, 0:2, :], prod[:, 0:2, :].rearrange("b k (h e) -> b k h e", h=H), AX.X, ALU.add))
                    nc.vector.tensor_scalar(varb[:, :], sums[:, 0, :], 1.0 / HD, EPS_TTT, ALU.mult, ALU.add).then_inc(sq_ready, 1)
                    nc.vector.tensor_tensor(prod[:, 2, :], z, gam[:, :], ALU.mult)
                    ch(nc.vector.tensor_tensor(prod[:, 3, :], prod[:, 0, :], gam[:, :], ALU.mult))
                    ch(nc.vector.tensor_reduce(sums[:, 2:4, :], prod[:, 2:4, :].rearrange("b k (h e) -> b k h e", h=H), AX.X, ALU.add))
                    dve.wait_ge(rstd_ready, c * C + j + 1 + CREDIT)
                    nc.vector.tensor_tensor(scs[:, j, 1, :], sums[:, 1, :], coef[:, 2, :], ALU.mult)
                    ch(nc.vector.tensor_tensor(sums[:, 2:4, :], sums[:, 2:4, :], coef[:, 2:4, :], ALU.mult))
                    ch(nc.vector.tensor_tensor(sums[:, 2:4, :], sums[:, 2:4, :], scs[:, j, :, :], ALU.subtract))
                    ch(nc.vector.scalar_tensor_tensor(out=coef[:, 0:2, :], in0=sums[:, 2:4, :], scalar=1.0 / HD, in1=coef[:, 2:4, :], op0=ALU.mult, op1=ALU.mult))
                    g = gout[:, j, :]
                    wide = lambda v, n: v.unsqueeze(2).to_broadcast([B, n, HD])
                    he = lambda v: v.rearrange("b (h e) -> b h e", h=H)
                    nc.vector.tensor_tensor(xx[:, :, :].rearrange("b k (h e) -> b (k h) e", h=H), cz.rearrange("b k (h e) -> b (k h) e", h=H),
                                            wide(coef[:, 1:3, :].rearrange("b k h -> b (k h)"), 2 * H), ALU.mult)
                    ch(nc.vector.tensor_tensor(he(g), he(prod[:, 2, :]), wide(coef[:, 3, :], H), ALU.mult))
                    ch(nc.vector.tensor_tensor(g, g, xx[:, 0, :], ALU.subtract))
                    ch(nc.vector.tensor_tensor(g, g, xx[:, 1, :], ALU.subtract))
                    last = nc.vector.tensor_tensor(he(g), he(g), wide(coef[:, 0, :], H), ALU.subtract)
                    if j == C - 1:
                        last.then_inc(chunk_done, 1)
                        break
                    ch(last)
                    n = C - 1 - j
                    t4 = tmp[:, 0:n, :].rearrange("b t (h e) -> b t h e", h=H)
                    ch(nc.vector.tensor_tensor(
                        t4, mkb[:, p, j, :, j + 1:C].rearrange("b h t -> b t h").unsqueeze(3).to_broadcast([B, n, H, HD]),
                        he(g).unsqueeze(1).to_broadcast([B, n, H, HD]), ALU.mult))
                    ch(nc.vector.tensor_tensor(zc[:, p, j + 1:C, 0, :], zc[:, p, j + 1:C, 0, :], tmp[:, 0:n, :], ALU.subtract))
                ch.close()

            def body(c, p, n, i, k):
                for q in range(NQ):
                    dve.wait_ge(caught, n + q + 1 + CREDIT)
                    dve.wait_ge(corr_out, 64 * (n + q) + CREDIT)
                    o = q % 2 * 4
                    for x in range(2, 4):
                        last = nc.vector.tensor_copy(cev[:, 0, 2 * x:2 * x + 2, :], bk[o + x][:, 0:2 * D].rearrange("p (k d) -> p k d", k=2))
                    last.then_inc(evac_v, 1)
                dve.wait_ge(zc_in[p], 32 * (i + 1 if p == 1 else i + 2) + CREDIT)
                dve.wait_ge(corr_in, 16 * c + CREDIT)
                dve.wait_ge(hist_in, 16 * c + CREDIT)
                nc.vector.tensor_tensor(zc[:, p, :, 0, :], zc[:, p, :, 0, :], corr[:, :, :], ALU.subtract).then_inc(corr_used, 1)
                dve.wait_ge(corr_used, c + CREDIT)
                scan(c, p)

            chunks(dve, body, lambda: (dve.wait_ge(zc_in[0], 32 + CREDIT), scan(0, 0)))


class Norm:

    def __init__(self, nc, m, of_turn):
        self.nc, self.of_turn = nc, of_turn
        self.st, self.mv = m.sb("bn_st", [128, GB, 6]), m.sb("bn_mv", [128, GB, 2])
        self.rs = m.sb("bn_rs", [128, GB])
        self.half, self.junk = m.sb("bn_half", [128, 16]), m.sb("bn_junk", [128, 1])
        self.half_set, self.var_ready, self.rstd_ready = m.sem("half_set"), m.sem("var_ready"), m.sem("rstd_ready")

    def pool_start(self, pool):
        self.nc.gpsimd.memset(self.half[:, :], -0.5).then_inc(self.half_set, 1)
        pool.wait_ge(self.half_set, 1 + CREDIT)

    def pool(self, pool, turn, k, var=None, out=None):
        var = self.mv[:, :, 1] if var is None else var
        out = self.rs[:, :] if out is None else out
        pool.wait_ge(self.var_ready, turn * self.of_turn + k + 1 + CREDIT)
        self.nc.gpsimd.tensor_tensor(out, var, self.half[:, 0:out.shape[-1]], ALU.pow).then_inc(self.rstd_ready, 1)

    def dve(self, dve, c, turn, k, src, dst, eps):
        for j in range(GB):
            last = self.nc.vector.bn_stats(self.st[:, j, :], src(j))
        c(last)
        self.nc.vector.memset(self.junk[:, :], 0.0)
        for j in range(GB):
            last = self.nc.vector.bn_aggr(self.mv[:, j, :], self.st[:, j, :])
        c(last)
        self.nc.vector.tensor_scalar(self.mv[:, :, 1], self.mv[:, :, 1], eps, None, ALU.add).then_inc(self.var_ready, 1)
        dve.wait_ge(self.rstd_ready, turn * self.of_turn + k + 1 + CREDIT)
        for j in range(GB):
            last = self.nc.vector.tensor_scalar(dst(j), src(j), self.mv[:, j, 0:1], self.rs[:, j:j + 1], ALU.subtract, ALU.mult)
        return last


P3_DVE = 11


def ttt_finish(nc, a, s, keep):
    with ExitStack() as ctx:
        m = Mem(nc, ctx, "p3")
        sb, sem = m.sb, m.sem
        ident, hist = keep.ident, keep.hist
        mq, qz, h = sb("mq", [T, GB, H, T]), sb("qz", [T, GB, 2, D]), sb("h", [T, GB, D])
        zq, sq = sb("zq", [T, GB, D]), sb("sq", [T, GB, D])
        var12, rs12 = sb("var12", [T, GB * H]), sb("rs12", [T, GB * H])
        gam, bet = sb("gam", [T, D]), sb("bet", [T, D])
        wo0, wo1, wu0, wu1 = sb("wo0", [DL, D]), sb("wo1", [DH, D]), sb("wu0", [DL, D]), sb("wu1", [DH + 1, D])
        pg, pb = sb("pg", [DL, 2, 2]), sb("pb", [DL, 2, 2])
        yn = sb("yn", [T, GB, D])
        yt0, yt1 = sb("yt0", [DL, GB * T]), sb("yt1", [DH + 1, GB * T])
        xt0, xt1 = sb("xt0", [DL, GB * T]), sb("xt1", [DH, GB * T])
        bk = m.banks()
        nm = Norm(nc, m, 4)
        weights_in, ones_set, chain = sem("weights_in"), sem("ones_set"), sem("chain")
        mq_in, qz_in, h_in = sem("mq_in"), sem("qz_in"), sem("h_in")
        zq_done, zq_read, qz_read = sem("zq_done"), sem("zq_read"), sem("qz_read")
        rows_ready, rows_flipped, cols_a, cols_v = sem("rows_ready"), sem("rows_flipped"), sem("cols_a"), sem("cols_v")
        proj_done, h_ready, h_stored, xt_stored = sem("proj_done"), sem("h_ready"), sem("h_stored"), sem("xt_stored")
        block = m.block()
        NF = 3

        @block.sync
        def _(sp):
            loads = [(gam[:, :], rows(a.L0_attn_ttt_g.rearrange("h e -> (h e)"), T)), (bet[:, :], rows(a.L0_attn_ttt_b.rearrange("h e -> (h e)"), T)),
                     (wo0[:, :], a.L0_attn_Wo[0:DL, :]), (wo1[:, :], a.L0_attn_Wo[DL:D, :]),
                     (wu0[:, :], a.L0_attn_W_up[0:DL, :]), (wu1[0:DH, :], a.L0_attn_W_up[DL:D, :]), (wu1[DH:DH + 1, :], a.L0_attn_b_up[None, :])]
            for k, (gn, bn) in enumerate(((a.L0_attn_post_g, a.L0_attn_post_b), (a.L0_attn_norm_g, a.L0_attn_norm_b))):
                for dst, src in ((pg, gn), (pb, bn)):
                    loads += [(dst[:, k, 0:1], src[0:DL, None]), (dst[0:DH, k, 1:2], src[DL:D, None])]
            assert len(loads) == 15
            for dst, src in loads:
                sp.dma_start(dst, src).then_inc(weights_in, 16)
            with sp.Fori(0, NG) as g:
                sp.wait_ge(zq_done, g + CREDIT)
                sp.dma_start(mq[:, :, :, :].rearrange("s b h t -> s b (h t)"), s.mq[bass.ts(g, GB), :, :, :].rearrange("b s h t -> s b (h t)")).then_inc(mq_in, 16)
                sp.wait_ge(qz_read, g + CREDIT)
                sp.dma_start(qz[:, :, :, :].rearrange("t b k d -> t b (k d)"), s.qz[bass.ts(g, GB), :, :].rearrange("b t d -> t b d")).then_inc(qz_in, 16)
                sp.wait_ge(rows_ready, NF * g + CREDIT)
                sp.wait_ge(h_stored, 16 * g + CREDIT)
                sp.dma_start(h[:, :, :], s.h[bass.ts(g, GB), :, :].rearrange("b t d -> t b d")).then_inc(h_in, 16)
                sp.wait_ge(h_ready, g + 1 + CREDIT)
                sp.dma_start(s.h[bass.ts(g, GB), :, :].rearrange("b t d -> t b d"), h[:, :, :]).then_inc(h_stored, 16)
                sp.wait_ge(cols_v, NF * (g + 1) + CREDIT)
                sp.wait_ge(cols_a, NF * (g + 1) + CREDIT)
                sp.dma_start(s.xt[bass.ds(g, 1), 0:DL, :].rearrange("o p n -> (o p) n"), xt0[:, :]).then_inc(xt_stored, 16)
                sp.dma_start(s.xt[bass.ds(g, 1), DL:D, :].rearrange("o p n -> (o p) n"), xt1[:, :]).then_inc(xt_stored, 16)
            sp.wait_ge(h_stored, 16 * NG + CREDIT)
            sp.wait_ge(xt_stored, 32 * NG + CREDIT)

        @block.gpsimd
        def _(pool):
            nm.pool_start(pool)
            with pool.Fori(0, NG) as g:
                nm.pool(pool, g, 0, var12[:, :], rs12[:, :])
                for k in range(1, 4):
                    nm.pool(pool, g, k)

        @block.scalar
        def _(act):
            act.wait_ge(weights_in, 16 * 15 + CREDIT)
            with act.Fori(0, NG) as g:
                for f in range(NF):
                    act.wait_ge(rows_flipped, NF * g + f + 1 + CREDIT)
                    if f < 2:
                        nc.scalar.activation(yt1[0:DH, :], bk[3][0:DH, :], ACT.Identity, scale=pg[0:DH, f, 1:2], bias=pb[0:DH, f, 1:2]).then_inc(cols_a, 1)
                    else:
                        act.wait_ge(xt_stored, 32 * g + CREDIT)
                        nc.scalar.activation(xt1[:, :], bk[3][0:DH, :], ACT.Copy).then_inc(cols_a, 1)

        @block.vector
        def _(dve):
            nc.vector.memset(yt1[DH:DH + 1, :], 1.0).then_inc(ones_set, 1)
            dve.wait_ge(weights_in, 16 * 15 + CREDIT)
            with dve.Fori(0, NG) as g:
                c = Chain(dve, chain, g, P3_DVE)
                dve.wait_ge(qz_in, 16 * (g + 1) + CREDIT)
                dve.wait_ge(zq_done, g + 1 + CREDIT)
                for x in range(2):
                    last = nc.vector.tensor_tensor(zq[:, 2 * x:2 * x + 2, :], qz[:, 2 * x:2 * x + 2, 1, :], bk[x][:, 0:2 * D].rearrange("t (b d) -> t b d", b=2), ALU.subtract)
                last.then_inc(zq_read, 1)
                dve.wait_ge(zq_read, g + 1 + CREDIT)
                c(nc.vector.tensor_tensor(sq[:, :, :], zq[:, :, :], zq[:, :, :], ALU.mult))
                heads = lambda v: v[:, :, :].rearrange("t b (h e) -> t (b h) e", h=H)
                c(nc.vector.tensor_reduce(var12[:, :], heads(sq), AX.X, ALU.add))
                nc.vector.tensor_scalar(var12[:, :], var12[:, :], 1.0 / HD, EPS_TTT, ALU.mult, ALU.add).then_inc(nm.var_ready, 1)
                dve.wait_ge(nm.rstd_ready, 4 * g + 1 + CREDIT)
                c(nc.vector.tensor_tensor(heads(zq), heads(zq), rs12[:, :].unsqueeze(2).to_broadcast([T, GB * H, HD]), ALU.mult))
                bc = lambda v: v[:, :].unsqueeze(1).to_broadcast([T, GB, D])
                c(nc.vector.tensor_tensor(zq[:, :, :], zq[:, :, :], bc(gam), ALU.mult))
                c(nc.vector.tensor_tensor(zq[:, :, :], zq[:, :, :], bc(bet), ALU.add))
                nc.vector.tensor_tensor(zq[:, :, :], zq[:, :, :], qz[:, :, 0, :], ALU.add).then_inc(qz_read, 1)
                dve.wait_ge(qz_read, g + 1 + CREDIT)

                def flip(f):
                    dve.wait_ge(rows_flipped, NF * g + f + 1 + CREDIT)
                    if f < 2:
                        nc.vector.tensor_scalar(yt0[:, :], bk[2][:, :], pg[:, f, 0:1], pb[:, f, 0:1], ALU.mult, ALU.add).then_inc(cols_v, 1)
                    else:
                        dve.wait_ge(xt_stored, 32 * g + CREDIT)
                        nc.vector.tensor_copy(xt0[:, :], bk[2][:, :]).then_inc(cols_v, 1)

                nm.dve(dve, c, g, 1, lambda j: zq[:, j, :], lambda j: yn[:, j, :], 1e-6).then_inc(rows_ready, 1)
                flip(0)
                dve.wait_ge(proj_done, 2 * g + 1 + CREDIT)
                nm.dve(dve, c, g, 2, lambda j: bk[4 + j // 2][:, j % 2 * D:(j % 2 + 1) * D], lambda j: yn[:, j, :], 1e-6).then_inc(rows_ready, 1)
                flip(1)
                dve.wait_ge(proj_done, 2 * g + 2 + CREDIT)
                dve.wait_ge(h_in, 16 * (g + 1) + CREDIT)
                for x in range(2):
                    last = nc.vector.tensor_tensor(h[:, 2 * x:2 * x + 2, :], h[:, 2 * x:2 * x + 2, :], bk[6 + x][:, 0:2 * D].rearrange("t (b d) -> t b d", b=2), ALU.add)
                last.then_inc(h_ready, 1)
                dve.wait_ge(h_ready, g + 1 + CREDIT)
                nm.dve(dve, c, g, 3, lambda j: h[:, j, :], lambda j: yn[:, j, :], 1e-5).then_inc(rows_ready, 1)
                flip(2)
                c.close()

        @block.tensor
        def _(pe):
            pe.wait_ge(weights_in, 16 * 15 + CREDIT)
            pe.wait_ge(ones_set, 1 + CREDIT)
            with pe.Fori(0, NG) as g:
                pe.wait_ge(mq_in, 16 * (g + 1) + CREDIT)
                pe.wait_ge(zq_read, g + CREDIT)
                for j in range(GB):
                    for h_ in range(H):
                        col = j % 2 * D + h_ * HD
                        last = nc.tensor.matmul(bk[j // 2][:, col:col + HD], mq[:, j, h_, :],
                                                hist[:, bass.ds(g * GB + j, 1), h_ * HD:(h_ + 1) * HD].rearrange("s o e -> s (o e)"), start=True, stop=True)
                last.then_inc(zq_done, 1)

                def flip(f):
                    pe.wait_ge(rows_ready, NF * g + f + 1 + CREDIT)
                    pe.wait_ge(cols_a, NF * g + f + CREDIT)
                    pe.wait_ge(cols_v, NF * g + f + CREDIT)
                    for j in range(GB):
                        nc.tensor.transpose(bk[2][:, j * T:(j + 1) * T], yn[:, j, 0:DL], ident[:, :])
                    for j in range(GB):
                        last = nc.tensor.transpose(bk[3][0:DH, j * T:(j + 1) * T], yn[:, j, DL:D], ident[:, :])
                    last.then_inc(rows_flipped, 1)

                def project(f, o, w0, w1, n1):
                    pe.wait_ge(cols_a, NF * g + f + 1 + CREDIT)
                    pe.wait_ge(cols_v, NF * g + f + 1 + CREDIT)
                    for j in range(GB):
                        out = bk[o + j // 2][:, j % 2 * D:(j % 2 + 1) * D]
                        nc.tensor.matmul(out, yt0[:, j * T:(j + 1) * T], w0[:, :], start=True, stop=False)
                        last = nc.tensor.matmul(out, yt1[0:n1, j * T:(j + 1) * T], w1[:, :], start=False, stop=True)
                    last.then_inc(proj_done, 1)

                flip(0)
                project(0, 4, wo0, wo1, DH)
                flip(1)
                pe.wait_ge(h_ready, g + CREDIT)
                project(1, 6, wu0, wu1, DH + 1)
                flip(2)


NE, HE, HS = 8, 192, 768
HALL = NE * HE + HS
EXP_COLS = HALL
NHT = HALL // 128
NX = NE + 1
P4_DVE = 15


def moe(nc, a, s, keep):
    with ExitStack() as ctx:
        m = Mem(nc, ctx, "p4")
        sb, sem = m.sb, m.sem
        ident = keep.ident
        wg0, wg1, wu0, wu1 = sb("wg0", [DL, HALL]), sb("wg1", [DH, HALL]), sb("wu0", [DL, HALL]), sb("wu1", [DH, HALL])
        wdn = sb("wdn", [128, NHT, D])
        wr0, wr1, rb = sb("wr0", [DL, NX]), sb("wr1", [DH, NX]), sb("rb", [T, NX])
        exf, ex = sb("exf", [32, HALL]), sb("ex", [32, HALL], BF16)
        iota = sb("iota", [T, NE])
        xt0, xt1 = sb("xt0", [DL, 2, GB * T]), sb("xt1", [DH, 2, GB * T])
        h = sb("h", [T, 2, GB, D])
        lg, top, topi, topf = sb("lg", [T, GB, NX]), sb("top", [T, GB, 8]), sb("topi", [T, GB, 8], U32), sb("topf", [T, GB, 2])
        th, gates = sb("th", [T, 2, GB]), sb("gates", [T, 4, GB])
        dense, pick = sb("dense", [T, GB, NX]), sb("pick", [T, GB, NE])
        part, parts = sb("part", [T, GB, NX], BF16), sb("parts", [T, GB, 32])
        gt = sb("gt", [32, GB * T], BF16)
        sil, up, hid = sb("sil", [128, 2, GB * T]), sb("up", [128, 2, GB * T]), sb("hid", [128, 2, GB * T])
        bk = m.banks()

        weights_in, setup, chain = sem("weights_in"), sem("setup"), sem("chain")
        xt_in, h_in = [sem(f"xt_in_{p}") for p in range(2)], [sem(f"h_in_{p}") for p in range(2)]
        h_stored = [sem(f"h_stored_{p}") for p in range(2)]
        logits_done, tanh_in, tanh_out, parts_ready, parts_flipped, gates_ready = (
            sem("logits_done"), sem("tanh_in"), sem("tanh_out"), sem("parts_ready"), sem("parts_flipped"), sem("gates_ready"))
        gu_done, sil_ready, up_ready, spread_done, hid_ready, down_done, h_ready = (
            sem("gu_done"), sem("sil_ready"), sem("up_ready"), sem("spread_done"), sem("hid_ready"), sem("down_done"), sem("h_ready"))
        block = m.block()

        @block.sync
        def _(sp):
            loads = [(iota[:, :], a.c_iota), (exf[:, :], a.c_expand), (rb[:, NE:NX], rows(a.L0_ffn_sg_b, T))]
            for lo, hi, wg, wu, wr in ((0, DL, wg0, wu0, wr0), (DL, D, wg1, wu1, wr1)):
                loads += [(wr[:, 0:NE], a.L0_ffn_router_w[lo:hi, :]), (wr[:, NE:NX], a.L0_ffn_sg_w[lo:hi, :])]
                for w, routed, shared in ((wg, a.L0_ffn_w_gate, a.L0_ffn_ws_gate), (wu, a.L0_ffn_w_up, a.L0_ffn_ws_up)):
                    loads += [(w[:, 0:NE * HE].rearrange("d (e h) -> d e h", e=NE), routed[:, lo:hi, :].rearrange("e d h -> d e h")),
                              (w[:, NE * HE:HALL], shared[lo:hi, :])]
            loads += [(wdn[:, 0:NE * HE // 128, :], a.L0_ffn_w_down.rearrange("e h d -> (e h) d").rearrange("(k p) d -> p k d", p=128)),
                      (wdn[:, NE * HE // 128:NHT, :], a.L0_ffn_ws_down.rearrange("(k p) d -> p k d", p=128))]
            assert len(loads) == 17
            for dst, src in loads:
                sp.dma_start(dst, src).then_inc(weights_in, 16)

            def load(g, p):
                sp.dma_start(xt0[:, p, :], s.xt[bass.ds(g, 1), 0:DL, :].rearrange("o p n -> (o p) n")).then_inc(xt_in[p], 16)
                sp.dma_start(xt1[:, p, :], s.xt[bass.ds(g, 1), DL:D, :].rearrange("o p n -> (o p) n")).then_inc(xt_in[p], 16)
                sp.dma_start(h[:, p, :, :], s.h[bass.ts(g, GB), :, :].rearrange("b t d -> t b d")).then_inc(h_in[p], 16)

            def store(g, n, p, i):
                sp.wait_ge(h_ready, n + CREDIT)
                sp.dma_start(s.h[bass.ts(g, GB), :, :].rearrange("b t d -> t b d"), h[:, p, :, :]).then_inc(h_stored[p], 16)

            load(0, 0)
            load(1, 1)
            with sp.Fori(0, NG // 2 - 1) as i:
                for p in range(2):
                    g = 2 * i + p
                    store(g, g + 1, p, i)
                    sp.wait_ge(h_stored[p], 16 * (i + 1) + CREDIT)
                    load(g + 2, p)
            for p in range(2):
                store(NG - 2 + p, NG - 1 + p, p, NG // 2 - 1)
            for p in range(2):
                sp.wait_ge(h_stored[p], 16 * (NG // 2) + CREDIT)

        @block.scalar
        def _(act):
            with act.Fori(0, NG) as g:
                act.wait_ge(tanh_in, g + 1 + CREDIT)
                nc.scalar.activation(th[:, :, :], th[:, :, :], ACT.Tanh, scale=0.5).then_inc(tanh_out, 1)
                for k in range(NHT):
                    act.wait_ge(gu_done, NHT * g + k + 1 + CREDIT)
                    act.wait_ge(up_ready, NHT * g + max(k - 1, 0) + CREDIT)
                    nc.scalar.activation(sil[:, k % 2, :], bk[k % 2][:, :], ACT.Silu).then_inc(sil_ready, 1)

        @block.vector
        def _(dve):
            nc.vector.memset(rb[:, 0:NE], 0.0)
            nc.vector.memset(parts[:, :, :], 0.0)
            dve.wait_ge(weights_in, 16 * 17 + CREDIT)
            nc.vector.tensor_copy(ex[:, :], exf[:, :]).then_inc(setup, 1)
            dve.wait_ge(setup, 1 + CREDIT)

            def group(g, p, i):
                c = Chain(dve, chain, g, P4_DVE)
                dve.wait_ge(logits_done, g + 1 + CREDIT)
                c(nc.vector.tensor_tensor(lg[:, :, :], bk[7][:, 0:GB * 16].rearrange("t (b e) -> t b e", b=GB)[:, :, 0:NX],
                                          rb[:, :].unsqueeze(1).to_broadcast([T, GB, NX]), ALU.add))
                nc.vector.tensor_copy(th[:, 0, :], lg[:, :, NE])
                for j in range(GB):
                    last = nc.vector.max(top[:, j, :], lg[:, j, 0:NE])
                c(last)
                nc.vector.tensor_tensor(th[:, 1, :], top[:, :, 1], top[:, :, 0], ALU.subtract).then_inc(tanh_in, 1)
                for j in range(GB):
                    last = nc.vector.max_index(topi[:, j, :], top[:, j, :], lg[:, j, 0:NE])
                c(last)
                c(nc.vector.tensor_copy(topf[:, :, :], topi[:, :, 0:2]))
                dve.wait_ge(tanh_out, g + 1 + CREDIT)
                nc.vector.tensor_scalar(gates[:, 0, :], th[:, 0, :], -0.5, 0.5, ALU.mult, ALU.add)
                nc.vector.tensor_scalar(gates[:, 1, :], th[:, 0, :], 0.5, 0.5, ALU.mult, ALU.add)
                nc.vector.tensor_scalar(gates[:, 2, :], th[:, 1, :], -0.5, 0.5, ALU.mult, ALU.add)
                c(nc.vector.tensor_scalar(gates[:, 3, :], th[:, 1, :], 0.5, 0.5, ALU.mult, ALU.add))
                c(nc.vector.tensor_tensor(gates[:, 2:4, :], gates[:, 2:4, :], gates[:, 0, :].unsqueeze(1).to_broadcast([T, 2, GB]), ALU.mult))
                each = lambda v: v.unsqueeze(2).to_broadcast([T, GB, NE])
                ids = iota[:, :].unsqueeze(1).to_broadcast([T, GB, NE])
                nc.vector.tensor_tensor(dense[:, :, 0:NE], ids, each(topf[:, :, 0]), ALU.is_equal)
                nc.vector.tensor_copy(dense[:, :, NE], gates[:, 1, :])
                c(nc.vector.tensor_tensor(pick[:, :, :], ids, each(topf[:, :, 1]), ALU.is_equal))
                nc.vector.tensor_tensor(dense[:, :, 0:NE], dense[:, :, 0:NE], each(gates[:, 2, :]), ALU.mult)
                c(nc.vector.tensor_tensor(pick[:, :, :], pick[:, :, :], each(gates[:, 3, :]), ALU.mult))
                c(nc.vector.tensor_tensor(dense[:, :, 0:NE], dense[:, :, 0:NE], pick[:, :, :], ALU.add))
                for k in range(2):
                    c(nc.vector.tensor_copy(part[:, :, :], dense[:, :, :]))
                    c(nc.vector.tensor_copy(parts[:, :, k * NX:(k + 1) * NX], part[:, :, :]))
                    c(nc.vector.tensor_tensor(dense[:, :, :], dense[:, :, :], parts[:, :, k * NX:(k + 1) * NX], ALU.subtract))
                nc.vector.tensor_copy(parts[:, :, 2 * NX:3 * NX], dense[:, :, :]).then_inc(parts_ready, 1)
                dve.wait_ge(parts_flipped, g + 1 + CREDIT)
                nc.vector.tensor_copy(gt[:, :], bk[7][0:32, :]).then_inc(gates_ready, 1)

                def scale_up(k):
                    dve.wait_ge(sil_ready, NHT * g + k + 1 + CREDIT)
                    dve.wait_ge(spread_done, NHT * g + max(k - 1, 0) + CREDIT)
                    nc.vector.tensor_tensor(up[:, k % 2, :], sil[:, k % 2, :], bk[2 + k % 2][:, :], ALU.mult).then_inc(up_ready, 1)

                def gate(k):
                    dve.wait_ge(up_ready, NHT * g + k + 1 + CREDIT)
                    dve.wait_ge(spread_done, NHT * g + k + 1 + CREDIT)
                    dve.wait_ge(down_done, NHT * g + max(k - 1, 0) + CREDIT)
                    nc.vector.tensor_tensor(hid[:, k % 2, :], up[:, k % 2, :], bk[4 if k % 2 == 0 else 7][:, :], ALU.mult).then_inc(hid_ready, 1)

                for k in range(NHT):
                    scale_up(k)
                    gate(k)
                dve.wait_ge(down_done, NHT * (g + 1) + CREDIT)
                dve.wait_ge(h_in[p], 16 * (i + 1) + CREDIT)
                for x in range(2):
                    last = nc.vector.tensor_tensor(h[:, p, 2 * x:2 * x + 2, :], h[:, p, 2 * x:2 * x + 2, :],
                                                   bk[5 + x][:, 0:2 * D].rearrange("t (b d) -> t b d", b=2), ALU.add)
                last.then_inc(h_ready, 1)
                c.close()

            with dve.Fori(0, NG // 2) as i:
                for p in range(2):
                    group(2 * i + p, p, i)

        @block.tensor
        def _(pe):
            pe.wait_ge(weights_in, 16 * 17 + CREDIT)
            pe.wait_ge(setup, 1 + CREDIT)

            def group(g, p, i):
                pe.wait_ge(xt_in[p], 32 * (i + 1) + CREDIT)
                pe.wait_ge(hid_ready, NHT * g + CREDIT)
                for j in range(GB):
                    out = bk[7][:, 16 * j:16 * j + NX]
                    nc.tensor.matmul(out, xt0[:, p, j * T:(j + 1) * T], wr0[:, :], start=True, stop=False)
                    last = nc.tensor.matmul(out, xt1[:, p, j * T:(j + 1) * T], wr1[:, :], start=False, stop=True)
                last.then_inc(logits_done, 1)

                def gate_up(k):
                    pe.wait_ge(up_ready, NHT * g + max(k - 1, 0) + CREDIT)
                    for bank, w0, w1 in ((bk[k % 2], wg0, wg1), (bk[2 + k % 2], wu0, wu1)):
                        nc.tensor.matmul(bank[:, :], w0[:, 128 * k:128 * (k + 1)], xt0[:, p, :], start=True, stop=False)
                        last = nc.tensor.matmul(bank[:, :], w1[:, 128 * k:128 * (k + 1)], xt1[:, p, :], start=False, stop=True)
                    last.then_inc(gu_done, 1)

                def spread(k):
                    pe.wait_ge(hid_ready, NHT * g + max(k - 1, 0) + CREDIT)
                    nc.tensor.matmul(bk[4 if k % 2 == 0 else 7][:, :], ex[:, 128 * k:128 * (k + 1)], gt[:, :], start=True, stop=True).then_inc(spread_done, 1)

                def down(k):
                    pe.wait_ge(hid_ready, NHT * g + k + 1 + CREDIT)
                    for j in range(GB):
                        last = nc.tensor.matmul(bk[5 + j // 2][:, j % 2 * D:(j % 2 + 1) * D], hid[:, k % 2, j * T:(j + 1) * T], wdn[:, k, :],
                                                start=(k == 0 and j % 2 == 0), stop=(k == NHT - 1), skip_group_check=True)
                    last.then_inc(down_done, 1)

                gate_up(0)
                gate_up(1)
                pe.wait_ge(parts_ready, g + 1 + CREDIT)
                for j in range(GB):
                    last = nc.tensor.transpose(bk[7][0:32, j * T:(j + 1) * T], parts[:, j, :], ident[:, :])
                last.then_inc(parts_flipped, 1)
                pe.wait_ge(gates_ready, g + 1 + CREDIT)
                spread(0)
                spread(1)
                pe.wait_ge(h_ready, g + CREDIT)
                for k in range(NHT):
                    if k + 2 < NHT:
                        gate_up(k + 2)
                    down(k)
                    if k + 2 < NHT:
                        spread(k + 2)

            with pe.Fori(0, NG // 2) as i:
                for p in range(2):
                    group(2 * i + p, p, i)


DI, DS, NH, HP, DCONV = 2 * D, 128, 6, 64, 4
CD = DI + 2 * DS
NP = DI + CD + NH
NCT = CD // 128
NPT = -(-NP // 128)
A_LEAST = -110.0
P5_DVE = 2


def mamba_steps(nc, a, s, keep):
    with ExitStack() as ctx:
        m = Mem(nc, ctx, "p5")
        sb, sem = m.sb, m.sem
        ident = keep.ident
        wi0, wi1, wo, dt, da = keep.wi0, keep.wi1, keep.wo, keep.dt, keep.da
        wrow = sb("wrow", [128, NPT, D])
        orow0, orow1 = sb("orow0", [DL, DI]), sb("orow1", [DH, DI])
        dtb, al = sb("dtb", [T, NH]), sb("al", [T, NH])
        h, xn = sb("h", [T, GB, D]), sb("xn", [T, GB, D])
        xt0, xt1 = sb("xt0", [DL, GB * T]), sb("xt1", [DH, GB * T])
        pos, neg = sb("pos", [T, B, NH]), sb("neg", [T, B, NH])
        bk = m.banks()
        nm = Norm(nc, m, 1)
        weights_in, w_flipped, w_copied = sem("weights_in"), sem("w_flipped"), sem("w_copied")
        h_in, rows_ready, rows_flipped, cols_a, cols_v = sem("h_in"), sem("rows_ready"), sem("rows_flipped"), sem("cols_a"), sem("cols_v")
        xt_stored, dt_done, dt_copied, chain = sem("xt_stored"), sem("dt_done"), sem("dt_copied"), sem("chain")
        soft, soft_act, exp_a = sem("soft"), sem("soft_act"), sem("exp_a")
        block = m.block()

        @block.sync
        def _(sp):
            full = NPT - 1
            loads = [(wrow[:, 0:full, :], a.L1_attn_in_proj_w[0:128 * full, :].rearrange("(k p) d -> p k d", p=128)),
                     (wrow[0:NP - 128 * full, full, :], a.L1_attn_in_proj_w[128 * full:NP, :]),
                     (orow0[:, :], a.L1_attn_out_proj_w[0:DL, :]), (orow1[:, :], a.L1_attn_out_proj_w[DL:D, :]),
                     (dtb[:, :], rows(a.L1_attn_dt_bias, T)), (al[:, :], rows(a.L1_attn_A_log, T))]
            assert len(loads) == 6
            for dst, src in loads:
                sp.dma_start(dst, src).then_inc(weights_in, 16)
            with sp.Fori(0, NG) as g:
                sp.wait_ge(rows_ready, g + CREDIT)
                sp.dma_start(h[:, :, :], s.h[bass.ts(g, GB), :, :].rearrange("b t d -> t b d")).then_inc(h_in, 16)
                sp.wait_ge(cols_a, g + 1 + CREDIT)
                sp.wait_ge(cols_v, g + 1 + CREDIT)
                sp.dma_start(s.xt[bass.ds(g, 1), 0:DL, :].rearrange("o p n -> (o p) n"), xt0[:, :]).then_inc(xt_stored, 16)
                sp.dma_start(s.xt[bass.ds(g, 1), DL:D, :].rearrange("o p n -> (o p) n"), xt1[:, :]).then_inc(xt_stored, 16)
            sp.wait_ge(xt_stored, 32 * NG + CREDIT)

        @block.gpsimd
        def _(pool):
            nm.pool_start(pool)
            with pool.Fori(0, NG) as g:
                nm.pool(pool, g, 0)

        @block.scalar
        def _(act):
            with act.Fori(0, NG) as g:
                act.wait_ge(rows_flipped, g + 1 + CREDIT)
                act.wait_ge(xt_stored, 32 * g + CREDIT)
                act.wait_ge(dt_done, g + CREDIT)
                nc.scalar.activation(xt1[:, :], bk[1][0:DH, :], ACT.Copy).then_inc(cols_a, 1)
            act.wait_ge(soft, 2 + CREDIT)
            nc.scalar.activation(neg[:, :, :], neg[:, :, :], ACT.Exp).then_inc(soft_act, 1)
            act.wait_ge(soft_act, 1 + CREDIT)
            nc.scalar.activation(neg[:, :, :], neg[:, :, :], ACT.Ln, bias=1.0).then_inc(soft_act, 1)
            act.wait_ge(weights_in, 16 * 6 + CREDIT)
            nc.scalar.activation(al[:, :], al[:, :], ACT.Exp).then_inc(exp_a, 1)

        @block.vector
        def _(dve):
            for k in range(NPT):
                n = min(128, NP - 128 * k)
                dve.wait_ge(w_flipped, k + 1 + CREDIT)
                nc.vector.tensor_copy(wi0[:, 128 * k:128 * k + n], bk[2 * (k % 2)][:, 0:n])
                nc.vector.tensor_copy(wi1[:, 128 * k:128 * k + n], bk[2 * (k % 2) + 1][0:DH, 0:n]).then_inc(w_copied, 1)
            for k in range(DI // 128):
                dve.wait_ge(w_flipped, NPT + k + 1 + CREDIT)
                nc.vector.tensor_copy(wo[:, k, :], bk[4 + k][:, 0:D]).then_inc(w_copied, 1)
            dve.wait_ge(weights_in, 16 * 6 + CREDIT)
            with dve.Fori(0, NG) as g:
                c = Chain(dve, chain, g, P5_DVE)
                dve.wait_ge(h_in, 16 * (g + 1) + CREDIT)
                dve.wait_ge(rows_flipped, g + CREDIT)
                nm.dve(dve, c, g, 0, lambda j: h[:, j, :], lambda j: xn[:, j, :], 1e-5).then_inc(rows_ready, 1)
                dve.wait_ge(rows_flipped, g + 1 + CREDIT)
                dve.wait_ge(xt_stored, 32 * g + CREDIT)
                dve.wait_ge(dt_done, g + CREDIT)
                nc.vector.tensor_copy(xt0[:, :], bk[0][:, :]).then_inc(cols_v, 1)
                dve.wait_ge(dt_done, g + 1 + CREDIT)
                nc.vector.tensor_tensor(dt[:, bass.ts(g, GB), :], bk[2][:, 0:GB * NH].rearrange("t (b h) -> t b h", b=GB),
                                        dtb[:, :].unsqueeze(1).to_broadcast([T, GB, NH]), ALU.add).then_inc(dt_copied, 1)
                c.close()
            dve.wait_ge(dt_copied, NG + CREDIT)
            nc.vector.tensor_scalar(pos[:, :, :], dt[:, :, :], 0.0, None, ALU.max).then_inc(soft, 1)
            dve.wait_ge(soft, 1 + CREDIT)
            nc.vector.scalar_tensor_tensor(out=neg[:, :, :], in0=pos[:, :, :], scalar=-2.0, in1=dt[:, :, :], op0=ALU.mult, op1=ALU.add).then_inc(soft, 1)
            dve.wait_ge(soft_act, 2 + CREDIT)
            nc.vector.tensor_tensor(dt[:, :, :], pos[:, :, :], neg[:, :, :], ALU.add).then_inc(soft, 1)
            dve.wait_ge(soft, 3 + CREDIT)
            dve.wait_ge(exp_a, 1 + CREDIT)
            nc.vector.scalar_tensor_tensor(out=da[:, :, :], in0=al[:, :].unsqueeze(1).to_broadcast([T, B, NH]), scalar=-1.0, in1=dt[:, :, :],
                                           op0=ALU.mult, op1=ALU.mult).then_inc(soft, 1)
            dve.wait_ge(soft, 4 + CREDIT)
            nc.vector.tensor_scalar(da[:, :, :], da[:, :, :], A_LEAST, None, ALU.max).then_inc(soft, 1)
            dve.wait_ge(soft, 5 + CREDIT)

        @block.tensor
        def _(pe):
            pe.wait_ge(weights_in, 16 * 6 + CREDIT)
            for k in range(NPT):
                n = min(128, NP - 128 * k)
                if k >= 2:
                    pe.wait_ge(w_copied, k - 1 + CREDIT)
                nc.tensor.transpose(bk[2 * (k % 2)][:, 0:n], wrow[0:n, k, 0:DL], ident[0:n, 0:n])
                nc.tensor.transpose(bk[2 * (k % 2) + 1][0:DH, 0:n], wrow[0:n, k, DL:D], ident[0:n, 0:n]).then_inc(w_flipped, 1)
            for k in range(DI // 128):
                nc.tensor.transpose(bk[4 + k][:, 0:DL], orow0[:, 128 * k:128 * (k + 1)], ident[:, :])
                nc.tensor.transpose(bk[4 + k][:, DL:D], orow1[:, 128 * k:128 * (k + 1)], ident[0:DH, 0:DH]).then_inc(w_flipped, 1)
            pe.wait_ge(w_copied, NPT + DI // 128 + CREDIT)
            with pe.Fori(0, NG) as g:
                pe.wait_ge(rows_ready, g + 1 + CREDIT)
                pe.wait_ge(cols_a, g + CREDIT)
                pe.wait_ge(cols_v, g + CREDIT)
                for j in range(GB):
                    nc.tensor.transpose(bk[0][:, j * T:(j + 1) * T], xn[:, j, 0:DL], ident[:, :])
                for j in range(GB):
                    last = nc.tensor.transpose(bk[1][0:DH, j * T:(j + 1) * T], xn[:, j, DL:D], ident[:, :])
                last.then_inc(rows_flipped, 1)
                pe.wait_ge(cols_a, g + 1 + CREDIT)
                pe.wait_ge(cols_v, g + 1 + CREDIT)
                pe.wait_ge(dt_copied, g + CREDIT)
                for j in range(GB):
                    out = bk[2][:, NH * j:NH * (j + 1)]
                    nc.tensor.matmul(out, xt0[:, j * T:(j + 1) * T], wi0[:, DI + CD:NP], start=True, stop=False)
                    last = nc.tensor.matmul(out, xt1[:, j * T:(j + 1) * T], wi1[:, DI + CD:NP], start=False, stop=True)
                last.then_inc(dt_done, 1)


def second_layer(nc, a, s, keep):
    with ExitStack() as ctx:
        m = Mem(nc, ctx, "layer1")
        keep.wi0, keep.wi1 = m.sb("wi0", [DL, NP]), m.sb("wi1", [DH, NP])
        keep.wo = m.sb("wo", [128, DI // 128, D])
        keep.dt, keep.da = m.sb("dt", [T, B, NH]), m.sb("da", [T, B, NH])
        mamba_steps(nc, a, s, keep)
        mamba(nc, a, s, keep)
    feed_forward(nc, a, s, keep)


P6_DVE = 2 * NCT
EPS_GATED = 1e-5
W6 = 4 + NCT + DI // 128


def mamba(nc, a, s, keep):
    with ExitStack() as ctx:
        m = Mem(nc, ctx, "p6")
        sb, sem = m.sb, m.sem
        ident, mask2, wi0, wi1, wo, dt, da = keep.ident, keep.mask2, keep.wi0, keep.wi1, keep.wo, keep.dt, keep.da
        after = sb("after", [T, T])
        cw, cb = sb("cw", [128, NCT, DCONV]), sb("cb", [128, NCT])
        dd, nw, g1 = sb("dd", [T, NH]), sb("nw", [128, DI // 128]), sb("g1", [T, 1])
        xt0, xt1 = sb("xt0", [DL, GB * T]), sb("xt1", [DH, GB * T])
        h = sb("h", [T, GB, D])
        pad = sb("pad", [128, 2, GB, T + DCONV - 1])
        u, th = sb("u", [128, 2, GB, T]), sb("th", [128, 2, GB, T])
        xbc = sb("xbc", [128, NCT, GB, T])
        tz, sz = sb("tz", [T, DI]), sb("sz", [T, 2, DI])
        cbm = sb("cbm", [T, T])
        am = sb("am", [T, NH, T])
        dec, mm = sb("dec", [T, NH, T]), sb("mm", [T, NH, T])
        xd, xs = sb("xd", [T, NH, HP]), sb("xs", [T, NH, HP])
        y, sq, yt = sb("y", [T, DI]), sb("sq", [T, DI]), sb("yt", [128, DI // 128, T])
        ms, ms2, rs, rg, half = (sb(n, [T, 1]) for n in ("ms", "ms2", "rs", "rg", "half"))
        bk = m.banks()

        weights_in, tuned, gate_tanh, half_set = sem("weights_in"), sem("tuned"), sem("gate_tanh"), sem("half_set")
        xt_in, h_in, h_stored = sem("xt_in"), sem("h_in"), sem("h_stored")
        conv_in, padded, conv_done, conv_tanh, chan_ready, chain, act_chain = (
            sem("conv_in"), sem("padded"), sem("conv_done"), sem("conv_tanh"), sem("chan_ready"), sem("chain"), sem("act_chain"))
        z_done, z_tanh, z_ready = sem("z_done"), sem("z_tanh"), sem("z_ready")
        cb_done, cbm_ready, am_ready, seg_done, dec_ready, mm_ready = (
            sem("cb_done"), sem("cbm_ready"), sem("am_ready"), sem("seg_done"), sem("dec_ready"), sem("mm_ready"))
        x_flipped, x_ready, y_done, y_ready, y_sum, y_sq, ms_ready, rstd_ready = (
            sem("x_flipped"), sem("x_ready"), sem("y_done"), sem("y_ready"), sem("y_sum"), sem("y_sq"), sem("ms_ready"), sem("rstd_ready"))
        y_flipped, yt_ready, out_done, scaled, h_ready = sem("y_flipped"), sem("yt_ready"), sem("out_done"), sem("scaled"), sem("h_ready")
        block = m.block()

        @block.sync
        def _(sp):
            loads = [(after[:, :], a.c_after), (cw[:, :, :], a.L1_attn_conv_w.rearrange("(k p) w -> p k w", p=128)),
                     (dd[:, :], rows(a.L1_attn_D, T)),
                     (g1[:, :], rows(a.L1_attn_gate1, T))]
            for dst, src in ((cb, a.L1_attn_conv_b), (nw, a.L1_attn_norm_w)):
                loads += [(dst[:, k:k + 1], src[128 * k:128 * (k + 1), None]) for k in range(dst.shape[1])]
            assert len(loads) == W6
            for dst, src in loads:
                sp.dma_start(dst, src).then_inc(weights_in, 16)
            with sp.Fori(0, NG) as g:
                sp.wait_ge(z_done, GB * g + CREDIT)
                sp.dma_start(xt0[:, :], s.xt[bass.ds(g, 1), 0:DL, :].rearrange("o p n -> (o p) n")).then_inc(xt_in, 16)
                sp.dma_start(xt1[:, :], s.xt[bass.ds(g, 1), DL:D, :].rearrange("o p n -> (o p) n")).then_inc(xt_in, 16)
                sp.wait_ge(h_stored, 16 * g + CREDIT)
                sp.dma_start(h[:, :, :], s.h[bass.ts(g, GB), :, :].rearrange("b t d -> t b d")).then_inc(h_in, 16)
                sp.wait_ge(h_ready, GB * (g + 1) + CREDIT)
                sp.dma_start(s.h[bass.ts(g, GB), :, :].rearrange("b t d -> t b d"), h[:, :, :]).then_inc(h_stored, 16)
            sp.wait_ge(h_stored, 16 * NG + CREDIT)

        @block.gpsimd
        def _(pool):
            nc.gpsimd.memset(half[:, :], -0.5).then_inc(half_set, 1)
            pool.wait_ge(half_set, 1 + CREDIT)
            with pool.Fori(0, B) as b:
                pool.wait_ge(ms_ready, b + 1 + CREDIT)
                pool.wait_ge(scaled, b + CREDIT)
                nc.gpsimd.tensor_tensor(rs[:, :], ms[:, :], half[:, :], ALU.pow).then_inc(rstd_ready, 1)

        @block.scalar
        def _(act):
            act.wait_ge(weights_in, 16 * W6 + CREDIT)
            nc.scalar.activation(g1[:, :], g1[:, :], ACT.Tanh, scale=0.5).then_inc(gate_tanh, 1)
            act.wait_ge(tuned, 3 + CREDIT)
            with act.Fori(0, NG) as g:
                def take(k):
                    n = NCT * g + k
                    act.wait_ge(conv_in, n + 1 + CREDIT)
                    act.wait_ge(chan_ready, NCT * g + max(k - 1, 0) + CREDIT)
                    nc.scalar.activation(pad[:, k % 2, :, DCONV - 1:], bk[k % 2][:, :].rearrange("p (b t) -> p b t", b=GB), ACT.Copy)
                    nc.scalar.activation(u[:, k % 2, :, :], bk[k % 2][:, :].rearrange("p (b t) -> p b t", b=GB), ACT.Identity,
                                         scale=cw[:, k, DCONV - 1:DCONV], bias=cb[:, k:k + 1]).then_inc(padded, 1)

                def bend(k):
                    act.wait_ge(conv_done, NCT * g + k + 1 + CREDIT)
                    nc.scalar.activation(th[:, k % 2, :, :], u[:, k % 2, :, :], ACT.Tanh).then_inc(conv_tanh, 1)

                take(0)
                for k in range(NCT):
                    if k + 1 < NCT:
                        take(k + 1)
                    bend(k)
                for j in range(GB):
                    n = GB * g + j
                    act.wait_ge(z_done, n + 1 + CREDIT)
                    act.wait_ge(z_ready, n + CREDIT)
                    nc.scalar.activation(tz[:, :], bk[2][:, 0:DI], ACT.Tanh, scale=0.5).then_inc(z_tanh, 1)
                    act.wait_ge(seg_done, n + 1 + CREDIT)
                    act.wait_ge(mm_ready, n + CREDIT)
                    for x in range(2):
                        last = nc.scalar.activation(dec[:, 3 * x:3 * x + 3, :], bk[4 + x][:, 0:3 * T].rearrange("s (h t) -> s h t", h=3), ACT.Exp)
                    last.then_inc(dec_ready, 1)
                    act.wait_ge(y_ready, n + 1 + CREDIT)
                    act.wait_ge(ms_ready, n + CREDIT)
                    nc.scalar.activation(sq[:, :], y[:, :], ACT.Square, accum_out=ms2[:, :]).then_inc(y_sq, 1)

        @block.vector
        def _(dve):
            dve.wait_ge(weights_in, 16 * W6 + CREDIT)
            nc.vector.memset(pad[:, :, :, 0:DCONV - 1], 0.0)
            nc.vector.tensor_scalar(cw[:, :, :], cw[:, :, :], 0.5, None, ALU.mult).then_inc(tuned, 1)
            nc.vector.tensor_scalar(cb[:, :], cb[:, :], 0.5, None, ALU.mult).then_inc(tuned, 1)
            dve.wait_ge(gate_tanh, 1 + CREDIT)
            nc.vector.tensor_scalar(g1[:, :], g1[:, :], 0.5, 0.5, ALU.mult, ALU.add).then_inc(tuned, 1)
            dve.wait_ge(tuned, 3 + CREDIT)
            with dve.Fori(0, NG) as g:
                c = Chain(dve, chain, g, P6_DVE)

                def taps(k):
                    dve.wait_ge(padded, NCT * g + k + 1 + CREDIT)
                    for w in range(DCONV - 1):
                        ins = nc.vector.scalar_tensor_tensor(out=u[:, k % 2, :, :], in0=pad[:, k % 2, :, w:w + T], scalar=cw[:, k, w:w + 1],
                                                             in1=u[:, k % 2, :, :], op0=ALU.mult, op1=ALU.add)
                        if w == DCONV - 2:
                            ins.then_inc(conv_done, 1)
                        else:
                            c(ins)

                def finish(k):
                    dve.wait_ge(conv_tanh, NCT * g + k + 1 + CREDIT)
                    dve.wait_ge(y_done, GB * g + CREDIT)
                    nc.vector.scalar_tensor_tensor(out=xbc[:, k, :, :], in0=th[:, k % 2, :, :], scalar=1.0, in1=u[:, k % 2, :, :],
                                                   op0=ALU.add, op1=ALU.mult).then_inc(chan_ready, 1)

                taps(0)
                for k in range(NCT):
                    if k + 1 < NCT:
                        taps(k + 1)
                    finish(k)
                for j in range(GB):
                    n = GB * g + j
                    dve.wait_ge(seg_done, n + CREDIT)
                    nc.vector.tensor_tensor(am[:, :, :], da[:, bass.ds(n, 1), :].rearrange("t o h -> t (o h)").unsqueeze(2).to_broadcast([T, NH, T]),
                                            mask2[:, 1, :].unsqueeze(1).to_broadcast([T, NH, T]), ALU.mult).then_inc(am_ready, 1)
                    dve.wait_ge(cb_done, n + 1 + CREDIT)
                    dve.wait_ge(mm_ready, n + CREDIT)
                    nc.vector.tensor_tensor(cbm[:, :], bk[3][:, 0:T], mask2[:, 1, :], ALU.mult).then_inc(cbm_ready, 1)
                    dve.wait_ge(x_flipped, n + 1 + CREDIT)
                    dve.wait_ge(y_done, n + CREDIT)
                    xh = bk[6][:, 0:DI].rearrange("t (h p) -> t h p", h=NH)
                    nc.vector.tensor_tensor(xd[:, :, :], xh, dt[:, bass.ds(n, 1), :].rearrange("t o h -> t (o h)").unsqueeze(2).to_broadcast([T, NH, HP]), ALU.mult)
                    nc.vector.tensor_tensor(xs[:, :, :], xh, dd[:, :].unsqueeze(2).to_broadcast([T, NH, HP]), ALU.mult).then_inc(x_ready, 1)
                    dve.wait_ge(z_tanh, n + 1 + CREDIT)
                    nc.vector.scalar_tensor_tensor(out=sz[:, j % 2, :], in0=tz[:, :], scalar=1.0, in1=bk[2][:, 0:DI], op0=ALU.add, op1=ALU.mult).then_inc(z_ready, 1)
                    dve.wait_ge(dec_ready, n + 1 + CREDIT)
                    dve.wait_ge(cbm_ready, n + 1 + CREDIT)
                    dve.wait_ge(y_done, n + CREDIT)
                    nc.vector.tensor_tensor(mm[:, :, :], dec[:, :, :], cbm[:, :].unsqueeze(1).to_broadcast([T, NH, T]), ALU.mult).then_inc(mm_ready, 1)
                    dve.wait_ge(y_done, n + 1 + CREDIT)
                    dve.wait_ge(x_ready, n + 1 + CREDIT)
                    dve.wait_ge(y_sq, n + CREDIT)
                    dve.wait_ge(y_flipped, n + CREDIT)
                    nc.vector.tensor_tensor(y[:, :], bk[7][:, 0:DI], xs[:, :, :].rearrange("t h p -> t (h p)"), ALU.add).then_inc(y_sum, 1)
                    dve.wait_ge(y_sum, n + 1 + CREDIT)
                    dve.wait_ge(z_ready, n + 1 + CREDIT)
                    nc.vector.scalar_tensor_tensor(out=y[:, :], in0=y[:, :], scalar=0.5, in1=sz[:, j % 2, :], op0=ALU.mult, op1=ALU.mult).then_inc(y_ready, 1)
                    dve.wait_ge(y_sq, n + 1 + CREDIT)
                    nc.vector.tensor_scalar(ms[:, :], ms2[:, :], 1.0 / DI, EPS_GATED, ALU.mult, ALU.add).then_inc(ms_ready, 1)
                    dve.wait_ge(y_flipped, n + 1 + CREDIT)
                    dve.wait_ge(out_done, n + CREDIT)
                    nc.vector.tensor_tensor(yt[:, :, :], bk[6][:, 0:DI].rearrange("p (k t) -> p k t", k=DI // 128),
                                            nw[:, :].unsqueeze(2).to_broadcast([128, DI // 128, T]), ALU.mult).then_inc(yt_ready, 1)
                    dve.wait_ge(rstd_ready, n + 1 + CREDIT)
                    nc.vector.tensor_tensor(rg[:, :], rs[:, :], g1[:, :], ALU.mult).then_inc(scaled, 1)
                    dve.wait_ge(scaled, n + 1 + CREDIT)
                    dve.wait_ge(out_done, n + 1 + CREDIT)
                    dve.wait_ge(h_in, 16 * (g + 1) + CREDIT)
                    nc.vector.scalar_tensor_tensor(out=h[:, j, :], in0=bk[3][:, T:T + D], scalar=rg[:, :], in1=h[:, j, :], op0=ALU.mult, op1=ALU.add).then_inc(h_ready, 1)
                c.close()

        @block.tensor
        def _(pe):
            pe.wait_ge(weights_in, 16 * W6 + CREDIT)
            with pe.Fori(0, NG) as g:
                pe.wait_ge(xt_in, 32 * (g + 1) + CREDIT)
                for k in range(NCT):
                    pe.wait_ge(padded, NCT * g + max(k - 1, 0) + CREDIT)
                    col = DI + 128 * k
                    nc.tensor.matmul(bk[k % 2][:, :], wi0[:, col:col + 128], xt0[:, :], start=True, stop=False)
                    nc.tensor.matmul(bk[k % 2][:, :], wi1[:, col:col + 128], xt1[:, :], start=False, stop=True).then_inc(conv_in, 1)
                for j in range(GB):
                    n = GB * g + j
                    rows_ = slice(j * T, (j + 1) * T)
                    pe.wait_ge(z_ready, n + CREDIT)
                    nc.tensor.matmul(bk[2][:, 0:DI], xt0[:, rows_], wi0[:, 0:DI], start=True, stop=False)
                    nc.tensor.matmul(bk[2][:, 0:DI], xt1[:, rows_], wi1[:, 0:DI], start=False, stop=True).then_inc(z_done, 1)
                    pe.wait_ge(am_ready, n + 1 + CREDIT)
                    pe.wait_ge(dec_ready, n + CREDIT)
                    for x in range(2):
                        last = nc.tensor.matmul(bk[4 + x][:, 0:3 * T], after[:, :], am[:, 3 * x:3 * x + 3, :].rearrange("j h t -> j (h t)"), start=True, stop=True)
                    last.then_inc(seg_done, 1)
                    pe.wait_ge(chan_ready, NCT * (g + 1) + CREDIT)
                    pe.wait_ge(h_ready, n + CREDIT)
                    nc.tensor.matmul(bk[3][:, 0:T], xbc[:, 3, j, :], xbc[:, 4, j, :], start=True, stop=True).then_inc(cb_done, 1)
                    pe.wait_ge(yt_ready, n + CREDIT)
                    for k in range(DI // 128):
                        last = nc.tensor.transpose(bk[6][:, k * 128:(k + 1) * 128], xbc[:, k, j, :], ident[:, :])
                    last.then_inc(x_flipped, 1)
                    pe.wait_ge(mm_ready, n + 1 + CREDIT)
                    pe.wait_ge(x_ready, n + 1 + CREDIT)
                    pe.wait_ge(y_sum, n + CREDIT)
                    for h_ in range(NH):
                        last = nc.tensor.matmul(bk[7][:, h_ * HP:(h_ + 1) * HP], mm[:, h_, :], xd[:, h_, :], start=True, stop=True)
                    last.then_inc(y_done, 1)
                    pe.wait_ge(y_ready, n + 1 + CREDIT)
                    for k in range(DI // 128):
                        last = nc.tensor.transpose(bk[6][:, k * 128:(k + 1) * 128], y[:, k * 128:(k + 1) * 128], ident[:, :])
                    last.then_inc(y_flipped, 1)
                    pe.wait_ge(yt_ready, n + 1 + CREDIT)
                    pe.wait_ge(cbm_ready, n + 1 + CREDIT)
                    for k in range(DI // 128):
                        last = nc.tensor.matmul(bk[3][:, T:T + D], yt[:, k, :], wo[:, k, :], start=(k == 0), stop=(k == DI // 128 - 1))
                    last.then_inc(out_done, 1)


NODES = 21
DEPTH = 11
NPAD = 32
P7_DVE = 17


def feed_forward(nc, a, s, keep):
    LAST = NODES - 1
    with ExitStack() as ctx:
        m = Mem(nc, ctx, "p7")
        sb, sem = m.sb, m.sem
        ident = keep.ident
        wrow, win0, win1, wout = sb("wrow", [NODES, D]), sb("win0", [DL, NODES]), sb("win1", [DH, NODES]), sb("wout", [NPAD, D])
        h, xn, res = sb("h", [T, GB, D]), sb("xn", [T, GB, D]), sb("res", [T, GB, D])
        xt0, xt1 = sb("xt0", [DL, GB * T]), sb("xt1", [DH, GB * T])
        lg, gl, bit = sb("lg", [T, GB, NODES]), sb("gl", [T, GB, NODES]), sb("bit", [T, GB, NODES])
        on, low = sb("on", [T, GB, 16]), sb("low", [T, GB, 6])
        terms = sb("terms", [T, GB, 14])
        coef = sb("coef", [T, GB, NPAD])
        ct = sb("ct", [NPAD, GB * T])
        bk = m.banks()
        nm = Norm(nc, m, 1)
        weights_in, w_flipped, w_copied, zeroed = sem("weights_in"), sem("w_flipped"), sem("w_copied"), sem("zeroed")
        h_in, rows_ready, rows_flipped, cols_a, cols_v = sem("h_in"), sem("rows_ready"), sem("rows_flipped"), sem("cols_a"), sem("cols_v")
        logits_done, logits_copied, gelu_ready, coef_ready, coef_flipped, ct_ready = (
            sem("logits_done"), sem("logits_copied"), sem("gelu_ready"), sem("coef_ready"), sem("coef_flipped"), sem("ct_ready"))
        out_done, res_ready, stored, chain = sem("out_done"), sem("res_ready"), sem("stored"), sem("chain")
        block = m.block()

        @block.sync
        def _(sp):
            sp.dma_start(wrow[:, :], a.L1_ffn_weights_in).then_inc(weights_in, 16)
            sp.wait_ge(zeroed, 1 + CREDIT)
            sp.dma_start(wout[0:NODES, :], a.L1_ffn_weights_out).then_inc(weights_in, 16)
            with sp.Fori(0, NG) as g:
                sp.wait_ge(res_ready, g + CREDIT)
                sp.dma_start(h[:, :, :], s.h[bass.ts(g, GB), :, :].rearrange("b t d -> t b d")).then_inc(h_in, 16)
                sp.wait_ge(res_ready, g + 1 + CREDIT)
                sp.dma_start(keep.out[bass.ts(g, GB), :, :].rearrange("b t d -> t b d"), res[:, :, :]).then_inc(stored, 16)
            sp.wait_ge(stored, 16 * NG + CREDIT)

        @block.gpsimd
        def _(pool):
            nm.pool_start(pool)
            with pool.Fori(0, NG) as g:
                nm.pool(pool, g, 0)

        @block.scalar
        def _(act):
            with act.Fori(0, NG) as g:
                act.wait_ge(rows_flipped, g + 1 + CREDIT)
                act.wait_ge(logits_done, g + CREDIT)
                nc.scalar.activation(xt1[:, :], bk[1][0:DH, :], ACT.Copy).then_inc(cols_a, 1)
                act.wait_ge(logits_copied, g + 1 + CREDIT)
                nc.scalar.activation(gl[:, :, :], lg[:, :, :], ACT.Gelu).then_inc(gelu_ready, 1)

        @block.vector
        def _(dve):
            nc.vector.memset(wout[:, :], 0.0).then_inc(zeroed, 1)
            nc.vector.memset(coef[:, :, :], 0.0)
            dve.wait_ge(w_flipped, 1 + CREDIT)
            nc.vector.tensor_copy(win0[:, :], bk[2][:, 0:NODES])
            nc.vector.tensor_copy(win1[:, :], bk[3][0:DH, 0:NODES]).then_inc(w_copied, 1)
            dve.wait_ge(w_copied, 1 + CREDIT)
            with dve.Fori(0, NG) as g:
                c = Chain(dve, chain, g, P7_DVE)
                dve.wait_ge(h_in, 16 * (g + 1) + CREDIT)
                nm.dve(dve, c, g, 0, lambda j: h[:, j, :], lambda j: xn[:, j, :], 1e-5).then_inc(rows_ready, 1)
                dve.wait_ge(rows_flipped, g + 1 + CREDIT)
                dve.wait_ge(logits_done, g + CREDIT)
                nc.vector.tensor_copy(xt0[:, :], bk[0][:, :]).then_inc(cols_v, 1)
                dve.wait_ge(logits_done, g + 1 + CREDIT)
                nc.vector.tensor_copy(lg[:, :, :], bk[2][:, 0:GB * NPAD].rearrange("t (b n) -> t b n", b=GB)[:, :, 0:NODES]).then_inc(logits_copied, 1)
                dve.wait_ge(logits_copied, g + 1 + CREDIT)
                c(nc.vector.tensor_scalar(bit[:, :, :], lg[:, :, :], 0.0, None, ALU.is_gt))
                tt = nc.vector.tensor_tensor
                nc.vector.tensor_copy(on[:, :, 2], bit[:, :, 0])
                c(nc.vector.tensor_scalar(on[:, :, 1], bit[:, :, 0], -1.0, 1.0, ALU.mult, ALU.add))
                for lo, hi in ((1, 3), (3, 7)):
                    right, left = on[:, :, 2 * lo + 2:2 * hi + 1:2], on[:, :, 2 * lo + 1:2 * hi:2]
                    c(tt(right, on[:, :, lo:hi], bit[:, :, lo:hi], ALU.mult))
                    c(tt(left, on[:, :, lo:hi], right, ALU.subtract))
                c(tt(low[:, :, 1:4:2], on[:, :, 7:9], bit[:, :, 7:9], ALU.mult))
                c(tt(low[:, :, 0:3:2], on[:, :, 7:9], low[:, :, 1:4:2], ALU.subtract))
                c(tt(low[:, :, 4], on[:, :, 9], bit[:, :, 9], ALU.mult))
                c(tt(low[:, :, 4], on[:, :, 9], low[:, :, 4], ALU.subtract))
                c(nc.vector.tensor_reduce(low[:, :, 5], low[:, :, 0:5], AX.X, ALU.add))
                c(nc.vector.tensor_scalar(low[:, :, 5], low[:, :, 5], -1.0, 1.0, ALU.mult, ALU.add))
                dve.wait_ge(gelu_ready, g + 1 + CREDIT)
                twice = lambda lo, hi: gl[:, :, lo:hi].unsqueeze(3).to_broadcast([T, GB, hi - lo, 2])
                pairs = lambda v: v.rearrange("t b (n k) -> t b n k", k=2)
                c(tt(coef[:, :, 1:3], on[:, :, 1:3], gl[:, :, 0:1].to_broadcast([T, GB, 2]), ALU.mult))
                tt(pairs(coef[:, :, 3:7]), pairs(on[:, :, 3:7]), twice(1, 3), ALU.mult)
                tt(pairs(coef[:, :, 7:15]), pairs(on[:, :, 7:15]), twice(3, 7), ALU.mult)
                tt(pairs(coef[:, :, 15:19]), pairs(low[:, :, 0:4]), twice(7, 9), ALU.mult)
                c(tt(coef[:, :, 19], low[:, :, 4], gl[:, :, 9], ALU.mult))
                tt(terms[:, :, 0:6], on[:, :, 9:15], gl[:, :, 9:15], ALU.mult)
                tt(terms[:, :, 6:12], low[:, :, :], gl[:, :, 15:NODES], ALU.mult)
                nc.vector.tensor_scalar(terms[:, :, 12], gl[:, :, LAST], float(DEPTH - 6), None, ALU.mult)
                c(nc.vector.tensor_scalar(terms[:, :, 13], coef[:, :, 19], -1.0, None, ALU.mult))
                nc.vector.tensor_reduce(coef[:, :, LAST], terms[:, :, :], AX.X, ALU.add).then_inc(coef_ready, 1)
                dve.wait_ge(coef_flipped, g + 1 + CREDIT)
                nc.vector.tensor_copy(ct[:, :], bk[3][0:NPAD, :]).then_inc(ct_ready, 1)
                dve.wait_ge(out_done, g + 1 + CREDIT)
                dve.wait_ge(stored, 16 * g + CREDIT)
                for x in range(2):
                    last = tt(res[:, 2 * x:2 * x + 2, :], h[:, 2 * x:2 * x + 2, :], bk[4 + x][:, 0:2 * D].rearrange("t (b d) -> t b d", b=2), ALU.add)
                last.then_inc(res_ready, 1)
                c.close()

        @block.tensor
        def _(pe):
            pe.wait_ge(weights_in, 32 + CREDIT)
            nc.tensor.transpose(bk[2][:, 0:NODES], wrow[:, 0:DL], ident[0:NODES, 0:NODES])
            nc.tensor.transpose(bk[3][0:DH, 0:NODES], wrow[:, DL:D], ident[0:NODES, 0:NODES]).then_inc(w_flipped, 1)
            pe.wait_ge(w_copied, 1 + CREDIT)
            with pe.Fori(0, NG) as g:
                pe.wait_ge(rows_ready, g + 1 + CREDIT)
                for j in range(GB):
                    nc.tensor.transpose(bk[0][:, j * T:(j + 1) * T], xn[:, j, 0:DL], ident[:, :])
                for j in range(GB):
                    last = nc.tensor.transpose(bk[1][0:DH, j * T:(j + 1) * T], xn[:, j, DL:D], ident[:, :])
                last.then_inc(rows_flipped, 1)
                pe.wait_ge(cols_a, g + 1 + CREDIT)
                pe.wait_ge(cols_v, g + 1 + CREDIT)
                for j in range(GB):
                    out = bk[2][:, NPAD * j:NPAD * j + NODES]
                    nc.tensor.matmul(out, xt0[:, j * T:(j + 1) * T], win0[:, :], start=True, stop=False)
                    last = nc.tensor.matmul(out, xt1[:, j * T:(j + 1) * T], win1[:, :], start=False, stop=True)
                last.then_inc(logits_done, 1)
                pe.wait_ge(coef_ready, g + 1 + CREDIT)
                for j in range(GB):
                    last = nc.tensor.transpose(bk[3][0:NPAD, j * T:(j + 1) * T], coef[:, j, :], ident[:, :])
                last.then_inc(coef_flipped, 1)
                pe.wait_ge(ct_ready, g + 1 + CREDIT)
                for j in range(GB):
                    last = nc.tensor.matmul(bk[4 + j // 2][:, j % 2 * D:(j % 2 + 1) * D], ct[:, j * T:(j + 1) * T], wout[:, :], start=True, stop=True)
                last.then_inc(out_done, 1)


SCRATCH_KIND = "Internal"


class Keep:
    pass


def build(nc, a, s, out):
    with ExitStack() as ctx:
        m = Mem(nc, ctx, "keep")
        keep = Keep()
        keep.out = out
        keep.ident = m.sb("ident", [128, 128])
        keep.mask2 = m.sb("mask2", [T, 2, T])
        with ExitStack() as ttt:
            keep.hist = Mem(nc, ttt, "ttt").sb("hist", [T, B, D])
            ttt_prepare(nc, a, s, keep)
            ttt_scan(nc, a, s, keep)
            ttt_finish(nc, a, s, keep)
        moe(nc, a, s, keep)
        second_layer(nc, a, s, keep)


class Arrays:
    pass


def _constants():
    import numpy as np
    i = np.arange(T)
    col = np.arange(EXP_COLS)
    expert = np.minimum(col // D, NE)
    return {
        "c_ident": np.eye(128, dtype=np.float32),
        "c_mask2": np.stack([i[:, None] < i[None, :], i[:, None] <= i[None, :]], axis=1).astype(np.float32),
        "c_after": (i[:, None] > i[None, :]).astype(np.float32),
        "c_expand": np.concatenate([np.arange(NE + 1)[:, None] == expert[None, :]] * 3 + [np.zeros((5, EXP_COLS), bool)]).astype(np.float32),
        "c_iota": np.broadcast_to(np.arange(NE, dtype=np.float32), (128, NE)).copy(),
    }


def kernel(**inputs):
    import numpy as np
    import concourse.bacc as bacc
    from concourse.bass_utils import run_bass_kernel_spmd

    nc = bacc.Bacc("TRN2", target_bir_lowering=False, num_devices=1)
    arrays, a, s = {}, Arrays(), Arrays()
    for name, value in list(inputs.items()) + list(_constants().items()):
        v = np.ascontiguousarray(value).reshape(np.shape(value) or (1,))
        arrays[f"in_{name}"] = v
        a.__dict__[name] = nc.dram_tensor(f"in_{name}", v.shape, mybir.dt.from_np(v.dtype), kind="ExternalInput").ap()
    scratch = {"pt": (2 * LOG_POS, D), "h": (B, T, D), "zc": (B, T, 2 * D), "qz": (B, T, 2 * D),
               "mk": (B, T, NC, H, C), "mq": (B, T, H, T), "g": (B, T, D), "corr": (B, C, D), "xt": (NG, D, GB * T)}
    for name, shape in scratch.items():
        s.__dict__[name] = nc.dram_tensor(f"s_{name}", shape, F32, kind=SCRATCH_KIND).ap()
    out = nc.dram_tensor("out_h", (B, T, D), F32, kind="ExternalOutput").ap()
    build(nc, a, s, out)
    r = run_bass_kernel_spmd(nc, [arrays], core_ids=[0])
    return r.results[0]["out_h"]
```

```python
import concourse.bass as bass
from concourse import mybir
from contextlib import ExitStack

F32 = mybir.dt.float32
BF16 = mybir.dt.bfloat16
I32 = mybir.dt.int32
U32 = mybir.dt.uint32
ACT = mybir.ActivationFunctionType
ALU = mybir.AluOpType
AX = mybir.AxisListType

B, T, D = 128, 128, 192
GB = 4
NG = B // GB
DL, DH = 128, D - 128
H, HD = 3, 64
C = 16
NC = T // C
CREDIT = 1
LOG_POS = 128
P1_DVE = 9
EMBED_LINKS = 5


class Chain:

    def __init__(self, eng, sem, turn=0, per=0, start=0):
        self.eng, self.sem, self.base, self.per, self.n = eng, sem, turn * per + start, per, 0

    def __call__(self, ins):
        ins.then_inc(self.sem, 1)
        self.n += 1
        self.eng.wait_ge(self.sem, self.base + self.n + CREDIT)

    def close(self):
        assert self.n == self.per, f"chain has {self.n} links, not {self.per}"


class Mem:

    def __init__(self, nc, ctx, tag):
        self.nc, self.ctx, self.tag, self.sems = nc, ctx, tag, []

    def sb(self, name, shape, dt=F32):
        return self.ctx.enter_context(self.nc.sbuf_tensor(f"{self.tag}_{name}", shape, dt))

    def banks(self, n=8):
        return [self.ctx.enter_context(self.nc.psum_tensor(f"{self.tag}_bank{i}", [128, 512], F32)) for i in range(n)]

    def sem(self, name):
        self.sems.append(self.sem_of_pool_dma(name))
        return self.sems[-1]

    def sem_of_pool_dma(self, name):
        return self.ctx.enter_context(self.nc.semaphore(f"{self.tag}_{name}"))

    def block(self):
        with self.nc.Block() as credits:
            @credits.sync
            def _(sp):
                for sem in self.sems:
                    sp.sem_clear(sem)
                    sp.sem_inc(sem, CREDIT)
        return self.ctx.enter_context(self.nc.Block())


def rows(ap, n):
    return ap[None, :].to_broadcast([n, ap.shape[0]])


def ttt_prepare(nc, a, s, keep):
    with ExitStack() as ctx:
        m = Mem(nc, ctx, "p1")
        sb, sem = m.sb, m.sem
        ident, mask2 = keep.ident, keep.mask2
        xi, ti = sb("xi", [B, T], I32), sb("ti", [B, T], I32)
        xf, tf, pf, junk, junk_pool = sb("xf", [B, T]), sb("tf", [B, T]), sb("pf", [B, T]), sb("junk", [128, 1]), sb("junk_pool", [128, 1])
        idx, idx_now = sb("idx", [T, 2, B], I32), sb("idx_now", [T, 2, GB], I32)
        pt = sb("pt", [LOG_POS, 2, D])
        typ = sb("typ", [128, 2, D])
        gam_tok, bet_tok = sb("gam_tok", [128, D]), sb("bet_tok", [128, D])
        wd0, wd1 = sb("wd0", [DL, D]), sb("wd1", [DH, D])
        bd0, bd1 = sb("bd0", [DL, 1]), sb("bd1", [DH, 1])
        NW = 3 * D + H
        wc0, wc1 = sb("wc0", [DL, NW]), sb("wc1", [DH + 1, NW])
        wk0, wk1 = sb("wk0", [DL, D]), sb("wk1", [DH, D])
        gam = sb("gam", [128, D])
        w1 = sb("w1", [HD + 1, H, HD])
        w1m = sb("w1m", [HD + 1, H])
        half = sb("half", [128, GB])
        te, pe_ = sb("te", [128, GB, D]), sb("pe", [128, GB, D])
        st, mv, rs = sb("st", [128, GB, 6]), sb("mv", [128, GB, 2]), sb("rs", [128, 2, GB])
        h0 = sb("h0", [128, GB, D])
        xn = sb("xn", [128, GB, D])
        xt0, xt1 = sb("xt0", [DL, GB, T]), sb("xt1", [DH, GB, T])
        ht0, ht1 = sb("ht0", [DL, GB, T]), sb("ht1", [DH + 1, GB, T])
        ksb = sb("ksb", [128, 2, D])
        eta = sb("eta", [128, 2, H])
        qz, zc = sb("qz", [128, GB, 2 * D]), sb("zc", [128, GB, 2 * D])
        kqt = sb("kqt", [HD + 1, 2, H, 2, T])
        mk, mq = sb("mk", [128, 2, NC, H, C]), sb("mq", [128, 2, H, T])
        bk = m.banks()

        ids_in, setup_done, idx_t, idx_out = sem("ids_in"), sem("setup_done"), sem("idx_t"), sem("idx_out")
        weights_in, pt_ready, pt_stored, act_chain, dve_chain, pool_chain = (
            sem("weights_in"), sem("pt_ready"), sem("pt_stored"), sem("act_chain"), sem("dve_chain"), sem("pool_chain"))
        setup_chain, half_set = sem("setup_chain"), sem("half_set")
        emb_sum, base_half = sem("emb_sum"), sem("base_half")
        gathered, emb_read, var_ready, rstd_ready = keep.gathered, sem("emb_read"), sem("var_ready"), sem("rstd_ready")
        h0_ready, h0_stored, xn_ready = sem("h0_ready"), sem("h0_stored"), sem("xn_ready")
        xt_done, xt_copied_a, xt_copied_v, ht_done, ht_ready = (
            sem("xt_done"), sem("xt_copied_a"), sem("xt_copied_v"), sem("ht_done"), sem("ht_ready"))
        qkv_done, qk_copied, c_copied, eta_tanh, eta_copied = sem("qkv_done"), sem("qk_copied"), sem("c_copied"), sem("eta_tanh"), sem("eta_copied")
        kqt_done, kqt_copied_a, kqt_copied_v = sem("kqt_done"), sem("kqt_copied_a"), sem("kqt_copied_v")
        gram_done, m_ready, base_copied = sem("gram_done"), sem("m_ready"), sem("base_copied")
        zq_stored = [sem(f"zq_stored_{j}") for j in range(GB)]
        m_stored = [sem(f"m_stored_{p}") for p in range(2)]

        block = m.block()

        @block.sync
        def _(sp):
            sp.dma_start(ident[:, :], a.c_ident).then_inc(ids_in, 16)
            sp.dma_start(mask2[:, :, :], a.c_mask2).then_inc(ids_in, 16)
            sp.dma_start(xi[:, :], a.x).then_inc(ids_in, 16)
            sp.dma_start(ti[:, :], a.mask_BS_i1_0).then_inc(ids_in, 16)
            sp.dma_start(pt[:, 0, :], a.L0_tok_pos_table).then_inc(ids_in, 16)
            sp.dma_start(pt[:, 1, :], a.L0_tok_pos_table).then_inc(ids_in, 16)
            for k in range(2):
                sp.dma_start(typ[:, k, :], rows(a.L0_tok_type_table[k, :], 128)).then_inc(ids_in, 16)
            loads = [
                (gam_tok[:, :], rows(a.L0_tok_gamma, 128)), (bet_tok[:, :], rows(a.L0_tok_beta, 128)),
                (wd0[:, :], a.L0_attn_W_down[0:DL, :]), (wd1[:, :], a.L0_attn_W_down[DL:D, :]),
                (bd0[:, :], a.L0_attn_b_down[0:DL, None]), (bd1[:, :], a.L0_attn_b_down[DL:D, None]),
                (wk0[:, :], a.L0_attn_Wk[0:DL, :]), (wk1[:, :], a.L0_attn_Wk[DL:D, :]),
                (gam[:, :], rows(a.L0_attn_ttt_g.rearrange("h e -> (h e)"), 128)),
                (w1[0:HD, :, :], a.L0_attn_W1.rearrange("h d e -> d h e")),
                (w1[HD:HD + 1, :, :], a.L0_attn_b1.rearrange("h o e -> o h e")),
                (wc1[DH:DH + 1, 2 * D:3 * D], a.L0_attn_ttt_b.rearrange("h e -> (h e)")[None, :]),
                (wc1[DH:DH + 1, 3 * D:NW], a.L0_attn_lr_b[None, :]),
            ]
            for dst, lo, hi in ((wc0, 0, DL), (wc1, DL, D)):
                n = hi - lo
                loads += [(dst[0:n, 0:D], a.L0_attn_Wq[lo:hi, :]), (dst[0:n, D:2 * D], a.L0_attn_Wk[lo:hi, :]),
                          (dst[0:n, 2 * D:3 * D], a.L0_attn_Wv[lo:hi, :]), (dst[0:n, 3 * D:NW], a.L0_attn_lr_w[lo:hi, :])]
            assert len(loads) == 21
            for dst, src in loads:
                sp.dma_start(dst, src).then_inc(weights_in, 16)
            sp.wait_ge(pt_ready, 1 + CREDIT)
            sp.dma_start(s.pt.rearrange("(k p) d -> p k d", p=LOG_POS), pt[:, :, :]).then_inc(pt_stored, 16)

            def store_h0(g):
                sp.wait_ge(h0_ready, g + 1 + CREDIT)
                sp.dma_start(s.h[bass.ts(g, GB), :, :].rearrange("b t d -> t b d"), h0[:, :, :]).then_inc(h0_stored, 16)

            def turn(g, last):
                for j in range(GB):
                    b = g * GB + j
                    sp.wait_ge(m_ready, g * GB + j + 1 + CREDIT)
                    sp.dma_start(s.mk[bass.ds(b, 1), :, :, :, :].rearrange("o s c h t -> (o s) (c h t)"),
                                 mk[:, j % 2, :, :, :].rearrange("s c h t -> s (c h t)")).then_inc(m_stored[j % 2], 16)
                    sp.dma_start(s.mq[bass.ds(b, 1), :, :, :].rearrange("o s h t -> (o s) (h t)"),
                                 mq[:, j % 2, :, :].rearrange("s h t -> s (h t)")).then_inc(m_stored[j % 2], 16)
                    sp.wait_ge(base_copied, g * GB + j + 1 + CREDIT)
                    sp.wait_ge(c_copied, g * GB + j + 1 + CREDIT)
                    sp.dma_start(s.zc[bass.ds(b, 1), :, :].rearrange("o t d -> (o t) d"), zc[:, j, :]).then_inc(zq_stored[j], 16)
                    sp.dma_start(s.qz[bass.ds(b, 1), :, :].rearrange("o t d -> (o t) d"), qz[:, j, :]).then_inc(zq_stored[j], 16)
                    if j == 1 and not last:
                        store_h0(g + 1)

            store_h0(0)
            with sp.Fori(0, NG - 1) as g:
                turn(g, False)
            turn(NG - 1, True)
            sp.wait_ge(h0_stored, 16 * NG + CREDIT)
            for p in range(2):
                sp.wait_ge(m_stored[p], 32 * B // 2 + CREDIT)
            for j in range(GB):
                sp.wait_ge(zq_stored[j], 32 * NG + CREDIT)

        @block.gpsimd
        def _(pool):
            nc.gpsimd.memset(half[:, :], -0.5).then_inc(half_set, 1)
            pool.wait_ge(half_set, 1 + CREDIT)
            pool.wait_ge(idx_out, 2 + CREDIT)
            pool.wait_ge(pt_stored, 16 + CREDIT)
            with pool.Fori(0, NG) as g:
                pool.wait_ge(emb_read, g + CREDIT)
                nc.gpsimd.tensor_tensor(junk_pool[:, :], half[:, 0:1], half[:, 0:1], ALU.mult)
                nc.gpsimd.tensor_copy(idx_now[:, :, :], idx[:, :, bass.ts(g, GB)]).then_inc(pool_chain, 1)
                pool.wait_ge(pool_chain, g + 1 + CREDIT)
                nc.gpsimd.tensor_tensor(junk_pool[:, :], half[:, 0:1], half[:, 0:1], ALU.mult)
                for j in range(GB):
                    nc.gpsimd.indirect_dma_start(
                        out=te[:, j, :], out_offset=None, in_=a.L0_tok_tok_table,
                        in_offset=bass.IndirectOffsetOnAxis(ap=idx_now[:, 0, j:j + 1].bitcast(U32), axis=0),
                    ).then_inc(gathered, 16)
                    nc.gpsimd.indirect_dma_start(
                        out=pe_[:, j, :], out_offset=None, in_=s.pt,
                        in_offset=bass.IndirectOffsetOnAxis(ap=idx_now[:, 1, j:j + 1].bitcast(U32), axis=0),
                    ).then_inc(gathered, 16)
                for k in range(2):
                    pool.wait_ge(var_ready, 2 * g + k + 1 + CREDIT)
                    nc.gpsimd.tensor_tensor(rs[:, k, :], mv[:, :, 1], half[:, :], ALU.pow).then_inc(rstd_ready, 1)

        @block.scalar
        def _(act):
            def columns(g):
                act.wait_ge(xt_done, g + 1 + CREDIT)
                act.wait_ge(ht_done, g + CREDIT)
                nc.scalar.activation(xt1[:, :, :], bk[1][0:DH, :].rearrange("p (j t) -> p j t", j=GB), ACT.Copy).then_inc(xt_copied_a, 1)

            def hidden(g):
                act.wait_ge(ht_done, g + 1 + CREDIT)
                act.wait_ge(qkv_done, g * GB + CREDIT)
                nc.scalar.activation(ht0[:, :, :], bk[4][:, :].rearrange("p (j t) -> p j t", j=GB), ACT.Silu, bias=bd0[:, :])
                nc.scalar.activation(ht1[0:DH, :, :], bk[3][0:DH, :].rearrange("p (j t) -> p j t", j=GB), ACT.Silu, bias=bd1[:, :]).then_inc(ht_ready, 1)

            def turn(g, last):
                def copy_qk(j):
                    p = j % 2
                    act.wait_ge(qkv_done, g * GB + j + 1 + CREDIT)
                    act.wait_ge(zq_stored[j], 32 * g + CREDIT)
                    nc.scalar.activation(qz[:, j, 0:D], bk[4 + p][:, 0:D], ACT.Copy).then_inc(qk_copied, 1)
                    nc.scalar.activation(ksb[:, p, :], bk[4 + p][:, D:2 * D], ACT.Copy).then_inc(qk_copied, 1)
                    act.wait_ge(eta_copied, g * GB + j + 1 + CREDIT)
                    nc.scalar.activation(eta[:, p, :], eta[:, p, :], ACT.Tanh, scale=0.5).then_inc(eta_tanh, 1)

                def copy_kqt(j):
                    p = j % 2
                    act.wait_ge(kqt_done, g * GB + j + 1 + CREDIT)
                    if j >= 2:
                        act.wait_ge(gram_done, g * GB + j - 1 + CREDIT)
                    else:
                        act.wait_ge(gram_done, g * GB + CREDIT)
                    nc.scalar.activation(kqt[0:HD, p, 2, :, :], bk[1][0:HD, 0:2 * T].rearrange("p (q t) -> p q t", q=2), ACT.Copy).then_inc(kqt_copied_a, 1)

                def copy_base(j):
                    p = j % 2
                    act.wait_ge(gram_done, g * GB + j + 1 + CREDIT)
                    nc.scalar.activation(zc[:, j, 0:D], bk[4 + p][:, 0:D], ACT.Copy).then_inc(base_half, 1)
                    act.wait_ge(base_half, g * GB + j + 1 + CREDIT)
                    nc.scalar.activation(qz[:, j, D:2 * D], bk[4 + p][:, D:2 * D], ACT.Copy).then_inc(base_copied, 1)

                for step in range(GB + 2):
                    if step == GB + 1 and not last:
                        columns(g + 1)
                    if step >= 2:
                        copy_base(step - 2)
                    if 1 <= step < GB + 1:
                        copy_kqt(step - 1)
                    if step < GB:
                        copy_qk(step)
                if not last:
                    hidden(g + 1)

            columns(0)
            hidden(0)
            with act.Fori(0, NG - 1) as g:
                turn(g, False)
            turn(NG - 1, True)

        @block.vector
        def _(dve):
            setup = Chain(dve, setup_chain)
            dve.wait_ge(ids_in, 8 * 16 + CREDIT)
            setup(nc.vector.tensor_copy(xf[:, :], xi[:, :]))
            setup(nc.vector.tensor_copy(tf[:, :], ti[:, :]))
            setup(nc.vector.tensor_scalar(pf[:, :], xf[:, :], float(LOG_POS - 1), None, ALU.min))
            setup(nc.vector.scalar_tensor_tensor(out=tf[:, :], in0=tf[:, :], scalar=float(LOG_POS), in1=pf[:, :],
                                                 op0=ALU.mult, op1=ALU.add))
            nc.vector.tensor_tensor(pt[:, :, :], pt[:, :, :], typ[:, :, :], ALU.add).then_inc(pt_ready, 1)
            setup(nc.vector.memset(ht1[DH:DH + 1, :, :], 1.0))
            setup(nc.vector.memset(kqt[HD:HD + 1, :, :, :, :], 1.0))
            dve.wait_ge(weights_in, 21 * 16 + CREDIT)
            for w, k, n in ((wc0, wk0, DL), (wc1, wk1, DH)):
                wv = w[0:n, 2 * D:3 * D]
                setup(nc.vector.tensor_tensor(wv, wv, k[:, :], ALU.subtract))
                setup(nc.vector.tensor_tensor(wv, wv, gam[0:n, :], ALU.mult))
            bias = wc1[DH:DH + 1, 2 * D:3 * D]
            setup(nc.vector.scalar_tensor_tensor(out=bias, in0=bias, scalar=-1.0, in1=gam[DH:DH + 1, :], op0=ALU.mult, op1=ALU.mult))
            setup(nc.vector.memset(wc1[DH:DH + 1, 0:2 * D], 0.0))
            setup(nc.vector.tensor_reduce(w1m[:, :], w1[:, :, :], AX.X, ALU.add))
            setup(nc.vector.tensor_scalar(w1m[:, :], w1m[:, :], 1.0 / HD, None, ALU.mult))
            setup(nc.vector.tensor_tensor(w1[:, :, :], w1[:, :, :], w1m[:, :].unsqueeze(2).to_broadcast([HD + 1, H, HD]), ALU.subtract))
            dve.wait_ge(idx_t, 2 + CREDIT)
            nc.vector.tensor_copy(idx[:, 0, :], bk[0][:, 0:B]).then_inc(idx_out, 1)
            nc.vector.tensor_copy(idx[:, 1, :], bk[1][:, 0:B]).then_inc(idx_out, 1)
            nc.vector.memset(junk[:, :], 0.0).then_inc(setup_done, 1)

            def variances(src, eps, c):
                for j in range(GB):
                    last = nc.vector.bn_stats(st[:, j, :], src[:, j, :])
                c(last)
                nc.vector.memset(junk[:, :], 0.0)
                for j in range(GB):
                    last = nc.vector.bn_aggr(mv[:, j, :], st[:, j, :])
                c(last)
                nc.vector.tensor_scalar(mv[:, :, 1], mv[:, :, 1], eps, None, ALU.add).then_inc(var_ready, 1)

            def normalise(dst, src, k, g):
                dve.wait_ge(rstd_ready, 2 * g + k + 1 + CREDIT)
                for j in range(GB):
                    last = nc.vector.tensor_scalar(dst[:, j, :], src[:, j, :], mv[:, j, 0:1], rs[:, k, j:j + 1], ALU.subtract, ALU.mult)
                return last

            def embed(g, c):
                dve.wait_ge(gathered, (g + 1) * (2 * GB * 16))
                nc.vector.tensor_tensor(te[:, :, :], te[:, :, :], pe_[:, :, :], ALU.add).then_inc(emb_sum, 1)
                dve.wait_ge(emb_sum, g + 1 + CREDIT)
                dve.wait_ge(xn_ready, g + CREDIT)
                variances(te, 1e-12, c)

            def residual(g, c):
                dve.wait_ge(h0_stored, 16 * g + CREDIT)
                c(normalise(h0, te, 0, g))
                bc = lambda v: v[:, :].unsqueeze(1).to_broadcast([128, GB, D])
                nc.vector.tensor_tensor(h0[:, :, :], h0[:, :, :], bc(gam_tok), ALU.mult).then_inc(emb_read, 1)
                dve.wait_ge(emb_read, g + 1 + CREDIT)
                nc.vector.tensor_tensor(h0[:, :, :], h0[:, :, :], bc(bet_tok), ALU.add).then_inc(h0_ready, 1)
                dve.wait_ge(h0_ready, g + 1 + CREDIT)
                variances(h0, 1e-5, c)

            def normed(g):
                dve.wait_ge(xt_done, g + CREDIT)
                normalise(xn, h0, 1, g).then_inc(xn_ready, 1)

            def columns(g):
                dve.wait_ge(xt_done, g + 1 + CREDIT)
                nc.vector.tensor_copy(xt0[:, :, :], bk[0][:, :].rearrange("p (j t) -> p j t", j=GB)).then_inc(xt_copied_v, 1)

            def turn(g, last_turn):
                c = Chain(dve, dve_chain, g, P1_DVE, EMBED_LINKS)

                def copy_c(j):
                    p = j % 2
                    dve.wait_ge(qkv_done, g * GB + j + 1 + CREDIT)
                    dve.wait_ge(zq_stored[j], 32 * g + CREDIT)
                    nc.vector.tensor_copy(eta[:, p, :], bk[6 + p][:, D:D + H]).then_inc(eta_copied, 1)
                    nc.vector.tensor_copy(zc[:, j, D:2 * D], bk[6 + p][:, 0:D]).then_inc(c_copied, 1)
                    dve.wait_ge(eta_tanh, g * GB + j + 1 + CREDIT)
                    c(nc.vector.tensor_scalar(eta[:, p, :], eta[:, p, :], 0.5 / HD, 0.5 / HD, ALU.mult, ALU.add))

                def copy_kqt(j):
                    p = j % 2
                    dve.wait_ge(kqt_done, g * GB + j + 1 + CREDIT)
                    if j >= 2:
                        dve.wait_ge(gram_done, g * GB + j - 1 + CREDIT)
                    else:
                        dve.wait_ge(gram_done, g * GB + CREDIT)
                    nc.vector.tensor_copy(kqt[0:HD, p, 0:2, :, :], bk[0][0:HD, :].rearrange("p (h q t) -> p h q t", h=2, q=2)).then_inc(kqt_copied_v, 1)

                def gram_scale(j):
                    p = j % 2
                    dve.wait_ge(gram_done, g * GB + j + 1 + CREDIT)
                    dve.wait_ge(m_stored[p], 32 * (g * (GB // 2) + j // 2) + CREDIT)
                    for h in range(H):
                        gr = bk[2][:, h * 2 * T:(h + 1) * 2 * T] if h < 2 else bk[6 + p][:, 2 * T:4 * T]
                        nc.vector.scalar_tensor_tensor(
                            out=mk[:, p, :, h, :], in0=gr[:, 0:T].rearrange("p (c t) -> p c t", c=NC), scalar=eta[:, p, h:h + 1],
                            in1=mask2[:, 0, :].rearrange("p (c t) -> p c t", c=NC), op0=ALU.mult, op1=ALU.mult)
                        last = nc.vector.scalar_tensor_tensor(
                            out=mq[:, p, h, :], in0=gr[:, T:2 * T], scalar=eta[:, p, h:h + 1],
                            in1=mask2[:, 1, :], op0=ALU.mult, op1=ALU.mult)
                    last.then_inc(m_ready, 1)

                for step in range(GB + 2):
                    if step == GB + 1 and not last_turn:
                        columns(g + 1)
                    if step >= 2:
                        gram_scale(step - 2)
                    if 1 <= step < GB + 1:
                        copy_kqt(step - 1)
                    if step < GB:
                        copy_c(step)
                    if not last_turn:
                        if step == 2:
                            embed(g + 1, c)
                        elif step == 3:
                            residual(g + 1, c)
                        elif step == 4:
                            normed(g + 1)
                if not last_turn:
                    c.close()

            first = Chain(dve, dve_chain, 0, EMBED_LINKS)
            embed(0, first)
            residual(0, first)
            normed(0)
            first.close()
            columns(0)
            with dve.Fori(0, NG - 1) as g:
                turn(g, False)
            turn(NG - 1, True)

        @block.tensor
        def _(pe):
            pe.wait_ge(ids_in, 8 * 16 + CREDIT)
            pe.wait_ge(setup_chain, 4 + CREDIT)
            nc.tensor.transpose(bk[0][:, 0:B], xf[:, :], ident[:, :]).then_inc(idx_t, 1)
            nc.tensor.transpose(bk[1][:, 0:B], tf[:, :], ident[:, :]).then_inc(idx_t, 1)
            pe.wait_ge(setup_done, 1 + CREDIT)

            def flip_rows(g):
                pe.wait_ge(xn_ready, g + 1 + CREDIT)
                pe.wait_ge(kqt_copied_v, g * GB + CREDIT)
                pe.wait_ge(kqt_copied_a, g * GB + CREDIT)
                for j in range(GB):
                    nc.tensor.transpose(bk[0][:, j * T:(j + 1) * T], xn[:, j, 0:DL], ident[:, :])
                for j in range(GB):
                    last = nc.tensor.transpose(bk[1][0:DH, j * T:(j + 1) * T], xn[:, j, DL:D], ident[:, :])
                last.then_inc(xt_done, 1)

            def down(g):
                pe.wait_ge(xt_copied_v, g + 1 + CREDIT)
                pe.wait_ge(xt_copied_a, g + 1 + CREDIT)
                if not isinstance(g, int) or g > 0:
                    pe.wait_ge(base_copied, g * GB - 1 + CREDIT)
                for bank, lo, n in ((bk[4], 0, DL), (bk[3], DL, DH)):
                    nc.tensor.matmul(bank[0:n, :], wd0[:, lo:lo + n], xt0[:, :, :].rearrange("p j t -> p (j t)"), start=True, stop=False)
                    last = nc.tensor.matmul(bank[0:n, :], wd1[:, lo:lo + n], xt1[:, :, :].rearrange("p j t -> p (j t)"), start=False, stop=True)
                last.then_inc(ht_done, 1)

            def turn(g, last_turn):
                pe.wait_ge(ht_ready, g + 1 + CREDIT)

                def qkv(j):
                    p = j % 2
                    n = g * GB + max(j - 1, 0)
                    pe.wait_ge(base_copied, n + CREDIT)
                    pe.wait_ge(m_ready, n + CREDIT)
                    for bank, lo, w in ((bk[4 + p], 0, 2 * D), (bk[6 + p], 2 * D, D + H)):
                        nc.tensor.matmul(bank[:, 0:w], ht0[:, j, :], wc0[:, lo:lo + w], start=True, stop=False)
                        last = nc.tensor.matmul(bank[:, 0:w], ht1[:, j, :], wc1[:, lo:lo + w], start=False, stop=True)
                    last.then_inc(qkv_done, 1)

                def flip(j):
                    p = j % 2
                    pe.wait_ge(qk_copied, 2 * (g * GB + j + 1) + CREDIT)
                    pe.wait_ge(kqt_copied_v, g * GB + j + CREDIT)
                    pe.wait_ge(kqt_copied_a, g * GB + j + CREDIT)
                    nc.tensor.transpose(bk[0][:, 0:T], ident[:, :], ident[:, :])
                    for h in range(H):
                        for q in range(2):
                            src = qz[:, j, h * HD:(h + 1) * HD] if q else ksb[:, p, h * HD:(h + 1) * HD]
                            col = (2 * h + q) % 4 * T
                            last = nc.tensor.transpose(bk[h // 2][0:HD, col:col + T], src, ident[:, :])
                    last.then_inc(kqt_done, 1)

                def gram(j):
                    p = j % 2
                    pe.wait_ge(kqt_copied_v, g * GB + j + 1 + CREDIT)
                    pe.wait_ge(kqt_copied_a, g * GB + j + 1 + CREDIT)
                    pe.wait_ge(m_ready, g * GB + j + CREDIT)
                    pe.wait_ge(c_copied, g * GB + j + 1 + CREDIT)
                    for h in range(H):
                        out = bk[2][:, h * 2 * T:(h + 1) * 2 * T] if h < 2 else bk[6 + p][:, 2 * T:4 * T]
                        nc.tensor.matmul(out, kqt[:, p, h, 0, :], kqt[:, p, h, :, :].rearrange("p q t -> p (q t)"), start=True, stop=True)
                    for q in range(2):
                        for h in range(H):
                            col = q * D + h * HD
                            last = nc.tensor.matmul(bk[4 + p][:, col:col + HD], kqt[:, p, h, q, :], w1[:, h, :], start=True, stop=True)
                    last.then_inc(gram_done, 1)

                for step in range(GB + 2):
                    if step == GB + 1 and not last_turn:
                        flip_rows(g + 1)
                    if step >= 2:
                        gram(step - 2)
                    if 1 <= step < GB + 1:
                        flip(step - 1)
                    if step < GB:
                        qkv(step)
                if not last_turn:
                    down(g + 1)

            flip_rows(0)
            down(0)
            with pe.Fori(0, NG - 1) as g:
                turn(g, False)
            turn(NG - 1, True)


EPS_TTT = 1e-6
CB = 32
P2_DVE = 1 + 12 * C + 3 * (C - 1)


def ttt_scan(nc, a, s, keep):
    with ExitStack() as ctx:
        m = Mem(nc, ctx, "p2")
        sb, sem = m.sb, m.sem
        hist = keep.hist
        zc = sb("zc", [B, 2, C, 2, D])
        mkb = sb("mkb", [B, 2, C, H, C])
        mkc = sb("mkc", [T, 2, CB, H * C])
        corr = sb("corr", [B, C, D])
        cev = sb("cev", [128, 1, CB // 4, D])
        gout = sb("gout", [B, C, D])
        tmp = corr
        gam = sb("gam", [B, D])
        prod = sb("prod", [B, 4, D])
        sums = sb("sums", [B, 4, H])
        mean = sb("mean", [B, H])
        varb = sb("varb", [B, H])
        coef = sb("coef", [B, 4, H])
        scs = sb("scs", [B, C, 2, H])
        xx = sb("xx", [B, 2, D])
        half = sb("half", [B, H])
        bk = m.banks()

        const_in, half_set, hist_zero, bank_zero = sem("const_in"), sem("half_set"), sem("hist_zero"), sem("bank_zero")
        zc_in = [sem(f"zc_in_{p}") for p in range(2)]
        mkc_in = [sem(f"mkc_in_{p}") for p in range(2)]
        caught, evac_a, evac_v = sem("caught"), sem("evac_a"), sem("evac_v")
        corr_in, corr_used = sem("corr_in"), sem("corr_used")
        sq_ready, rstd_ready, chunk_done, hist_in, chain = (
            sem("sq_ready"), sem("rstd_ready"), sem("chunk_done"), sem("hist_in"), sem("chain"))
        var_set, corr_out, g_out = sem("var_set"), sem("corr_out"), sem("g_out")
        setup_chain = sem("setup_chain")
        block = m.block()
        NQ = B // CB

        @block.sync
        def _(sp):
            sp.dma_start(gam[:, :], rows(a.L0_attn_ttt_g.rearrange("h e -> (h e)"), B)).then_inc(const_in, 16)

            def load_chunk(c, p, first):
                sp.dma_start(zc[:, p, :, :, :], s.zc[:, bass.ts(c, C), :].rearrange("b t (k d) -> b t k d", k=2)).then_inc(zc_in[p], 16)
                sp.dma_start(mkb[:, p, :, :, :].rearrange("b s h t -> b s (h t)"),
                             s.mk[:, bass.ts(c, C), bass.ds(c, 1), :, :].rearrange("b s o h t -> b s (o h t)")).then_inc(zc_in[p], 16)

            def load_grams(c, q, n):
                if q >= 2 or n is not None:
                    sp.wait_ge(caught, (q - 1) + (0 if n is None else n) + CREDIT)
                sp.dma_start(mkc[:, q % 2, :, :], s.mk[q * CB:(q + 1) * CB, :, bass.ds(c, 1), :, :].rearrange("b s o h t -> s b (o h t)")).then_inc(mkc_in[q % 2], 16)

            def spread(c, q, n):
                sp.wait_ge(evac_a, n + q + 1 + CREDIT)
                sp.wait_ge(evac_v, n + q + 1 + CREDIT)
                for r in range(4):
                    sp.dma_start(s.corr[q * CB + r:(q + 1) * CB:4, :, :].rearrange("b t d -> t b d"),
                                 cev[32 * r:32 * r + C, 0, :, :]).then_inc(corr_out, 16)
                if q == NQ - 1:
                    sp.wait_ge(corr_out, 64 * (n + q + 1) + CREDIT)
                    sp.dma_start(corr[:, :, :], s.corr).then_inc(corr_in, 16)

            def keep_gradients(c, n):
                sp.wait_ge(chunk_done, n + CREDIT)
                sp.dma_start(s.g[:, bass.ts(c, C), :], gout[:, :, :]).then_inc(g_out, 16)
                sp.wait_ge(g_out, 16 * n + CREDIT)
                sp.dma_start(hist[bass.ts(c, C), :, :], s.g[:, bass.ts(c, C), :].rearrange("b t d -> t b d")).then_inc(hist_in, 16)

            load_chunk(0, 0, True)
            load_chunk(1, 1, True)
            sp.wait_ge(hist_zero, 1 + CREDIT)
            keep_gradients(0, 1)
            for q in range(2):
                load_grams(1, q, None)
            def chunk(c, p, n, last):
                for q in range(NQ):
                    spread(c, q, n)
                    if q + 2 < NQ:
                        load_grams(c, q + 2, n)
                if not last:
                    load_chunk(c + 1, 1 - p, False)
                keep_gradients(c, c + 1)
                if not last:
                    for q in range(2):
                        load_grams(c + 1, q, n + NQ)

            for c in range(1, NC):
                chunk(c, c % 2, (c - 1) * NQ, c == NC - 1)
            sp.wait_ge(hist_in, 16 * NC + CREDIT)

        @block.gpsimd
        def _(pool):
            nc.gpsimd.memset(half[:, :], -0.5).then_inc(half_set, 1)
            pool.wait_ge(half_set, 1 + CREDIT)
            with pool.Fori(0, T) as t:
                pool.wait_ge(sq_ready, t + 1 + CREDIT)
                nc.gpsimd.tensor_tensor(coef[:, 2, :], varb[:, :], half[:, :], ALU.pow).then_inc(var_set, 1)
                pool.wait_ge(var_set, t + 1 + CREDIT)
                nc.gpsimd.tensor_tensor(coef[:, 3, :], coef[:, 2, :], coef[:, 2, :], ALU.mult).then_inc(rstd_ready, 1)

        def chunks(eng, body, first):
            first()
            with eng.Fori(0, (NC - 2) // 2) as i:
                body(2 * i + 1, 1, (2 * i) * NQ, i, 0)
                body(2 * i + 2, 0, (2 * i + 1) * NQ, i, 1)
            body(NC - 1, 1, (NC - 2) * NQ, (NC - 2) // 2, 0)

        @block.scalar
        def _(act):
            def body(c, p, n, i, k):
                for q in range(NQ):
                    act.wait_ge(caught, n + q + 1 + CREDIT)
                    if q == 0:
                        act.wait_ge(corr_out, 64 * n + CREDIT)
                    else:
                        act.wait_ge(corr_out, 64 * (n + q) + CREDIT)
                    o = q % 2 * 4
                    for x in range(2):
                        last = nc.scalar.activation(cev[:, 0, 2 * x:2 * x + 2, :], bk[o + x][:, 0:2 * D].rearrange("p (k d) -> p k d", k=2), ACT.Copy)
                    last.then_inc(evac_a, 1)
            chunks(act, body, lambda: None)

        @block.tensor
        def _(pe):
            pe.wait_ge(bank_zero, 1 + CREDIT)

            def body(c, p, n, i, k):
                pe.wait_ge(hist_in, 16 * c + CREDIT)
                for q in range(NQ):
                    pe.wait_ge(mkc_in[q % 2], 16 * (n // 2 + q // 2 + 1) + CREDIT if isinstance(n, int) else 16 * ((2 * i + k) * (NQ // 2) + q // 2 + 1) + CREDIT)
                    pe.wait_ge(evac_a, n + q - 1 + CREDIT if q >= 2 else n + CREDIT)
                    pe.wait_ge(evac_v, n + q - 1 + CREDIT if q >= 2 else n + CREDIT)
                    o = q % 2 * 4
                    for b in range(CB):
                        r, kk = b % 4, b // 4
                        for h in range(H):
                            col = kk % 2 * D + h * HD
                            last = nc.tensor.matmul(bk[o + kk // 2][32 * r:32 * r + C, col:col + HD],
                                                    mkc[:, q % 2, b, h * C:(h + 1) * C], hist[:, q * CB + b, h * HD:(h + 1) * HD],
                                                    start=True, stop=True)
                    last.then_inc(caught, 1)
            chunks(pe, body, lambda: None)

        @block.vector
        def _(dve):
            for b in range(8):
                last = nc.vector.memset(bk[b][:, :], 0.0)
            last.then_inc(bank_zero, 1)
            nc.vector.memset(hist[:, :, :], 0.0).then_inc(hist_zero, 1)
            dve.wait_ge(const_in, 16 + CREDIT)
            su = Chain(dve, setup_chain, 0, 1)
            su(nc.vector.tensor_tensor(gam[:, :], gam[:, :], gam[:, :], ALU.mult))

            def scan(c, p):
                ch = Chain(dve, chain, c, P2_DVE)
                ch(nc.vector.tensor_reduce(scs[:, :, 0, :], zc[:, p, :, 1, :].rearrange("b t (h e) -> b t h e", h=H), AX.X, ALU.add))
                for j in range(C):
                    z, cz = zc[:, p, j, 0, :], zc[:, p, j, :, :]
                    zh = z.rearrange("b (h e) -> b h e", h=H)
                    ch(nc.vector.tensor_reduce(mean[:, :], zh, AX.X, ALU.add))
                    ch(nc.vector.scalar_tensor_tensor(out=zh, in0=mean[:, :].unsqueeze(2).to_broadcast([B, H, HD]), scalar=-1.0 / HD, in1=zh,
                                                      op0=ALU.mult, op1=ALU.add))
                    ch(nc.vector.tensor_tensor(prod[:, 0:2, :], cz, z.unsqueeze(1).to_broadcast([B, 2, D]), ALU.mult))
                    ch(nc.vector.tensor_reduce(sums[:, 0:2, :], prod[:, 0:2, :].rearrange("b k (h e) -> b k h e", h=H), AX.X, ALU.add))
                    nc.vector.tensor_scalar(varb[:, :], sums[:, 0, :], 1.0 / HD, EPS_TTT, ALU.mult, ALU.add).then_inc(sq_ready, 1)
                    nc.vector.tensor_tensor(prod[:, 2, :], z, gam[:, :], ALU.mult)
                    ch(nc.vector.tensor_tensor(prod[:, 3, :], prod[:, 0, :], gam[:, :], ALU.mult))
                    ch(nc.vector.tensor_reduce(sums[:, 2:4, :], prod[:, 2:4, :].rearrange("b k (h e) -> b k h e", h=H), AX.X, ALU.add))
                    dve.wait_ge(rstd_ready, c * C + j + 1 + CREDIT)
                    nc.vector.tensor_tensor(scs[:, j, 1, :], sums[:, 1, :], coef[:, 2, :], ALU.mult)
                    ch(nc.vector.tensor_tensor(sums[:, 2:4, :], sums[:, 2:4, :], coef[:, 2:4, :], ALU.mult))
                    ch(nc.vector.tensor_tensor(sums[:, 2:4, :], sums[:, 2:4, :], scs[:, j, :, :], ALU.subtract))
                    ch(nc.vector.scalar_tensor_tensor(out=coef[:, 0:2, :], in0=sums[:, 2:4, :], scalar=1.0 / HD, in1=coef[:, 2:4, :], op0=ALU.mult, op1=ALU.mult))
                    g = gout[:, j, :]
                    wide = lambda v, n: v.unsqueeze(2).to_broadcast([B, n, HD])
                    he = lambda v: v.rearrange("b (h e) -> b h e", h=H)
                    nc.vector.tensor_tensor(xx[:, :, :].rearrange("b k (h e) -> b (k h) e", h=H), cz.rearrange("b k (h e) -> b (k h) e", h=H),
                                            wide(coef[:, 1:3, :].rearrange("b k h -> b (k h)"), 2 * H), ALU.mult)
                    ch(nc.vector.tensor_tensor(he(g), he(prod[:, 2, :]), wide(coef[:, 3, :], H), ALU.mult))
                    ch(nc.vector.tensor_tensor(g, g, xx[:, 0, :], ALU.subtract))
                    ch(nc.vector.tensor_tensor(g, g, xx[:, 1, :], ALU.subtract))
                    last = nc.vector.tensor_tensor(he(g), he(g), wide(coef[:, 0, :], H), ALU.subtract)
                    if j == C - 1:
                        last.then_inc(chunk_done, 1)
                        break
                    ch(last)
                    n = C - 1 - j
                    t4 = tmp[:, 0:n, :].rearrange("b t (h e) -> b t h e", h=H)
                    ch(nc.vector.tensor_tensor(
                        t4, mkb[:, p, j, :, j + 1:C].rearrange("b h t -> b t h").unsqueeze(3).to_broadcast([B, n, H, HD]),
                        he(g).unsqueeze(1).to_broadcast([B, n, H, HD]), ALU.mult))
                    ch(nc.vector.tensor_tensor(zc[:, p, j + 1:C, 0, :], zc[:, p, j + 1:C, 0, :], tmp[:, 0:n, :], ALU.subtract))
                ch.close()

            def body(c, p, n, i, k):
                for q in range(NQ):
                    dve.wait_ge(caught, n + q + 1 + CREDIT)
                    dve.wait_ge(corr_out, 64 * (n + q) + CREDIT)
                    o = q % 2 * 4
                    for x in range(2, 4):
                        last = nc.vector.tensor_copy(cev[:, 0, 2 * x:2 * x + 2, :], bk[o + x][:, 0:2 * D].rearrange("p (k d) -> p k d", k=2))
                    last.then_inc(evac_v, 1)
                dve.wait_ge(zc_in[p], 32 * (i + 1 if p == 1 else i + 2) + CREDIT)
                dve.wait_ge(corr_in, 16 * c + CREDIT)
                dve.wait_ge(hist_in, 16 * c + CREDIT)
                nc.vector.tensor_tensor(zc[:, p, :, 0, :], zc[:, p, :, 0, :], corr[:, :, :], ALU.subtract).then_inc(corr_used, 1)
                dve.wait_ge(corr_used, c + CREDIT)
                scan(c, p)

            chunks(dve, body, lambda: (dve.wait_ge(zc_in[0], 32 + CREDIT), scan(0, 0)))


class Norm:

    def __init__(self, nc, m, of_turn, n=GB, tag="bn"):
        self.nc, self.of_turn, self.batches = nc, of_turn, n
        self.st, self.mv = m.sb(f"{tag}_st", [128, n, 6]), m.sb(f"{tag}_mv", [128, n, 2])
        self.rs = m.sb(f"{tag}_rs", [128, n])
        self.half, self.junk = m.sb(f"{tag}_half", [128, 16]), m.sb(f"{tag}_junk", [128, 1])
        self.half_set, self.var_ready, self.rstd_ready = (
            m.sem(f"{tag}_half_set"), m.sem(f"{tag}_var_ready"), m.sem(f"{tag}_rstd_ready"))

    def pool_start(self, pool):
        self.nc.gpsimd.memset(self.half[:, :], -0.5).then_inc(self.half_set, 1)
        pool.wait_ge(self.half_set, 1 + CREDIT)

    def pool(self, pool, turn, k, var=None, out=None):
        var = self.mv[:, :, 1] if var is None else var
        out = self.rs[:, :] if out is None else out
        pool.wait_ge(self.var_ready, turn * self.of_turn + k + 1 + CREDIT)
        self.nc.gpsimd.tensor_tensor(out, var, self.half[:, 0:out.shape[-1]], ALU.pow).then_inc(self.rstd_ready, 1)

    def stats(self, src):
        for j in range(self.batches):
            last = self.nc.vector.bn_stats(self.st[:, j, :], src(j))
        return last

    def aggregate(self):
        self.nc.vector.memset(self.junk[:, :], 0.0)
        for j in range(self.batches):
            last = self.nc.vector.bn_aggr(self.mv[:, j, :], self.st[:, j, :])
        return last

    def variance(self, eps):
        self.nc.vector.tensor_scalar(self.mv[:, :, 1], self.mv[:, :, 1], eps, None, ALU.add).then_inc(self.var_ready, 1)

    def normalise(self, dve, turn, k, src, dst):
        dve.wait_ge(self.rstd_ready, turn * self.of_turn + k + 1 + CREDIT)
        for j in range(self.batches):
            last = self.nc.vector.tensor_scalar(dst(j), src(j), self.mv[:, j, 0:1], self.rs[:, j:j + 1], ALU.subtract, ALU.mult)
        return last

    def dve(self, dve, c, turn, k, src, dst, eps):
        c(self.stats(src))
        c(self.aggregate())
        self.variance(eps)
        return self.normalise(dve, turn, k, src, dst)


P3_LINKS = 9
NF = 3


def ttt_finish(nc, a, s, keep):
    with ExitStack() as ctx:
        m = Mem(nc, ctx, "p3")
        sb, sem = m.sb, m.sem
        ident, hist = keep.ident, keep.hist
        both = range(2)
        pair = lambda name, shape: [sb(f"{name}_{p}", shape) for p in both]
        sem_pair = lambda name: [sem(f"{name}_{p}") for p in both]
        mq, qz, h = pair("mq", [T, GB, H, T]), pair("qz", [T, GB, 2, D]), pair("h", [T, GB, D])
        zq, sq, qb = pair("zq", [T, GB, D]), pair("sq", [T, GB, D]), pair("qb", [T, GB, D])
        var12, rs12 = pair("var12", [T, GB * H]), pair("rs12", [T, GB * H])
        gam, bet = sb("gam", [T, D]), sb("bet", [T, D])
        wo0, wo1, wu0, wu1 = sb("wo0", [DL, D]), sb("wo1", [DH, D]), sb("wu0", [DL, D]), sb("wu1", [DH + 1, D])
        pg, pb = sb("pg", [DL, 2, 2]), sb("pb", [DL, 2, 2])
        yn = pair("yn", [T, GB, D])
        yt0, yt1 = pair("yt0", [DL, GB * T]), pair("yt1", [DH + 1, GB * T])
        xt0, xt1 = pair("xt0", [DL, GB * T]), pair("xt1", [DH, GB * T])
        bk = m.banks()
        rows_bk = [bk[0:2], bk[4:6]]
        cols_bk = [bk[2:4], bk[6:8]]
        nm = [Norm(nc, m, 4, GB, f"bn{p}") for p in both]
        weights_in, ones_set = sem("weights_in"), sem("ones_set")
        chain, mq_in, qz_in, h_in = sem_pair("chain"), sem_pair("mq_in"), sem_pair("qz_in"), sem_pair("h_in")
        zq_done, zq_read, sq_ready, qb_ready, zq_ready = (
            sem_pair("zq_done"), sem_pair("zq_read"), sem_pair("sq_ready"), sem_pair("qb_ready"), sem_pair("zq_ready"))
        rows_ready, rows_flipped, cols_ready = sem_pair("rows_ready"), sem_pair("rows_flipped"), sem_pair("cols_ready")
        proj_done, h_ready, h_stored, xt_stored = sem_pair("proj_done"), sem_pair("h_ready"), sem_pair("h_stored"), sem_pair("xt_stored")
        block = m.block()
        LAST = NG // 2 - 1
        halves = lambda v: v.rearrange("t (b d) -> t b d", b=2)

        @block.sync
        def _(sp):
            loads = [(gam[:, :], rows(a.L0_attn_ttt_g.rearrange("h e -> (h e)"), T)), (bet[:, :], rows(a.L0_attn_ttt_b.rearrange("h e -> (h e)"), T)),
                     (wo0[:, :], a.L0_attn_Wo[0:DL, :]), (wo1[:, :], a.L0_attn_Wo[DL:D, :]),
                     (wu0[:, :], a.L0_attn_W_up[0:DL, :]), (wu1[0:DH, :], a.L0_attn_W_up[DL:D, :]), (wu1[DH:DH + 1, :], a.L0_attn_b_up[None, :])]
            for k, (gn, bn) in enumerate(((a.L0_attn_post_g, a.L0_attn_post_b), (a.L0_attn_norm_g, a.L0_attn_norm_b))):
                for dst, src in ((pg, gn), (pb, bn)):
                    loads += [(dst[:, k, 0:1], src[0:DL, None]), (dst[0:DH, k, 1:2], src[DL:D, None])]
            assert len(loads) == 15
            for dst, src in loads:
                sp.dma_start(dst, src).then_inc(weights_in, 16)

            def load_mq(g, p):
                sp.dma_start(mq[p][:, :, :, :].rearrange("s b h t -> s b (h t)"), s.mq[bass.ts(g, GB), :, :, :].rearrange("b s h t -> s b (h t)")).then_inc(mq_in[p], 16)

            def load_qz(g, p):
                sp.dma_start(qz[p][:, :, :, :].rearrange("t b k d -> t b (k d)"), s.qz[bass.ts(g, GB), :, :].rearrange("b t d -> t b d")).then_inc(qz_in[p], 16)

            def turn(i, last=False):
                for p in both:
                    sp.wait_ge(rows_ready[p], i * NF + CREDIT)
                    sp.wait_ge(h_stored[p], i * 16 + CREDIT)
                    sp.dma_start(h[p][:, :, :], s.h[bass.ts(i * 2 + p, GB), :, :].rearrange("b t d -> t b d")).then_inc(h_in[p], 16)
                if not last:
                    for p in both:
                        sp.wait_ge(zq_done[p], i + 1 + CREDIT)
                        load_mq(i * 2 + 2 + p, p)
                    for p in both:
                        sp.wait_ge(zq_read[p], i + 1 + CREDIT)
                        sp.wait_ge(qb_ready[p], i + 1 + CREDIT)
                        load_qz(i * 2 + 2 + p, p)
                for p in both:
                    sp.wait_ge(h_ready[p], i + 1 + CREDIT)
                    sp.dma_start(s.h[bass.ts(i * 2 + p, GB), :, :].rearrange("b t d -> t b d"), h[p][:, :, :]).then_inc(h_stored[p], 16)
                for p in both:
                    sp.wait_ge(cols_ready[p], i * NF + NF + CREDIT)
                    sp.dma_start(s.xt[bass.ds(i * 2 + p, 1), 0:DL, :].rearrange("o p n -> (o p) n"), xt0[p][:, :]).then_inc(xt_stored[p], 16)
                    sp.dma_start(s.xt[bass.ds(i * 2 + p, 1), DL:D, :].rearrange("o p n -> (o p) n"), xt1[p][:, :]).then_inc(xt_stored[p], 16)

            for p in both:
                load_mq(p, p)
                load_qz(p, p)
            with sp.Fori(0, LAST) as i:
                turn(i)
            turn(LAST, last=True)
            for p in both:
                sp.wait_ge(h_stored[p], 16 * (NG // 2) + CREDIT)
                sp.wait_ge(xt_stored[p], 32 * (NG // 2) + CREDIT)

        @block.gpsimd
        def _(pool):
            for p in both:
                nm[p].pool_start(pool)
            pool.wait_ge(weights_in, 16 * 15 + CREDIT)
            with pool.Fori(0, NG // 2) as i:
                for p in both:
                    pool.wait_ge(qz_in[p], i * 16 + 16 + CREDIT)
                    pool.wait_ge(zq_ready[p], i + CREDIT)
                    nc.gpsimd.tensor_tensor(qb[p][:, :, :], qz[p][:, :, 0, :], bet[:, :].unsqueeze(1).to_broadcast([T, GB, D]), ALU.add).then_inc(qb_ready[p], 1)
                for p in both:
                    nm[p].pool(pool, i, 0, var12[p][:, :], rs12[p][:, :])
                for k in range(1, 4):
                    for p in both:
                        nm[p].pool(pool, i, k)

        @block.scalar
        def _(act):
            act.wait_ge(weights_in, 16 * 15 + CREDIT)
            with act.Fori(0, NG // 2) as i:
                for p in both:
                    act.wait_ge(zq_read[p], i + 1 + CREDIT)
                    nc.scalar.activation(sq[p][:, :, :], zq[p][:, :, :], ACT.Square).then_inc(sq_ready[p], 1)
                for f in range(NF):
                    for p in both:
                        act.wait_ge(rows_flipped[p], i * NF + f + 1 + CREDIT)
                        top, low = cols_bk[p]
                        if f < 2:
                            nc.scalar.activation(yt0[p][:, :], top[:, :], ACT.Identity, scale=pg[:, f, 0:1], bias=pb[:, f, 0:1])
                            nc.scalar.activation(yt1[p][0:DH, :], low[0:DH, :], ACT.Identity, scale=pg[0:DH, f, 1:2], bias=pb[0:DH, f, 1:2]).then_inc(cols_ready[p], 1)
                        else:
                            act.wait_ge(xt_stored[p], i * 32 + CREDIT)
                            nc.scalar.activation(xt0[p][:, :], top[:, :], ACT.Copy)
                            nc.scalar.activation(xt1[p][:, :], low[0:DH, :], ACT.Copy).then_inc(cols_ready[p], 1)

        @block.vector
        def _(dve):
            for p in both:
                last = nc.vector.memset(yt1[p][DH:DH + 1, :], 1.0)
            last.then_inc(ones_set, 1)
            dve.wait_ge(weights_in, 16 * 15 + CREDIT)
            with dve.Fori(0, NG // 2) as i:
                links = [0, 0]

                def link(p, ins):
                    links[p] += 1
                    ins.then_inc(chain[p], 1)

                def linked(p):
                    dve.wait_ge(chain[p], i * P3_LINKS + links[p] + CREDIT)

                def norm(k, src, eps):
                    for p in both:
                        link(p, nm[p].stats(lambda j: src(p, j)))
                    for p in both:
                        linked(p)
                        link(p, nm[p].aggregate())
                    for p in both:
                        linked(p)
                        nm[p].variance(eps)
                    for p in both:
                        nm[p].normalise(dve, i, k, lambda j: src(p, j), lambda j: yn[p][:, j, :]).then_inc(rows_ready[p], 1)

                for p in both:
                    dve.wait_ge(qz_in[p], i * 16 + 16 + CREDIT)
                    dve.wait_ge(zq_done[p], i + 1 + CREDIT)
                    for x in range(2):
                        last = nc.vector.tensor_tensor(zq[p][:, 2 * x:2 * x + 2, :], qz[p][:, 2 * x:2 * x + 2, 1, :], halves(rows_bk[p][x][:, 0:2 * D]), ALU.subtract)
                    last.then_inc(zq_read[p], 1)
                heads = lambda v: v[:, :, :].rearrange("t b (h e) -> t (b h) e", h=H)
                for p in both:
                    dve.wait_ge(sq_ready[p], i + 1 + CREDIT)
                    link(p, nc.vector.tensor_reduce(var12[p][:, :], heads(sq[p]), AX.X, ALU.add))
                for p in both:
                    linked(p)
                    nc.vector.tensor_scalar(var12[p][:, :], var12[p][:, :], 1.0 / HD, EPS_TTT, ALU.mult, ALU.add).then_inc(nm[p].var_ready, 1)
                for p in both:
                    dve.wait_ge(nm[p].rstd_ready, i * 4 + 1 + CREDIT)
                    link(p, nc.vector.tensor_tensor(heads(zq[p]), heads(zq[p]), rs12[p][:, :].unsqueeze(2).to_broadcast([T, GB * H, HD]), ALU.mult))
                for p in both:
                    linked(p)
                    link(p, nc.vector.tensor_tensor(zq[p][:, :, :], zq[p][:, :, :], gam[:, :].unsqueeze(1).to_broadcast([T, GB, D]), ALU.mult))
                for p in both:
                    linked(p)
                    dve.wait_ge(qb_ready[p], i + 1 + CREDIT)
                    nc.vector.tensor_tensor(zq[p][:, :, :], zq[p][:, :, :], qb[p][:, :, :], ALU.add).then_inc(zq_ready[p], 1)
                for p in both:
                    dve.wait_ge(zq_ready[p], i + 1 + CREDIT)
                    dve.wait_ge(rows_flipped[p], i * NF + CREDIT)
                norm(1, lambda p, j: zq[p][:, j, :], 1e-6)
                for p in both:
                    dve.wait_ge(proj_done[p], i * 2 + 1 + CREDIT)
                norm(2, lambda p, j: rows_bk[p][j // 2][:, j % 2 * D:(j % 2 + 1) * D], 1e-6)
                for p in both:
                    dve.wait_ge(proj_done[p], i * 2 + 2 + CREDIT)
                    dve.wait_ge(h_in[p], i * 16 + 16 + CREDIT)
                    for x in range(2):
                        last = nc.vector.tensor_tensor(h[p][:, 2 * x:2 * x + 2, :], h[p][:, 2 * x:2 * x + 2, :], halves(rows_bk[p][x][:, 0:2 * D]), ALU.add)
                    last.then_inc(h_ready[p], 1)
                for p in both:
                    dve.wait_ge(h_ready[p], i + 1 + CREDIT)
                norm(3, lambda p, j: h[p][:, j, :], 1e-5)
                assert links == [P3_LINKS] * 2, links

        @block.tensor
        def _(pe):
            pe.wait_ge(weights_in, 16 * 15 + CREDIT)
            pe.wait_ge(ones_set, 1 + CREDIT)

            def zq_products(i, p):
                pe.wait_ge(mq_in[p], i * 16 + 16 + CREDIT)
                pe.wait_ge(h_ready[p], i + CREDIT)
                for j in range(GB):
                    for h_ in range(H):
                        col = j % 2 * D + h_ * HD
                        last = nc.tensor.matmul(rows_bk[p][j // 2][:, col:col + HD], mq[p][:, j, h_, :],
                                                hist[:, bass.ds((i * 2 + p) * GB + j, 1), h_ * HD:(h_ + 1) * HD].rearrange("s o e -> s (o e)"), start=True, stop=True)
                last.then_inc(zq_done[p], 1)

            def flip(i, p, f):
                pe.wait_ge(rows_ready[p], i * NF + f + 1 + CREDIT)
                pe.wait_ge(cols_ready[p], i * NF + f + CREDIT)
                top, low = cols_bk[p]
                for j in range(GB):
                    nc.tensor.transpose(top[:, j * T:(j + 1) * T], yn[p][:, j, 0:DL], ident[:, :])
                for j in range(GB):
                    last = nc.tensor.transpose(low[0:DH, j * T:(j + 1) * T], yn[p][:, j, DL:D], ident[:, :])
                last.then_inc(rows_flipped[p], 1)

            def project(i, p, f, w0, w1, n1):
                pe.wait_ge(cols_ready[p], i * NF + f + 1 + CREDIT)
                for j in range(GB):
                    out = rows_bk[p][j // 2][:, j % 2 * D:(j % 2 + 1) * D]
                    nc.tensor.matmul(out, yt0[p][:, j * T:(j + 1) * T], w0[:, :], start=True, stop=False)
                    last = nc.tensor.matmul(out, yt1[p][0:n1, j * T:(j + 1) * T], w1[:, :], start=False, stop=True)
                last.then_inc(proj_done[p], 1)

            def turn(i, last=False):
                for f, w in enumerate(((wo0, wo1, DH), (wu0, wu1, DH + 1))):
                    for p in both:
                        flip(i, p, f)
                    for p in both:
                        project(i, p, f, *w)
                if not last:
                    for p in both:
                        zq_products(i + 1, p)
                for p in both:
                    flip(i, p, 2)

            for p in both:
                zq_products(0, p)
            with pe.Fori(0, LAST) as i:
                turn(i)
            turn(LAST, last=True)


NE, HE, HS = 8, 192, 768
HALL = NE * HE + HS
EXP_COLS = HALL
NHT = HALL // 128
NX = NE + 1
P4_DVE = 15


def moe(nc, a, s, keep):
    with ExitStack() as ctx:
        m = Mem(nc, ctx, "p4")
        sb, sem = m.sb, m.sem
        ident = keep.ident
        wg0, wu0, wgu1 = sb("wg0", [DL, HALL]), sb("wu0", [DL, HALL]), sb("wgu1", [2 * DH, HALL])
        wg1, wu1 = wgu1[0:DH, :], wgu1[DH:2 * DH, :]
        wdn = sb("wdn", [128, NHT, D])
        wr0, wr1, rb = sb("wr0", [DL, NX]), sb("wr1", [DH, NX]), sb("rb", [T, NX])
        exf, ex = sb("exf", [32, HALL]), sb("ex", [32, HALL], BF16)
        iota = sb("iota", [T, NE])
        xt0, xt1 = sb("xt0", [DL, 2, GB * T]), sb("xt1", [2 * DH, 2, GB * T])
        h = sb("h", [T, 2, GB, D])
        lg, top, topi, topf = sb("lg", [T, GB, NX]), sb("top", [T, GB, 8]), sb("topi", [T, GB, 8], U32), sb("topf", [T, GB, 2])
        th, gates = sb("th", [T, 2, GB]), sb("gates", [T, 4, GB])
        dense, pick = sb("dense", [T, GB, NX]), sb("pick", [T, GB, NE])
        part, parts = sb("part", [T, GB, NX], BF16), sb("parts", [T, GB, 32])
        gt = sb("gt", [32, GB * T], BF16)
        sil, up, hid = sb("sil", [128, 2, GB * T]), sb("up", [128, 2, GB * T]), sb("hid", [128, 2, GB * T])
        bk = m.banks()

        weights_in, setup, chain = sem("weights_in"), sem("setup"), sem("chain")
        xt_in, h_in = [sem(f"xt_in_{p}") for p in range(2)], [sem(f"h_in_{p}") for p in range(2)]
        h_stored = [sem(f"h_stored_{p}") for p in range(2)]
        logits_done, tanh_in, tanh_out, parts_ready, parts_flipped, gates_ready = (
            sem("logits_done"), sem("tanh_in"), sem("tanh_out"), sem("parts_ready"), sem("parts_flipped"), sem("gates_ready"))
        gu_done, sil_ready, up_ready, spread_done, hid_ready, down_done, h_ready = (
            sem("gu_done"), sem("sil_ready"), sem("up_ready"), sem("spread_done"), sem("hid_ready"), sem("down_done"), sem("h_ready"))
        block = m.block()

        @block.sync
        def _(sp):
            loads = [(iota[:, :], a.c_iota), (exf[:, :], a.c_expand), (rb[:, NE:NX], rows(a.L0_ffn_sg_b, T))]
            for lo, hi, wg, wu, wr in ((0, DL, wg0, wu0, wr0), (DL, D, wg1, wu1, wr1)):
                loads += [(wr[:, 0:NE], a.L0_ffn_router_w[lo:hi, :]), (wr[:, NE:NX], a.L0_ffn_sg_w[lo:hi, :])]
                for w, routed, shared in ((wg, a.L0_ffn_w_gate, a.L0_ffn_ws_gate), (wu, a.L0_ffn_w_up, a.L0_ffn_ws_up)):
                    loads += [(w[:, 0:NE * HE].rearrange("d (e h) -> d e h", e=NE), routed[:, lo:hi, :].rearrange("e d h -> d e h")),
                              (w[:, NE * HE:HALL], shared[lo:hi, :])]
            loads += [(wdn[:, 0:NE * HE // 128, :], a.L0_ffn_w_down.rearrange("e h d -> (e h) d").rearrange("(k p) d -> p k d", p=128)),
                      (wdn[:, NE * HE // 128:NHT, :], a.L0_ffn_ws_down.rearrange("(k p) d -> p k d", p=128))]
            assert len(loads) == 17
            for dst, src in loads:
                sp.dma_start(dst, src).then_inc(weights_in, 16)

            def load(g, p):
                sp.dma_start(xt0[:, p, :], s.xt[bass.ds(g, 1), 0:DL, :].rearrange("o p n -> (o p) n")).then_inc(xt_in[p], 16)
                for lo in (0, DH):
                    sp.dma_start(xt1[lo:lo + DH, p, :], s.xt[bass.ds(g, 1), DL:D, :].rearrange("o p n -> (o p) n")).then_inc(xt_in[p], 16)
                sp.dma_start(h[:, p, :, :], s.h[bass.ts(g, GB), :, :].rearrange("b t d -> t b d")).then_inc(h_in[p], 16)

            def store(g, n, p, i):
                sp.wait_ge(h_ready, n + CREDIT)
                sp.dma_start(s.h[bass.ts(g, GB), :, :].rearrange("b t d -> t b d"), h[:, p, :, :]).then_inc(h_stored[p], 16)

            load(0, 0)
            load(1, 1)
            with sp.Fori(0, NG // 2 - 1) as i:
                for p in range(2):
                    g = 2 * i + p
                    store(g, g + 1, p, i)
                    sp.wait_ge(h_stored[p], 16 * (i + 1) + CREDIT)
                    load(g + 2, p)
            for p in range(2):
                store(NG - 2 + p, NG - 1 + p, p, NG // 2 - 1)
            for p in range(2):
                sp.wait_ge(h_stored[p], 16 * (NG // 2) + CREDIT)

        @block.scalar
        def _(act):
            with act.Fori(0, NG) as g:
                act.wait_ge(tanh_in, g + 1 + CREDIT)
                nc.scalar.activation(th[:, :, :], th[:, :, :], ACT.Tanh, scale=0.5).then_inc(tanh_out, 1)
                for k in range(NHT):
                    act.wait_ge(gu_done, NHT * g + k + 1 + CREDIT)
                    act.wait_ge(up_ready, NHT * g + max(k - 1, 0) + CREDIT)
                    nc.scalar.activation(sil[:, k % 2, :], bk[k % 2][:, :], ACT.Silu).then_inc(sil_ready, 1)

        @block.vector
        def _(dve):
            nc.vector.memset(rb[:, 0:NE], 0.0)
            nc.vector.memset(parts[:, :, :], 0.0)
            dve.wait_ge(weights_in, 16 * 17 + CREDIT)
            nc.vector.tensor_copy(ex[:, :], exf[:, :]).then_inc(setup, 1)
            dve.wait_ge(setup, 1 + CREDIT)

            def group(g, p, i):
                c = Chain(dve, chain, g, P4_DVE)
                dve.wait_ge(logits_done, g + 1 + CREDIT)
                c(nc.vector.tensor_tensor(lg[:, :, :], bk[7][:, 0:GB * 16].rearrange("t (b e) -> t b e", b=GB)[:, :, 0:NX],
                                          rb[:, :].unsqueeze(1).to_broadcast([T, GB, NX]), ALU.add))
                nc.vector.tensor_copy(th[:, 0, :], lg[:, :, NE])
                for j in range(GB):
                    last = nc.vector.max(top[:, j, :], lg[:, j, 0:NE])
                c(last)
                nc.vector.tensor_tensor(th[:, 1, :], top[:, :, 1], top[:, :, 0], ALU.subtract).then_inc(tanh_in, 1)
                for j in range(GB):
                    last = nc.vector.max_index(topi[:, j, :], top[:, j, :], lg[:, j, 0:NE])
                c(last)
                c(nc.vector.tensor_copy(topf[:, :, :], topi[:, :, 0:2]))
                dve.wait_ge(tanh_out, g + 1 + CREDIT)
                nc.vector.tensor_scalar(gates[:, 0, :], th[:, 0, :], -0.5, 0.5, ALU.mult, ALU.add)
                nc.vector.tensor_scalar(gates[:, 1, :], th[:, 0, :], 0.5, 0.5, ALU.mult, ALU.add)
                nc.vector.tensor_scalar(gates[:, 2, :], th[:, 1, :], -0.5, 0.5, ALU.mult, ALU.add)
                c(nc.vector.tensor_scalar(gates[:, 3, :], th[:, 1, :], 0.5, 0.5, ALU.mult, ALU.add))
                c(nc.vector.tensor_tensor(gates[:, 2:4, :], gates[:, 2:4, :], gates[:, 0, :].unsqueeze(1).to_broadcast([T, 2, GB]), ALU.mult))
                each = lambda v: v.unsqueeze(2).to_broadcast([T, GB, NE])
                ids = iota[:, :].unsqueeze(1).to_broadcast([T, GB, NE])
                nc.vector.tensor_tensor(dense[:, :, 0:NE], ids, each(topf[:, :, 0]), ALU.is_equal)
                nc.vector.tensor_copy(dense[:, :, NE], gates[:, 1, :])
                c(nc.vector.tensor_tensor(pick[:, :, :], ids, each(topf[:, :, 1]), ALU.is_equal))
                nc.vector.tensor_tensor(dense[:, :, 0:NE], dense[:, :, 0:NE], each(gates[:, 2, :]), ALU.mult)
                c(nc.vector.tensor_tensor(pick[:, :, :], pick[:, :, :], each(gates[:, 3, :]), ALU.mult))
                c(nc.vector.tensor_tensor(dense[:, :, 0:NE], dense[:, :, 0:NE], pick[:, :, :], ALU.add))
                for k in range(2):
                    c(nc.vector.tensor_copy(part[:, :, :], dense[:, :, :]))
                    c(nc.vector.tensor_copy(parts[:, :, k * NX:(k + 1) * NX], part[:, :, :]))
                    c(nc.vector.tensor_tensor(dense[:, :, :], dense[:, :, :], parts[:, :, k * NX:(k + 1) * NX], ALU.subtract))
                nc.vector.tensor_copy(parts[:, :, 2 * NX:3 * NX], dense[:, :, :]).then_inc(parts_ready, 1)
                dve.wait_ge(parts_flipped, g + 1 + CREDIT)
                nc.vector.tensor_copy(gt[:, :], bk[7][0:32, :]).then_inc(gates_ready, 1)

                def scale_up(k):
                    dve.wait_ge(sil_ready, NHT * g + k + 1 + CREDIT)
                    dve.wait_ge(spread_done, NHT * g + max(k - 1, 0) + CREDIT)
                    nc.vector.tensor_tensor(up[:, k % 2, :], sil[:, k % 2, :], bk[2 + k % 2][:, :], ALU.mult).then_inc(up_ready, 1)

                def gate(k):
                    dve.wait_ge(up_ready, NHT * g + k + 1 + CREDIT)
                    dve.wait_ge(spread_done, NHT * g + k + 1 + CREDIT)
                    dve.wait_ge(down_done, NHT * g + max(k - 1, 0) + CREDIT)
                    nc.vector.tensor_tensor(hid[:, k % 2, :], up[:, k % 2, :], bk[4 if k % 2 == 0 else 7][:, :], ALU.mult).then_inc(hid_ready, 1)

                for k in range(NHT):
                    scale_up(k)
                    gate(k)
                dve.wait_ge(down_done, NHT * (g + 1) + CREDIT)
                dve.wait_ge(h_in[p], 16 * (i + 1) + CREDIT)
                for x in range(2):
                    last = nc.vector.tensor_tensor(h[:, p, 2 * x:2 * x + 2, :], h[:, p, 2 * x:2 * x + 2, :],
                                                   bk[5 + x][:, 0:2 * D].rearrange("t (b d) -> t b d", b=2), ALU.add)
                last.then_inc(h_ready, 1)
                c.close()

            with dve.Fori(0, NG // 2) as i:
                for p in range(2):
                    group(2 * i + p, p, i)

        @block.tensor
        def _(pe):
            pe.wait_ge(weights_in, 16 * 17 + CREDIT)
            pe.wait_ge(setup, 1 + CREDIT)

            def group(g, p, i):
                pe.wait_ge(xt_in[p], 48 * (i + 1) + CREDIT)
                pe.wait_ge(hid_ready, NHT * g + CREDIT)
                for j in range(GB):
                    out = bk[7][:, 16 * j:16 * j + NX]
                    nc.tensor.matmul(out, xt0[:, p, j * T:(j + 1) * T], wr0[:, :], start=True, stop=False)
                    last = nc.tensor.matmul(out, xt1[0:DH, p, j * T:(j + 1) * T], wr1[:, :], start=False, stop=True)
                last.then_inc(logits_done, 1)

                def gate_up(k):
                    pe.wait_ge(up_ready, NHT * g + max(k - 1, 0) + CREDIT)
                    for bank, w0 in ((bk[k % 2], wg0), (bk[2 + k % 2], wu0)):
                        nc.tensor.matmul(bank[:, :], w0[:, 128 * k:128 * (k + 1)], xt0[:, p, :], start=True, stop=False)
                    for bank, lo in ((bk[k % 2], 0), (bk[2 + k % 2], DH)):
                        last = nc.tensor.matmul(bank[:, :], wgu1[lo:lo + DH, 128 * k:128 * (k + 1)], xt1[lo:lo + DH, p, :], start=False, stop=True)
                    last.then_inc(gu_done, 1)

                def spread(k):
                    pe.wait_ge(hid_ready, NHT * g + max(k - 1, 0) + CREDIT)
                    nc.tensor.matmul(bk[4 if k % 2 == 0 else 7][:, :], ex[:, 128 * k:128 * (k + 1)], gt[:, :], start=True, stop=True).then_inc(spread_done, 1)

                def down(k):
                    pe.wait_ge(hid_ready, NHT * g + k + 1 + CREDIT)
                    for j in range(GB):
                        last = nc.tensor.matmul(bk[5 + j // 2][:, j % 2 * D:(j % 2 + 1) * D], hid[:, k % 2, j * T:(j + 1) * T], wdn[:, k, :],
                                                start=(k == 0 and j % 2 == 0), stop=(k == NHT - 1), skip_group_check=True)
                    last.then_inc(down_done, 1)

                gate_up(0)
                gate_up(1)
                pe.wait_ge(parts_ready, g + 1 + CREDIT)
                for j in range(GB):
                    last = nc.tensor.transpose(bk[7][0:32, j * T:(j + 1) * T], parts[:, j, :], ident[:, :])
                last.then_inc(parts_flipped, 1)
                pe.wait_ge(gates_ready, g + 1 + CREDIT)
                spread(0)
                spread(1)
                pe.wait_ge(h_ready, g + CREDIT)
                for k in range(NHT):
                    if k + 2 < NHT:
                        gate_up(k + 2)
                    down(k)
                    if k + 2 < NHT:
                        spread(k + 2)

            with pe.Fori(0, NG // 2) as i:
                for p in range(2):
                    group(2 * i + p, p, i)


DI, DS, NH, HP, DCONV = 2 * D, 128, 6, 64, 4
CD = DI + 2 * DS
NP = DI + CD + NH
NCT = CD // 128
NPT = -(-NP // 128)
A_LEAST = -110.0
WB = 2 * GB
NW = B // WB
WH = WB * T // 512
NORM_LINKS = 2


class Turn:

    def __init__(self, i, r):
        self.i, self.r, self.t = i, r, i * 2 + r
        self.p, self.earlier = r % 2, i + r // 2
        self.last = isinstance(self.t, int) and self.t == NW - 1

    def next(self):
        return Turn(self.i, self.r + 1)


def turns(eng, do):
    with eng.Fori(0, NW // 2 - 1) as i:
        for r in range(2):
            do(Turn(i, r))
    for r in range(2):
        do(Turn(NW // 2 - 1, r))


def mamba_steps(nc, a, s, keep):
    with ExitStack() as ctx:
        m = Mem(nc, ctx, "p5")
        sb, sem = m.sb, m.sem
        ident = keep.ident
        wi0, wi1, wo, dt, da = keep.wi0, keep.wi1, keep.wo, keep.dt, keep.da
        wrow = sb("wrow", [128, NPT, D])
        orow0, orow1 = sb("orow0", [DL, DI]), sb("orow1", [DH, DI])
        dtb, al = sb("dtb", [T, NH]), sb("al", [T, NH])
        h, xn = sb("h", [T, 2, WB, D]), sb("xn", [T, WB, D])
        xt0, xt1 = sb("xt0", [DL, 2, WB * T]), sb("xt1", [DH, 2, WB * T])
        pos, neg = sb("pos", [T, B, NH]), sb("neg", [T, B, NH])
        bk = m.banks()
        nm = Norm(nc, m, 1, WB)
        weights_in, w_flipped, w_copied = sem("weights_in"), sem("w_flipped"), sem("w_copied")
        h_in, xt_stored = ([sem(f"{n}_{p}") for p in range(2)] for n in ("h_in", "xt_stored"))
        rows_ready, rows_flipped, cols_a, cols_v = sem("rows_ready"), sem("rows_flipped"), sem("cols_a"), sem("cols_v")
        dt_done, dt_copied, chain = sem("dt_done"), sem("dt_copied"), sem("chain")
        soft, soft_act, exp_a = sem("soft"), sem("soft_act"), sem("exp_a")
        block = m.block()

        @block.sync
        def _(sp):
            full = NPT - 1
            loads = [(wrow[:, 0:full, :], a.L1_attn_in_proj_w[0:128 * full, :].rearrange("(k p) d -> p k d", p=128)),
                     (wrow[0:NP - 128 * full, full, :], a.L1_attn_in_proj_w[128 * full:NP, :]),
                     (orow0[:, :], a.L1_attn_out_proj_w[0:DL, :]), (orow1[:, :], a.L1_attn_out_proj_w[DL:D, :]),
                     (dtb[:, :], rows(a.L1_attn_dt_bias, T)), (al[:, :], rows(a.L1_attn_A_log, T))]
            assert len(loads) == 6
            for dst, src in loads:
                sp.dma_start(dst, src).then_inc(weights_in, 16)

            def load(t, p):
                sp.dma_start(h[:, p, :, :], s.h[bass.ts(t, WB), :, :].rearrange("b t d -> t b d")).then_inc(h_in[p], 16)

            def store(w):
                sp.wait_ge(cols_a, w.t + 1 + CREDIT)
                sp.wait_ge(cols_v, w.t + 1 + CREDIT)
                for lo, hi, xt in ((0, DL, xt0), (DL, D, xt1)):
                    sp.dma_start(s.xt[bass.ts(w.t, WB // GB), lo:hi, :].rearrange("g p n -> p g n"),
                                 xt[:, w.p, :].rearrange("p (g n) -> p g n", n=GB * T)).then_inc(xt_stored[w.p], 16)

            load(0, 0)
            load(1, 1)
            with sp.Fori(0, NW // 2 - 1) as i:
                for r in range(2):
                    sp.wait_ge(rows_ready, i * 2 + r + 1 + CREDIT)
                    load(i * 2 + r + 2, r)
                    store(Turn(i, r))
            for r in range(2):
                store(Turn(NW // 2 - 1, r))
            for p in range(2):
                sp.wait_ge(xt_stored[p], 32 * (NW // 2) + CREDIT)

        @block.gpsimd
        def _(pool):
            nm.pool_start(pool)
            with pool.Fori(0, NW) as g:
                nm.pool(pool, g, 0)

        @block.scalar
        def _(act):
            def columns(w):
                act.wait_ge(rows_flipped, w.t + 1 + CREDIT)
                act.wait_ge(xt_stored[w.p], w.earlier * 32 + CREDIT)
                act.wait_ge(dt_done, w.t + CREDIT)
                for x in range(WH):
                    last = nc.scalar.activation(xt1[:, w.p, x * 512:(x + 1) * 512], bk[2 + x][0:DH, :], ACT.Copy)
                last.then_inc(cols_a, 1)

            turns(act, columns)
            act.wait_ge(soft, 2 + CREDIT)
            nc.scalar.activation(neg[:, :, :], neg[:, :, :], ACT.Exp).then_inc(soft_act, 1)
            act.wait_ge(soft_act, 1 + CREDIT)
            nc.scalar.activation(neg[:, :, :], neg[:, :, :], ACT.Ln, bias=1.0).then_inc(soft_act, 1)
            act.wait_ge(weights_in, 16 * 6 + CREDIT)
            nc.scalar.activation(al[:, :], al[:, :], ACT.Exp).then_inc(exp_a, 1)

        @block.vector
        def _(dve):
            for k in range(NPT):
                n = min(128, NP - 128 * k)
                dve.wait_ge(w_flipped, k + 1 + CREDIT)
                nc.vector.tensor_copy(wi0[:, 128 * k:128 * k + n], bk[2 * (k % 2)][:, 0:n])
                nc.vector.tensor_copy(wi1[:, 128 * k:128 * k + n], bk[2 * (k % 2) + 1][0:DH, 0:n]).then_inc(w_copied, 1)
            for k in range(DI // 128):
                dve.wait_ge(w_flipped, NPT + k + 1 + CREDIT)
                nc.vector.tensor_copy(wo[:, k, :], bk[4 + k][:, 0:D]).then_inc(w_copied, 1)
            dve.wait_ge(weights_in, 16 * 6 + CREDIT)

            def norm(w):
                c = Chain(dve, chain, w.t, NORM_LINKS)
                dve.wait_ge(h_in[w.p], w.earlier * 16 + 16 + CREDIT)
                dve.wait_ge(rows_flipped, w.t + CREDIT)
                nm.dve(dve, c, w.t, 0, lambda j: h[:, w.p, j, :], lambda j: xn[:, j, :], 1e-5).then_inc(rows_ready, 1)
                c.close()

            def turn(w):
                dve.wait_ge(rows_flipped, w.t + 1 + CREDIT)
                dve.wait_ge(xt_stored[w.p], w.earlier * 32 + CREDIT)
                dve.wait_ge(dt_done, w.t + CREDIT)
                for x in range(WH):
                    last = nc.vector.tensor_copy(xt0[:, w.p, x * 512:(x + 1) * 512], bk[x][:, :])
                last.then_inc(cols_v, 1)
                if not w.last:
                    norm(w.next())
                dve.wait_ge(dt_done, w.t + 1 + CREDIT)
                nc.vector.tensor_tensor(dt[:, bass.ts(w.t, WB), :], bk[4][:, 0:WB * NH].rearrange("t (b h) -> t b h", b=WB),
                                        dtb[:, :].unsqueeze(1).to_broadcast([T, WB, NH]), ALU.add).then_inc(dt_copied, 1)

            norm(Turn(0, 0))
            turns(dve, turn)
            dve.wait_ge(dt_copied, NW + CREDIT)
            nc.vector.tensor_scalar(pos[:, :, :], dt[:, :, :], 0.0, None, ALU.max).then_inc(soft, 1)
            dve.wait_ge(soft, 1 + CREDIT)
            nc.vector.scalar_tensor_tensor(out=neg[:, :, :], in0=pos[:, :, :], scalar=-2.0, in1=dt[:, :, :], op0=ALU.mult, op1=ALU.add).then_inc(soft, 1)
            dve.wait_ge(soft_act, 2 + CREDIT)
            nc.vector.tensor_tensor(dt[:, :, :], pos[:, :, :], neg[:, :, :], ALU.add).then_inc(soft, 1)
            dve.wait_ge(soft, 3 + CREDIT)
            dve.wait_ge(exp_a, 1 + CREDIT)
            nc.vector.scalar_tensor_tensor(out=da[:, :, :], in0=al[:, :].unsqueeze(1).to_broadcast([T, B, NH]), scalar=-1.0, in1=dt[:, :, :],
                                           op0=ALU.mult, op1=ALU.mult).then_inc(soft, 1)
            dve.wait_ge(soft, 4 + CREDIT)
            nc.vector.tensor_scalar(da[:, :, :], da[:, :, :], A_LEAST, None, ALU.max).then_inc(soft, 1)
            dve.wait_ge(soft, 5 + CREDIT)

        @block.tensor
        def _(pe):
            pe.wait_ge(weights_in, 16 * 6 + CREDIT)
            for k in range(NPT):
                n = min(128, NP - 128 * k)
                if k >= 2:
                    pe.wait_ge(w_copied, k - 1 + CREDIT)
                nc.tensor.transpose(bk[2 * (k % 2)][:, 0:n], wrow[0:n, k, 0:DL], ident[0:n, 0:n])
                nc.tensor.transpose(bk[2 * (k % 2) + 1][0:DH, 0:n], wrow[0:n, k, DL:D], ident[0:n, 0:n]).then_inc(w_flipped, 1)
            for k in range(DI // 128):
                nc.tensor.transpose(bk[4 + k][:, 0:DL], orow0[:, 128 * k:128 * (k + 1)], ident[:, :])
                nc.tensor.transpose(bk[4 + k][:, DL:D], orow1[:, 128 * k:128 * (k + 1)], ident[0:DH, 0:DH]).then_inc(w_flipped, 1)
            pe.wait_ge(w_copied, NPT + DI // 128 + CREDIT)

            def turn(w):
                pe.wait_ge(rows_ready, w.t + 1 + CREDIT)
                pe.wait_ge(cols_a, w.t + CREDIT)
                pe.wait_ge(cols_v, w.t + CREDIT)
                for j in range(WB):
                    x, at = j * T // 512, j * T % 512
                    nc.tensor.transpose(bk[x][:, at:at + T], xn[:, j, 0:DL], ident[:, :])
                for j in range(WB):
                    x, at = j * T // 512, j * T % 512
                    last = nc.tensor.transpose(bk[2 + x][0:DH, at:at + T], xn[:, j, DL:D], ident[:, :])
                last.then_inc(rows_flipped, 1)
                pe.wait_ge(cols_a, w.t + 1 + CREDIT)
                pe.wait_ge(cols_v, w.t + 1 + CREDIT)
                pe.wait_ge(dt_copied, w.t + CREDIT)
                for j in range(WB):
                    out = bk[4][:, NH * j:NH * (j + 1)]
                    nc.tensor.matmul(out, xt0[:, w.p, j * T:(j + 1) * T], wi0[:, DI + CD:NP], start=True, stop=False)
                    last = nc.tensor.matmul(out, xt1[:, w.p, j * T:(j + 1) * T], wi1[:, DI + CD:NP], start=False, stop=True)
                last.then_inc(dt_done, 1)

            turns(pe, turn)


def second_layer(nc, a, s, keep):
    with ExitStack() as ctx:
        m = Mem(nc, ctx, "layer1")
        keep.wi0, keep.wi1 = m.sb("wi0", [DL, NP]), m.sb("wi1", [DH, NP])
        keep.wo = m.sb("wo", [128, DI // 128, D])
        keep.dt, keep.da = m.sb("dt", [T, B, NH]), m.sb("da", [T, B, NH])
        mamba_steps(nc, a, s, keep)
        mamba(nc, a, s, keep)
    feed_forward(nc, a, s, keep)


EPS_GATED = 1e-5
W6 = 3 + NCT + DI // 128 + NH
TURN = 2 * GB
CONV_AT = ((0,), (1, 2), (3, 4), ())


class Slot:

    def __init__(self, i, r):
        self.i, self.r, self.n = i, r, i * TURN + r
        self.g, self.j, self.p = i * 2 + r // GB, r % GB, r // GB % 2
        self.loads = i + r // TURN + 1

    def next(self, d=1):
        return Slot(self.i, self.r + d)


def mamba(nc, a, s, keep):
    with ExitStack() as ctx:
        m = Mem(nc, ctx, "p6")
        sb, sem = m.sb, m.sem
        ident, mask2, wi0, wi1, wo, dt, da = keep.ident, keep.mask2, keep.wi0, keep.wi1, keep.wo, keep.dt, keep.da
        after = sb("after", [T, T])
        cw, cb = sb("cw", [128, NCT, DCONV]), sb("cb", [128, NCT])
        dd, diag_d = sb("dd", [128, DI // 128]), sb("diag_d", [128, DI // 128, 128])
        nw, g1 = sb("nw", [128, DI // 128]), sb("g1", [T, 1])
        xt0, xt1 = sb("xt0", [DL, 2, GB * T]), sb("xt1", [DH, 2, GB * T])
        h = sb("h", [T, 2, GB, D])
        pad = sb("pad", [128, NCT, GB, T + DCONV - 1])
        u, th = sb("u", [128, NCT, GB, T]), sb("th", [128, NCT, GB, T])
        xbc = sb("xbc", [128, 2, NCT, GB, T])
        tz, sz = sb("tz", [T, DI]), sb("sz", [T, DI])
        cbm = sb("cbm", [T, T])
        am = sb("am", [T, NH, T])
        dec, mm = sb("dec", [T, 2, NH, T]), sb("mm", [T, NH, T])
        xd = sb("xd", [T, NH, HP])
        y, sq, yt = sb("y", [T, DI]), sb("sq", [T, DI]), sb("yt", [128, DI // 128, T])
        ms, ms2, rs, rg, half = (sb(n, [T, 1]) for n in ("ms", "ms2", "rs", "rg", "half"))
        bk = m.banks()

        weights_in, tuned, gate_tanh, half_set = sem("weights_in"), sem("tuned"), sem("gate_tanh"), sem("half_set")
        xt_in, h_in, h_stored = ([sem(f"{n}_{p}") for p in range(2)] for n in ("xt_in", "h_in", "h_stored"))
        conv_in, padded, tap_done, conv_done, conv_tanh, chan_ready = (
            sem("conv_in"), sem("padded"), sem("tap_done"), sem("conv_done"), sem("conv_tanh"), sem("chan_ready"))
        z_done, z_tanh, z_ready = sem("z_done"), sem("z_tanh"), sem("z_ready")
        cbm_ready, am_ready, seg_done, dec_ready, mm_ready = (
            sem("cbm_ready"), sem("am_ready"), sem("seg_done"), sem("dec_ready"), sem("mm_ready"))
        x_flipped, x_ready, y_done, y_ready, y_sq, ms_ready, rstd_ready = (
            sem("x_flipped"), sem("x_ready"), sem("y_done"), sem("y_ready"), sem("y_sq"), sem("ms_ready"), sem("rstd_ready"))
        y_flipped, yt_ready, out_done, scaled, h_ready = sem("y_flipped"), sem("yt_ready"), sem("out_done"), sem("scaled"), sem("h_ready")
        block = m.block()

        def at_least_0(n):
            return max(n, 0) if isinstance(n, int) else n

        def two_ago(n):
            return at_least_0(n - 1)

        def tiles(slot):
            q = slot.next(GB)
            if isinstance(q.g, int) and q.g >= NG:
                return []
            return [tile(q, k) for k in CONV_AT[slot.j]]

        def tile(q, k):
            return q, q.g * NCT + k, k, q.p, (NCT * q.p + k) % 2

        def runs(slot, ahead):
            return not isinstance(slot.n, int) or slot.n + ahead < B

        FIRST = Slot(0, 0)

        def run(eng, slot):
            slot(FIRST)
            with eng.Fori(0, NG // 2 - 1) as i:
                for r in range(1, TURN + 1):
                    slot(Slot(i, r))
            for r in range(1, TURN):
                slot(Slot(NG // 2 - 1, r))

        @block.sync
        def _(sp):
            loads = [(after[:, :], a.c_after), (cw[:, :, :], a.L1_attn_conv_w.rearrange("(k p) w -> p k w", p=128)),
                     (g1[:, :], rows(a.L1_attn_gate1, T))]
            for dst, src in ((cb, a.L1_attn_conv_b), (nw, a.L1_attn_norm_w)):
                loads += [(dst[:, k:k + 1], src[128 * k:128 * (k + 1), None]) for k in range(dst.shape[1])]
            for h_ in range(NH):
                k, lo = h_ * HP // 128, h_ * HP % 128
                loads.append((dd[lo:lo + HP, k:k + 1], rows(a.L1_attn_D[h_:h_ + 1], HP)))
            assert len(loads) == W6
            for dst, src in loads:
                sp.dma_start(dst, src).then_inc(weights_in, 16)

            def load_xt(g, p):
                sp.dma_start(xt0[:, p, :], s.xt[bass.ds(g, 1), 0:DL, :].rearrange("o p n -> (o p) n")).then_inc(xt_in[p], 16)
                sp.dma_start(xt1[:, p, :], s.xt[bass.ds(g, 1), DL:D, :].rearrange("o p n -> (o p) n")).then_inc(xt_in[p], 16)

            def load_h(g, p):
                sp.dma_start(h[:, p, :, :], s.h[bass.ts(g, GB), :, :].rearrange("b t d -> t b d")).then_inc(h_in[p], 16)

            def store_h(g, p):
                sp.wait_ge(h_ready, g * GB + GB + CREDIT)
                sp.dma_start(s.h[bass.ts(g, GB), :, :].rearrange("b t d -> t b d"), h[:, p, :, :]).then_inc(h_stored[p], 16)

            for p in range(2):
                load_xt(p, p)
                load_h(p, p)
            with sp.Fori(0, NG // 2 - 1) as i:
                for p in range(2):
                    g = i * 2 + p
                    sp.wait_ge(z_done, g * GB + GB + CREDIT)
                    load_xt(g + 2, p)
                    store_h(g, p)
                    sp.wait_ge(h_stored[p], 16 * (i + 1) + CREDIT)
                    load_h(g + 2, p)
            for p in range(2):
                store_h(NG - 2 + p, p)
            for p in range(2):
                sp.wait_ge(h_stored[p], 16 * (NG // 2) + CREDIT)

        @block.gpsimd
        def _(pool):
            nc.gpsimd.memset(half[:, :], -0.5).then_inc(half_set, 1)
            pool.wait_ge(half_set, 1 + CREDIT)

            def exponents(n):
                pool.wait_ge(seg_done, n + CREDIT)
                nc.gpsimd.tensor_tensor(am[:, :, :], da[:, bass.ds(n, 1), :].rearrange("t o h -> t (o h)").unsqueeze(2).to_broadcast([T, NH, T]),
                                        mask2[:, 1, :].unsqueeze(1).to_broadcast([T, NH, T]), ALU.mult).then_inc(am_ready, 1)

            def rstd(n):
                pool.wait_ge(ms_ready, n + 1 + CREDIT)
                pool.wait_ge(scaled, n + CREDIT)
                nc.gpsimd.tensor_tensor(rs[:, :], ms[:, :], half[:, :], ALU.pow).then_inc(rstd_ready, 1)

            exponents(0)
            exponents(1)
            with pool.Fori(0, B - 2) as n:
                exponents(n + 2)
                rstd(n)
            for n in range(B - 2, B):
                rstd(n)

        @block.scalar
        def _(act):
            act.wait_ge(weights_in, 16 * W6 + CREDIT)
            nc.scalar.activation(g1[:, :], g1[:, :], ACT.Tanh, scale=0.5).then_inc(gate_tanh, 1)
            act.wait_ge(tuned, 5 + CREDIT)

            def take(q, n, k, p, x):
                act.wait_ge(conv_in, n + 1 + CREDIT)
                act.wait_ge(chan_ready, at_least_0(n - NCT + 1) + CREDIT)
                nc.scalar.activation(pad[:, k, :, DCONV - 1:], bk[x][:, :].rearrange("p (b t) -> p b t", b=GB), ACT.Copy)
                nc.scalar.activation(u[:, k, :, :], bk[x][:, :].rearrange("p (b t) -> p b t", b=GB), ACT.Identity,
                                     scale=cw[:, k, DCONV - 1:DCONV], bias=cb[:, k:k + 1]).then_inc(padded, 1)

            def bend(q, n, k, p, x):
                act.wait_ge(conv_done, n + 1 + CREDIT)
                nc.scalar.activation(th[:, k, :, :], u[:, k, :, :], ACT.Tanh).then_inc(conv_tanh, 1)

            def decays(t):
                act.wait_ge(seg_done, t.n + 1 + CREDIT)
                act.wait_ge(mm_ready, two_ago(t.n) + CREDIT)
                for x in range(2):
                    last = nc.scalar.activation(dec[:, t.r % 2, 3 * x:3 * x + 3, :], bk[4 + x][:, 0:3 * T].rearrange("s (h t) -> s h t", h=3), ACT.Exp)
                last.then_inc(dec_ready, 1)

            def gate(n):
                act.wait_ge(z_done, n + 1 + CREDIT)
                act.wait_ge(z_ready, n + CREDIT)
                nc.scalar.activation(tz[:, :], bk[2][:, 0:DI], ACT.Tanh, scale=0.5).then_inc(z_tanh, 1)

            def slot(t):
                act.wait_ge(y_ready, t.n + 1 + CREDIT)
                act.wait_ge(ms_ready, t.n + CREDIT)
                nc.scalar.activation(sq[:, :], y[:, :], ACT.Square, accum_out=ms2[:, :]).then_inc(y_sq, 1)
                for c in tiles(t.next()):
                    take(*c)
                if runs(t, 2):
                    decays(t.next(2))
                if runs(t, 1):
                    gate(t.n + 1)
                for c in tiles(t):
                    bend(*c)
                act.wait_ge(y_flipped, t.n + 1 + CREDIT)
                act.wait_ge(out_done, t.n + CREDIT)
                nc.scalar.activation(yt[:, :, :], bk[3][:, 0:DI].rearrange("p (k t) -> p k t", k=DI // 128), ACT.Copy).then_inc(yt_ready, 1)

            take(*tile(FIRST, 0))
            for k in range(NCT):
                if k + 1 < NCT:
                    take(*tile(FIRST, k + 1))
                bend(*tile(FIRST, k))
            decays(FIRST)
            decays(FIRST.next())
            gate(0)
            for c in tiles(FIRST):
                take(*c)
            run(act, slot)

        @block.vector
        def _(dve):
            dve.wait_ge(weights_in, 16 * W6 + CREDIT)
            nc.vector.memset(pad[:, :, :, 0:DCONV - 1], 0.0)
            nc.vector.tensor_scalar(cw[:, :, :], cw[:, :, :], 0.5, None, ALU.mult).then_inc(tuned, 1)
            nc.vector.tensor_scalar(cb[:, :], cb[:, :], 0.5, None, ALU.mult).then_inc(tuned, 1)
            nc.vector.tensor_tensor(wo[:, :, :], wo[:, :, :], nw[:, :].unsqueeze(2).to_broadcast([128, DI // 128, D]), ALU.mult).then_inc(tuned, 1)
            nc.vector.tensor_tensor(diag_d[:, :, :], ident[:, :].unsqueeze(1).to_broadcast([128, DI // 128, 128]),
                                    dd[:, :].unsqueeze(2).to_broadcast([128, DI // 128, 128]), ALU.mult).then_inc(tuned, 1)
            dve.wait_ge(gate_tanh, 1 + CREDIT)
            nc.vector.tensor_scalar(g1[:, :], g1[:, :], 0.5, 0.5, ALU.mult, ALU.add).then_inc(tuned, 1)
            dve.wait_ge(tuned, 5 + CREDIT)

            def taps(q, n, k, p, x):
                dve.wait_ge(padded, n + 1 + CREDIT)
                for w in range(DCONV - 1):
                    ins = nc.vector.scalar_tensor_tensor(out=u[:, k, :, :], in0=pad[:, k, :, w:w + T], scalar=cw[:, k, w:w + 1],
                                                         in1=u[:, k, :, :], op0=ALU.mult, op1=ALU.add)
                    if w == DCONV - 2:
                        ins.then_inc(conv_done, 1)
                    else:
                        ins.then_inc(tap_done, 1)
                        dve.wait_ge(tap_done, n * (DCONV - 2) + w + 1 + CREDIT)

            def finish(q, n, k, p, x):
                dve.wait_ge(conv_tanh, n + 1 + CREDIT)
                dve.wait_ge(x_flipped, (max(q.g - 1, 0) if isinstance(q.g, int) else q.g - 1) * GB + CREDIT)
                nc.vector.scalar_tensor_tensor(out=xbc[:, p, k, :, :], in0=th[:, k, :, :], scalar=1.0, in1=u[:, k, :, :],
                                               op0=ALU.add, op1=ALU.mult).then_inc(chan_ready, 1)

            def operands(n):
                dve.wait_ge(x_flipped, n + 1 + CREDIT)
                dve.wait_ge(mm_ready, n + CREDIT)
                nc.vector.tensor_tensor(cbm[:, :], bk[6][:, DI:DI + T], mask2[:, 1, :], ALU.mult).then_inc(cbm_ready, 1)
                dve.wait_ge(y_done, n + CREDIT)
                nc.vector.tensor_tensor(xd[:, :, :], bk[6][:, 0:DI].rearrange("t (h p) -> t h p", h=NH),
                                        dt[:, bass.ds(n, 1), :].rearrange("t o h -> t (o h)").unsqueeze(2).to_broadcast([T, NH, HP]), ALU.mult).then_inc(x_ready, 1)

            def masked(t):
                n = t.n
                dve.wait_ge(dec_ready, n + 1 + CREDIT)
                dve.wait_ge(cbm_ready, n + 1 + CREDIT)
                dve.wait_ge(y_done, n + CREDIT)
                nc.vector.tensor_tensor(mm[:, :, :], dec[:, t.r % 2, :, :], cbm[:, :].unsqueeze(1).to_broadcast([T, NH, T]), ALU.mult).then_inc(mm_ready, 1)

            def gate(n):
                dve.wait_ge(z_tanh, n + 1 + CREDIT)
                dve.wait_ge(y_ready, n + CREDIT)
                nc.vector.scalar_tensor_tensor(out=sz[:, :], in0=tz[:, :], scalar=1.0, in1=bk[2][:, 0:DI], op0=ALU.add, op1=ALU.mult).then_inc(z_ready, 1)

            def residual(t):
                dve.wait_ge(rstd_ready, t.n + 1 + CREDIT)
                dve.wait_ge(h_ready, t.n + CREDIT)
                nc.vector.tensor_tensor(rg[:, :], rs[:, :], g1[:, :], ALU.mult).then_inc(scaled, 1)
                dve.wait_ge(scaled, t.n + 1 + CREDIT)
                dve.wait_ge(out_done, t.n + 1 + CREDIT)
                dve.wait_ge(h_in[t.p], t.loads * 16 + CREDIT)
                nc.vector.scalar_tensor_tensor(out=h[:, t.p, t.j, :], in0=bk[3][:, 0:D], scalar=rg[:, :], in1=h[:, t.p, t.j, :],
                                               op0=ALU.mult, op1=ALU.add).then_inc(h_ready, 1)

            def slot(t):
                conv = tiles(t)
                dve.wait_ge(y_done, t.n + 1 + CREDIT)
                dve.wait_ge(z_ready, t.n + 1 + CREDIT)
                dve.wait_ge(y_sq, t.n + CREDIT)
                dve.wait_ge(y_flipped, t.n + CREDIT)
                nc.vector.scalar_tensor_tensor(out=y[:, :], in0=bk[7][:, 0:DI], scalar=0.5, in1=sz[:, :], op0=ALU.mult, op1=ALU.mult).then_inc(y_ready, 1)
                for c in conv:
                    taps(*c)
                if runs(t, 1):
                    operands(t.n + 1)
                if t is not FIRST:
                    residual(t.next(-1))
                if runs(t, 1):
                    masked(t.next())
                    gate(t.n + 1)
                dve.wait_ge(y_sq, t.n + 1 + CREDIT)
                nc.vector.tensor_scalar(ms[:, :], ms2[:, :], 1.0 / DI, EPS_GATED, ALU.mult, ALU.add).then_inc(ms_ready, 1)
                for c in conv:
                    finish(*c)

            taps(*tile(FIRST, 0))
            for k in range(NCT):
                if k + 1 < NCT:
                    taps(*tile(FIRST, k + 1))
                finish(*tile(FIRST, k))
            operands(0)
            masked(FIRST)
            gate(0)
            run(dve, slot)
            residual(Slot(NG // 2 - 1, TURN - 1))

        @block.tensor
        def _(pe):
            pe.wait_ge(weights_in, 16 * W6 + CREDIT)
            pe.wait_ge(tuned, 5 + CREDIT)

            def conv_product(q, n, k, p, x):
                pe.wait_ge(xt_in[p], q.loads * 32 + CREDIT)
                pe.wait_ge(padded, two_ago(n) + CREDIT)
                col = DI + 128 * k
                nc.tensor.matmul(bk[x][:, :], wi0[:, col:col + 128], xt0[:, p, :], start=True, stop=False)
                nc.tensor.matmul(bk[x][:, :], wi1[:, col:col + 128], xt1[:, p, :], start=False, stop=True).then_inc(conv_in, 1)

            def sums(n):
                pe.wait_ge(am_ready, n + 1 + CREDIT)
                pe.wait_ge(dec_ready, n + CREDIT)
                for x in range(2):
                    last = nc.tensor.matmul(bk[4 + x][:, 0:3 * T], after[:, :], am[:, 3 * x:3 * x + 3, :].rearrange("j h t -> j (h t)"), start=True, stop=True)
                last.then_inc(seg_done, 1)

            def x_and_cb(t):
                pe.wait_ge(chan_ready, t.g * NCT + NCT + CREDIT)
                pe.wait_ge(x_ready, t.n + CREDIT)
                pe.wait_ge(cbm_ready, t.n + CREDIT)
                for k in range(DI // 128):
                    nc.tensor.transpose(bk[6][:, k * 128:(k + 1) * 128], xbc[:, t.p, k, t.j, :], ident[:, :])
                nc.tensor.matmul(bk[6][:, DI:DI + T], xbc[:, t.p, 3, t.j, :], xbc[:, t.p, 4, t.j, :], start=True, stop=True).then_inc(x_flipped, 1)

            def z_product(t):
                pe.wait_ge(xt_in[t.p], t.loads * 32 + CREDIT)
                pe.wait_ge(z_ready, t.n + CREDIT)
                rows_ = slice(t.j * T, (t.j + 1) * T)
                nc.tensor.matmul(bk[2][:, 0:DI], xt0[:, t.p, rows_], wi0[:, 0:DI], start=True, stop=False)
                nc.tensor.matmul(bk[2][:, 0:DI], xt1[:, t.p, rows_], wi1[:, 0:DI], start=False, stop=True).then_inc(z_done, 1)

            def projection(n):
                pe.wait_ge(yt_ready, n + 1 + CREDIT)
                for k in range(DI // 128):
                    last = nc.tensor.matmul(bk[3][:, 0:D], yt[:, k, :], wo[:, k, :], start=(k == 0), stop=(k == DI // 128 - 1))
                last.then_inc(out_done, 1)

            def skip(t):
                pe.wait_ge(chan_ready, t.g * NCT + NCT + CREDIT)
                pe.wait_ge(y_ready, t.n + CREDIT)
                for k in range(DI // 128):
                    nc.tensor.matmul(bk[7][:, k * 128:(k + 1) * 128], xbc[:, t.p, k, t.j, :], diag_d[:, k, :],
                                     start=(k == 0), stop=False, skip_group_check=True)

            def slot(t):
                pe.wait_ge(mm_ready, t.n + 1 + CREDIT)
                pe.wait_ge(x_ready, t.n + 1 + CREDIT)
                for h_ in range(NH):
                    last = nc.tensor.matmul(bk[7][:, h_ * HP:(h_ + 1) * HP], mm[:, h_, :], xd[:, h_, :], start=False, stop=True, skip_group_check=True)
                last.then_inc(y_done, 1)
                if t.j < GB - 1:
                    for c in tiles(t.next()):
                        conv_product(*c)
                if runs(t, 1):
                    x_and_cb(t.next())
                if t is not FIRST:
                    projection(t.n - 1)
                if runs(t, 2):
                    sums(t.n + 2)
                if runs(t, 1):
                    z_product(t.next())
                if t.j == GB - 1:
                    for c in tiles(t.next()):
                        conv_product(*c)
                pe.wait_ge(y_ready, t.n + 1 + CREDIT)
                pe.wait_ge(h_ready, t.n + CREDIT)
                for k in range(DI // 128):
                    last = nc.tensor.transpose(bk[3][:, k * 128:(k + 1) * 128], y[:, k * 128:(k + 1) * 128], ident[:, :])
                last.then_inc(y_flipped, 1)
                if runs(t, 1):
                    skip(t.next())

            for k in range(NCT):
                conv_product(*tile(FIRST, k))
            sums(0)
            sums(1)
            x_and_cb(FIRST)
            z_product(FIRST)
            for c in tiles(FIRST):
                conv_product(*c)
            skip(FIRST)
            run(pe, slot)
            projection(B - 1)


NODES = 21
DEPTH = 11
NPAD = 32
P7_DVE = 17


def feed_forward(nc, a, s, keep):
    LAST = NODES - 1
    with ExitStack() as ctx:
        m = Mem(nc, ctx, "p7")
        sb, sem = m.sb, m.sem
        ident = keep.ident
        wrow, win0, win1, wout = sb("wrow", [NODES, D]), sb("win0", [DL, NODES]), sb("win1", [DH, NODES]), sb("wout", [NPAD, D])
        h, xn, res = sb("h", [T, 2, WB, D]), sb("xn", [T, WB, D]), sb("res", [T, 2, WB, D])
        xt0, xt1 = sb("xt0", [DL, WB * T]), sb("xt1", [DH, WB * T])
        lg, gl, bit = sb("lg", [T, WB, NODES]), sb("gl", [T, WB, NODES]), sb("bit", [T, WB, NODES])
        on, low = sb("on", [T, WB, 16]), sb("low", [T, WB, 6])
        terms = sb("terms", [T, WB, 14])
        coef = sb("coef", [T, WB, NPAD])
        ct = sb("ct", [NPAD, WB * T])
        bk = m.banks()
        nm = Norm(nc, m, 1, WB)
        weights_in, w_flipped, w_copied, zeroed = sem("weights_in"), sem("w_flipped"), sem("w_copied"), sem("zeroed")
        h_in, stored = ([sem(f"{n}_{p}") for p in range(2)] for n in ("h_in", "stored"))
        rows_ready, rows_flipped, cols_a, cols_v = sem("rows_ready"), sem("rows_flipped"), sem("cols_a"), sem("cols_v")
        logits_done, logits_copied, gelu_ready, coef_ready, coef_flipped, ct_ready = (
            sem("logits_done"), sem("logits_copied"), sem("gelu_ready"), sem("coef_ready"), sem("coef_flipped"), sem("ct_ready"))
        out_done, res_ready, chain = sem("out_done"), sem("res_ready"), sem("chain")
        block = m.block()

        @block.sync
        def _(sp):
            sp.dma_start(wrow[:, :], a.L1_ffn_weights_in).then_inc(weights_in, 16)
            sp.wait_ge(zeroed, 1 + CREDIT)
            sp.dma_start(wout[0:NODES, :], a.L1_ffn_weights_out).then_inc(weights_in, 16)

            def load(t, p):
                sp.dma_start(h[:, p, :, :], s.h[bass.ts(t, WB), :, :].rearrange("b t d -> t b d")).then_inc(h_in[p], 16)

            def store(w):
                sp.wait_ge(res_ready, w.t + 1 + CREDIT)
                sp.dma_start(keep.out[bass.ts(w.t, WB), :, :].rearrange("b t d -> t b d"), res[:, w.p, :, :]).then_inc(stored[w.p], 16)

            load(0, 0)
            load(1, 1)
            with sp.Fori(0, NW // 2 - 1) as i:
                for r in range(2):
                    store(Turn(i, r))
                    load(i * 2 + r + 2, r)
            for r in range(2):
                store(Turn(NW // 2 - 1, r))
            for p in range(2):
                sp.wait_ge(stored[p], 16 * (NW // 2) + CREDIT)

        @block.gpsimd
        def _(pool):
            nm.pool_start(pool)
            with pool.Fori(0, NW) as t:
                nm.pool(pool, t, 0)

        @block.scalar
        def _(act):
            def columns(t):
                act.wait_ge(rows_flipped, t + 1 + CREDIT)
                act.wait_ge(logits_done, t + CREDIT)
                for x in range(WH):
                    last = nc.scalar.activation(xt1[:, x * 512:(x + 1) * 512], bk[2 + x][0:DH, :], ACT.Copy)
                last.then_inc(cols_a, 1)

            def turn(w):
                act.wait_ge(logits_copied, w.t + 1 + CREDIT)
                nc.scalar.activation(gl[:, :, :], lg[:, :, :], ACT.Gelu).then_inc(gelu_ready, 1)
                act.wait_ge(coef_flipped, w.t + 1 + CREDIT)
                act.wait_ge(out_done, w.t + CREDIT)
                for x in range(WH):
                    last = nc.scalar.activation(ct[:, x * 512:(x + 1) * 512], bk[x][0:NPAD, :], ACT.Copy)
                last.then_inc(ct_ready, 1)
                if not w.last:
                    columns(w.t + 1)

            columns(0)
            turns(act, turn)

        @block.vector
        def _(dve):
            nc.vector.memset(wout[:, :], 0.0).then_inc(zeroed, 1)
            nc.vector.memset(coef[:, :, :], 0.0)
            dve.wait_ge(w_flipped, 1 + CREDIT)
            nc.vector.tensor_copy(win0[:, :], bk[2][:, 0:NODES])
            nc.vector.tensor_copy(win1[:, :], bk[3][0:DH, 0:NODES]).then_inc(w_copied, 1)
            dve.wait_ge(w_copied, 1 + CREDIT)

            def norm(w, c):
                dve.wait_ge(h_in[w.p], w.earlier * 16 + 16 + CREDIT)
                dve.wait_ge(rows_flipped, w.t + CREDIT)
                nm.dve(dve, c, w.t, 0, lambda j: h[:, w.p, j, :], lambda j: xn[:, j, :], 1e-5).then_inc(rows_ready, 1)

            def columns(t):
                dve.wait_ge(rows_flipped, t + 1 + CREDIT)
                dve.wait_ge(logits_done, t + CREDIT)
                for x in range(WH):
                    last = nc.vector.tensor_copy(xt0[:, x * 512:(x + 1) * 512], bk[x][:, :])
                last.then_inc(cols_v, 1)

            def turn(w):
                g = w.t
                c = Chain(dve, chain, g, P7_DVE, NORM_LINKS)
                dve.wait_ge(logits_done, g + 1 + CREDIT)
                nc.vector.tensor_copy(lg[:, :, :], bk[2][:, 0:WB * NPAD].rearrange("t (b n) -> t b n", b=WB)[:, :, 0:NODES]).then_inc(logits_copied, 1)
                dve.wait_ge(logits_copied, g + 1 + CREDIT)
                c(nc.vector.tensor_scalar(bit[:, :, :], lg[:, :, :], 0.0, None, ALU.is_gt))
                tt = nc.vector.tensor_tensor
                nc.vector.tensor_copy(on[:, :, 2], bit[:, :, 0])
                c(nc.vector.tensor_scalar(on[:, :, 1], bit[:, :, 0], -1.0, 1.0, ALU.mult, ALU.add))
                for lo, hi in ((1, 3), (3, 7)):
                    right, left = on[:, :, 2 * lo + 2:2 * hi + 1:2], on[:, :, 2 * lo + 1:2 * hi:2]
                    c(tt(right, on[:, :, lo:hi], bit[:, :, lo:hi], ALU.mult))
                    c(tt(left, on[:, :, lo:hi], right, ALU.subtract))
                c(tt(low[:, :, 1:4:2], on[:, :, 7:9], bit[:, :, 7:9], ALU.mult))
                c(tt(low[:, :, 0:3:2], on[:, :, 7:9], low[:, :, 1:4:2], ALU.subtract))
                c(tt(low[:, :, 4], on[:, :, 9], bit[:, :, 9], ALU.mult))
                c(tt(low[:, :, 4], on[:, :, 9], low[:, :, 4], ALU.subtract))
                c(nc.vector.tensor_reduce(low[:, :, 5], low[:, :, 0:5], AX.X, ALU.add))
                c(nc.vector.tensor_scalar(low[:, :, 5], low[:, :, 5], -1.0, 1.0, ALU.mult, ALU.add))
                dve.wait_ge(gelu_ready, g + 1 + CREDIT)
                dve.wait_ge(coef_flipped, g + CREDIT)
                twice = lambda lo, hi: gl[:, :, lo:hi].unsqueeze(3).to_broadcast([T, WB, hi - lo, 2])
                pairs = lambda v: v.rearrange("t b (n k) -> t b n k", k=2)
                c(tt(coef[:, :, 1:3], on[:, :, 1:3], gl[:, :, 0:1].to_broadcast([T, WB, 2]), ALU.mult))
                tt(pairs(coef[:, :, 3:7]), pairs(on[:, :, 3:7]), twice(1, 3), ALU.mult)
                tt(pairs(coef[:, :, 7:15]), pairs(on[:, :, 7:15]), twice(3, 7), ALU.mult)
                tt(pairs(coef[:, :, 15:19]), pairs(low[:, :, 0:4]), twice(7, 9), ALU.mult)
                c(tt(coef[:, :, 19], low[:, :, 4], gl[:, :, 9], ALU.mult))
                tt(terms[:, :, 0:6], on[:, :, 9:15], gl[:, :, 9:15], ALU.mult)
                tt(terms[:, :, 6:12], low[:, :, :], gl[:, :, 15:NODES], ALU.mult)
                nc.vector.tensor_scalar(terms[:, :, 12], gl[:, :, LAST], float(DEPTH - 6), None, ALU.mult)
                c(nc.vector.tensor_scalar(terms[:, :, 13], coef[:, :, 19], -1.0, None, ALU.mult))
                nc.vector.tensor_reduce(coef[:, :, LAST], terms[:, :, :], AX.X, ALU.add).then_inc(coef_ready, 1)
                if not w.last:
                    norm(w.next(), c)
                dve.wait_ge(out_done, g + 1 + CREDIT)
                dve.wait_ge(stored[w.p], w.earlier * 16 + CREDIT)
                for x in range(WB // 2):
                    last = tt(res[:, w.p, 2 * x:2 * x + 2, :], h[:, w.p, 2 * x:2 * x + 2, :], bk[4 + x][:, 0:2 * D].rearrange("t (b d) -> t b d", b=2), ALU.add)
                last.then_inc(res_ready, 1)
                if not w.last:
                    columns(g + 1)
                    c.close()

            norm(Turn(0, 0), Chain(dve, chain))
            columns(0)
            turns(dve, turn)

        @block.tensor
        def _(pe):
            pe.wait_ge(weights_in, 32 + CREDIT)
            nc.tensor.transpose(bk[2][:, 0:NODES], wrow[:, 0:DL], ident[0:NODES, 0:NODES])
            nc.tensor.transpose(bk[3][0:DH, 0:NODES], wrow[:, DL:D], ident[0:NODES, 0:NODES]).then_inc(w_flipped, 1)
            pe.wait_ge(w_copied, 1 + CREDIT)

            def flip(t):
                pe.wait_ge(rows_ready, t + 1 + CREDIT)
                pe.wait_ge(ct_ready, t + CREDIT)
                pe.wait_ge(logits_copied, t + CREDIT)
                for j in range(WB):
                    x, at = j * T // 512, j * T % 512
                    nc.tensor.transpose(bk[x][:, at:at + T], xn[:, j, 0:DL], ident[:, :])
                for j in range(WB):
                    x, at = j * T // 512, j * T % 512
                    last = nc.tensor.transpose(bk[2 + x][0:DH, at:at + T], xn[:, j, DL:D], ident[:, :])
                last.then_inc(rows_flipped, 1)

            def turn(w):
                g = w.t
                pe.wait_ge(cols_a, g + 1 + CREDIT)
                pe.wait_ge(cols_v, g + 1 + CREDIT)
                for j in range(WB):
                    out = bk[2][:, NPAD * j:NPAD * j + NODES]
                    nc.tensor.matmul(out, xt0[:, j * T:(j + 1) * T], win0[:, :], start=True, stop=False)
                    last = nc.tensor.matmul(out, xt1[:, j * T:(j + 1) * T], win1[:, :], start=False, stop=True)
                last.then_inc(logits_done, 1)
                pe.wait_ge(coef_ready, g + 1 + CREDIT)
                for j in range(WB):
                    x, at = j * T // 512, j * T % 512
                    last = nc.tensor.transpose(bk[x][0:NPAD, at:at + T], coef[:, j, :], ident[:, :])
                last.then_inc(coef_flipped, 1)
                pe.wait_ge(ct_ready, g + 1 + CREDIT)
                pe.wait_ge(res_ready, g + CREDIT)
                for j in range(WB):
                    last = nc.tensor.matmul(bk[4 + j // 2][:, j % 2 * D:(j % 2 + 1) * D], ct[:, j * T:(j + 1) * T], wout[:, :], start=True, stop=True)
                last.then_inc(out_done, 1)
                if not w.last:
                    flip(g + 1)

            flip(0)
            turns(pe, turn)


SCRATCH_KIND = "Internal"


class Keep:
    pass


def build(nc, a, s, out):
    with ExitStack() as ctx:
        m = Mem(nc, ctx, "keep")
        keep = Keep()
        keep.out = out
        keep.gathered = m.sem_of_pool_dma("gathered")
        keep.ident = m.sb("ident", [128, 128])
        keep.mask2 = m.sb("mask2", [T, 2, T])
        with ExitStack() as ttt:
            keep.hist = Mem(nc, ttt, "ttt").sb("hist", [T, B, D])
            ttt_prepare(nc, a, s, keep)
            ttt_scan(nc, a, s, keep)
            ttt_finish(nc, a, s, keep)
        moe(nc, a, s, keep)
        second_layer(nc, a, s, keep)


class Arrays:
    pass


def _constants():
    import numpy as np
    i = np.arange(T)
    col = np.arange(EXP_COLS)
    expert = np.minimum(col // D, NE)
    return {
        "c_ident": np.eye(128, dtype=np.float32),
        "c_mask2": np.stack([i[:, None] < i[None, :], i[:, None] <= i[None, :]], axis=1).astype(np.float32),
        "c_after": (i[:, None] > i[None, :]).astype(np.float32),
        "c_expand": np.concatenate([np.arange(NE + 1)[:, None] == expert[None, :]] * 3 + [np.zeros((5, EXP_COLS), bool)]).astype(np.float32),
        "c_iota": np.broadcast_to(np.arange(NE, dtype=np.float32), (128, NE)).copy(),
    }


def kernel(**inputs):
    import numpy as np
    import concourse.bacc as bacc
    from concourse.bass_utils import run_bass_kernel_spmd

    nc = bacc.Bacc("TRN2", target_bir_lowering=False, num_devices=1)
    arrays, a, s = {}, Arrays(), Arrays()
    for name, value in list(inputs.items()) + list(_constants().items()):
        v = np.ascontiguousarray(value).reshape(np.shape(value) or (1,))
        arrays[f"in_{name}"] = v
        a.__dict__[name] = nc.dram_tensor(f"in_{name}", v.shape, mybir.dt.from_np(v.dtype), kind="ExternalInput").ap()
    scratch = {"pt": (2 * LOG_POS, D), "h": (B, T, D), "zc": (B, T, 2 * D), "qz": (B, T, 2 * D),
               "mk": (B, T, NC, H, C), "mq": (B, T, H, T), "g": (B, T, D), "corr": (B, C, D), "xt": (NG, D, GB * T)}
    for name, shape in scratch.items():
        s.__dict__[name] = nc.dram_tensor(f"s_{name}", shape, F32, kind=SCRATCH_KIND).ap()
    out = nc.dram_tensor("out_h", (B, T, D), F32, kind="ExternalOutput").ap()
    build(nc, a, s, out)
    r = run_bass_kernel_spmd(nc, [arrays], core_ids=[0])
    return r.results[0]["out_h"]
```
